# Optimizing a Trainium2 kernel written in Bass

```python
import numpy as np
import jax
import jax.numpy as jnp

def _softmax(x, axis=-1):
    return jax.nn.softmax(x, axis=axis)

def _gelu(x):
    return jax.nn.gelu(x, approximate=True)

def _silu(x):
    return jax.nn.silu(x)

def _sigmoid(x):
    return jax.nn.sigmoid(x)

def _layernorm(x, axis=-1, eps=1e-05):
    m = jnp.mean(x, axis=axis, keepdims=True)
    v = jnp.var(x, axis=axis, keepdims=True)
    return (x - m) / jnp.sqrt(v + eps)

def _scatter_add(tgt, idx, src, axis=0):
    return tgt.at[idx].add(src)

def _segment_sum(src, seg, n):
    return jax.ops.segment_sum(src, seg, n)
kernel_name = 'mk_audio_tower_d1_tok_audfeat1024_r4_dcca8e'

def setup_inputs(seed: int=0):
    np.random.seed(seed)
    _w = jnp.asarray

    def _rec_inputs():
        import jax
        import jax.numpy as jnp
        _rk = jax.random.key(seed)
        x = -0.000392918 + 0.999932 * jax.random.normal(jax.random.fold_in(_rk, 1), (16, 375, 128), jnp.float32)
        return x
    x = _rec_inputs()

    def _L0_tok_setup():
        import jax, jax.numpy as jnp
        import numpy as np
        CONTEXT = 5
        DILATION = 1
        EPS = 1e-05
        key = jax.random.key(seed)
        ks = jax.random.split(key, 6)
        B, T, D, O = (32, 1024, 128, 256)
        K = D * CONTEXT
        x = jax.random.normal(ks[0], (B, T, D), dtype=jnp.float32)
        W = jax.random.normal(ks[1], (O, K), dtype=jnp.float32) * 0.02
        b = jnp.zeros((O,), dtype=jnp.float32)
        gamma = jnp.ones((O,), dtype=jnp.float32)
        beta = jnp.zeros((O,), dtype=jnp.float32)
        running_mean = jax.random.normal(ks[2], (O,), dtype=jnp.float32) * 0.1
        running_var = jax.random.uniform(ks[3], (O,), dtype=jnp.float32, minval=0.5, maxval=1.5)
        return {'x': x, 'W': W, 'b': b, 'gamma': gamma, 'beta': beta, 'running_mean': running_mean, 'running_var': running_var}
    _L0_tok_all = _L0_tok_setup()
    _L0_tok_in = {k: v for k, v in _L0_tok_all.items() if k in ('W', 'b', 'gamma', 'beta', 'running_mean', 'running_var')}
    del _L0_tok_all

    def _L0_attn_setup():
        import jax, jax.numpy as jnp
        import numpy as np
        DM = 256
        E = 512
        NS = 16
        R = 64
        K = 4
        BB, LL = (4, 256)
        EPS = 1e-05

        def rmsnorm(x, w):
            x = x.astype(jnp.float32)
            return x * jax.lax.rsqrt(jnp.mean(x * x, axis=-1, keepdims=True) + EPS) * w

        def causal_conv(x, w, b):
            xp = jnp.pad(x, ((0, 0), (K - 1, 0), (0, 0)))
            L = x.shape[1]
            y = sum((w[:, k] * xp[:, k:k + L, :] for k in range(K)))
            return y + b

        def ssm_scan(dt, Bm, Cm, x, A):

            def step(h, inp):
                dt_t, B_t, C_t, x_t = inp
                dA = jnp.exp(dt_t[..., None] * A)
                h = dA * h + (dt_t * x_t)[..., None] * B_t[:, None, :]
                y = jnp.einsum('ben,bn->be', h, C_t)
                return (h, y)
            h0 = jnp.zeros((dt.shape[0], A.shape[0], A.shape[1]), dt.dtype)
            xs = (dt.transpose(1, 0, 2), Bm.transpose(1, 0, 2), Cm.transpose(1, 0, 2), x.transpose(1, 0, 2))
            _, ys = jax.lax.scan(step, h0, xs)
            return ys.transpose(1, 0, 2)

        def mamba(h, inproj, convw, convb, xproj, dtw, dtb, Alog, Dp, outproj):
            xz = jnp.einsum('bld,ed->ble', h, inproj)
            xc, z = jnp.split(xz, 2, axis=-1)
            xc = jax.nn.silu(causal_conv(xc, convw, convb))
            xdbl = jnp.einsum('ble,fe->blf', xc, xproj)
            dt = jax.nn.softplus(jnp.einsum('blr,er->ble', xdbl[..., :R], dtw) + dtb)
            Bm = xdbl[..., R:R + NS]
            Cm = xdbl[..., R + NS:]
            A = -jnp.exp(Alog)
            y = ssm_scan(dt, Bm, Cm, xc, A) + xc * Dp
            y = y * jax.nn.silu(z)
            return jnp.einsum('ble,de->bld', y, outproj)

        def one_direction(x, norm_w, mixer_params, normf):
            residual = x.astype(jnp.float32)
            hidden = mamba(rmsnorm(residual, norm_w), *mixer_params)
            return rmsnorm(hidden + residual, normf)
        key = jax.random.key(seed)
        ks = iter(jax.random.split(key, 40))

        def w(shape, fan):
            return jax.random.normal(next(ks), shape, jnp.float32) / np.sqrt(fan)
        inp = {'x': jax.random.normal(next(ks), (BB, LL, DM), jnp.float32)}
        for pre in ('fwd', 'bwd'):
            inp[pre + '_norm'] = 1.0 + 0.02 * jax.random.normal(next(ks), (DM,), jnp.float32)
            inp[pre + '_inproj'] = w((2 * E, DM), DM)
            inp[pre + '_convw'] = w((E, K), K)
            inp[pre + '_convb'] = jnp.zeros((E,), jnp.float32)
            inp[pre + '_xproj'] = w((R + 2 * NS, E), E)
            inp[pre + '_dtw'] = w((E, R), R)
            inp[pre + '_dtb'] = jnp.log(jnp.expm1(0.01 * jnp.ones((E,), jnp.float32)))
            inp[pre + '_Alog'] = jnp.log(jnp.broadcast_to(jnp.arange(1, NS + 1, dtype=jnp.float32), (E, NS)))
            inp[pre + '_Dp'] = jnp.ones((E,), jnp.float32)
            inp[pre + '_outproj'] = w((DM, E), E)
        inp['normf'] = 1.0 + 0.02 * jax.random.normal(next(ks), (DM,), jnp.float32)
        return inp
    _L0_attn_all = _L0_attn_setup()
    _L0_attn_in = {k: v for k, v in _L0_attn_all.items() if k in ('fwd_norm', 'fwd_inproj', 'fwd_convw', 'fwd_convb', 'fwd_xproj', 'fwd_dtw', 'fwd_dtb', 'fwd_Alog', 'fwd_Dp', 'fwd_outproj', 'bwd_norm', 'bwd_inproj', 'bwd_convw', 'bwd_convb', 'bwd_xproj', 'bwd_dtw', 'bwd_dtb', 'bwd_Alog', 'bwd_Dp', 'bwd_outproj', 'normf')}
    del _L0_attn_all

    def _L0_ffn_setup():
        import jax, jax.numpy as jnp
        import numpy as np
        N_HEADS = 4
        key = jax.random.key(seed)
        k1, k2, k3, k4 = jax.random.split(key, 4)
        dmodel, n_experts, expert_size = (256, 64, 128)
        B, S = (4, 512)
        x = jax.random.normal(k1, (B, S, dmodel), dtype=jnp.float32)
        expert_sel = jax.random.normal(k2, (n_experts, dmodel), dtype=jnp.float32) * dmodel ** (-0.5)
        keys = jax.random.normal(k3, (n_experts, dmodel, expert_size), dtype=jnp.float32) * dmodel ** (-0.5)
        values = jax.random.normal(k4, (n_experts, expert_size, dmodel), dtype=jnp.float32) * (n_experts * expert_size) ** (-0.5)
        return {'x': x, 'expert_sel': expert_sel, 'keys': keys, 'values': values}
    _L0_ffn_all = _L0_ffn_setup()
    _L0_ffn_in = {k: v for k, v in _L0_ffn_all.items() if k in ('expert_sel', 'keys', 'values')}
    del _L0_ffn_all
    return {'x': x, 'L0_tok_W': _L0_tok_in['W'], 'L0_tok_b': _L0_tok_in['b'], 'L0_tok_gamma': _L0_tok_in['gamma'], 'L0_tok_beta': _L0_tok_in['beta'], 'L0_tok_running_mean': _L0_tok_in['running_mean'], 'L0_tok_running_var': _L0_tok_in['running_var'], 'L0_attn_fwd_norm': _L0_attn_in['fwd_norm'], 'L0_attn_fwd_inproj': _L0_attn_in['fwd_inproj'], 'L0_attn_fwd_convw': _L0_attn_in['fwd_convw'], 'L0_attn_fwd_convb': _L0_attn_in['fwd_convb'], 'L0_attn_fwd_xproj': _L0_attn_in['fwd_xproj'], 'L0_attn_fwd_dtw': _L0_attn_in['fwd_dtw'], 'L0_attn_fwd_dtb': _L0_attn_in['fwd_dtb'], 'L0_attn_fwd_Alog': _L0_attn_in['fwd_Alog'], 'L0_attn_fwd_Dp': _L0_attn_in['fwd_Dp'], 'L0_attn_fwd_outproj': _L0_attn_in['fwd_outproj'], 'L0_attn_bwd_norm': _L0_attn_in['bwd_norm'], 'L0_attn_bwd_inproj': _L0_attn_in['bwd_inproj'], 'L0_attn_bwd_convw': _L0_attn_in['bwd_convw'], 'L0_attn_bwd_convb': _L0_attn_in['bwd_convb'], 'L0_attn_bwd_xproj': _L0_attn_in['bwd_xproj'], 'L0_attn_bwd_dtw': _L0_attn_in['bwd_dtw'], 'L0_attn_bwd_dtb': _L0_attn_in['bwd_dtb'], 'L0_attn_bwd_Alog': _L0_attn_in['bwd_Alog'], 'L0_attn_bwd_Dp': _L0_attn_in['bwd_Dp'], 'L0_attn_bwd_outproj': _L0_attn_in['bwd_outproj'], 'L0_attn_normf': _L0_attn_in['normf'], 'L0_ffn_expert_sel': _L0_ffn_in['expert_sel'], 'L0_ffn_keys': _L0_ffn_in['keys'], 'L0_ffn_values': _L0_ffn_in['values']}

def reference(x, L0_tok_W, L0_tok_b, L0_tok_gamma, L0_tok_beta, L0_tok_running_mean, L0_tok_running_var, L0_attn_fwd_norm, L0_attn_fwd_inproj, L0_attn_fwd_convw, L0_attn_fwd_convb, L0_attn_fwd_xproj, L0_attn_fwd_dtw, L0_attn_fwd_dtb, L0_attn_fwd_Alog, L0_attn_fwd_Dp, L0_attn_fwd_outproj, L0_attn_bwd_norm, L0_attn_bwd_inproj, L0_attn_bwd_convw, L0_attn_bwd_convb, L0_attn_bwd_xproj, L0_attn_bwd_dtw, L0_attn_bwd_dtb, L0_attn_bwd_Alog, L0_attn_bwd_Dp, L0_attn_bwd_outproj, L0_attn_normf, L0_ffn_expert_sel, L0_ffn_keys, L0_ffn_values):
    import jax
    import jax.numpy as jnp

    def _L0_tok_ref(x, W, b, gamma, beta, running_mean, running_var):
        import jax, jax.numpy as jnp
        import numpy as np
        CONTEXT = 5
        DILATION = 1
        EPS = 1e-05
        B, T, D = x.shape
        Tp = T - DILATION * (CONTEXT - 1)
        idx = jnp.arange(Tp)[:, None] + jnp.arange(CONTEXT)[None, :] * DILATION
        win = x[:, idx, :].reshape(B, Tp, CONTEXT * D)
        h = jnp.einsum('btk,ok->bto', win, W) + b
        h = jax.nn.relu(h)
        h = gamma * (h - running_mean) * jax.lax.rsqrt(running_var + EPS) + beta
        return h

    def _L0_attn_ref(x, fwd_norm, fwd_inproj, fwd_convw, fwd_convb, fwd_xproj, fwd_dtw, fwd_dtb, fwd_Alog, fwd_Dp, fwd_outproj, bwd_norm, bwd_inproj, bwd_convw, bwd_convb, bwd_xproj, bwd_dtw, bwd_dtb, bwd_Alog, bwd_Dp, bwd_outproj, normf):
        import jax, jax.numpy as jnp
        import numpy as np
        DM = 256
        E = 512
        NS = 16
        R = 64
        K = 4
        BB, LL = (4, 256)
        EPS = 1e-05

        def rmsnorm(x, w):
            x = x.astype(jnp.float32)
            return x * jax.lax.rsqrt(jnp.mean(x * x, axis=-1, keepdims=True) + EPS) * w

        def causal_conv(x, w, b):
            xp = jnp.pad(x, ((0, 0), (K - 1, 0), (0, 0)))
            L = x.shape[1]
            y = sum((w[:, k] * xp[:, k:k + L, :] for k in range(K)))
            return y + b

        def ssm_scan(dt, Bm, Cm, x, A):

            def step(h, inp):
                dt_t, B_t, C_t, x_t = inp
                dA = jnp.exp(dt_t[..., None] * A)
                h = dA * h + (dt_t * x_t)[..., None] * B_t[:, None, :]
                y = jnp.einsum('ben,bn->be', h, C_t)
                return (h, y)
            h0 = jnp.zeros((dt.shape[0], A.shape[0], A.shape[1]), dt.dtype)
            xs = (dt.transpose(1, 0, 2), Bm.transpose(1, 0, 2), Cm.transpose(1, 0, 2), x.transpose(1, 0, 2))
            _, ys = jax.lax.scan(step, h0, xs)
            return ys.transpose(1, 0, 2)

        def mamba(h, inproj, convw, convb, xproj, dtw, dtb, Alog, Dp, outproj):
            xz = jnp.einsum('bld,ed->ble', h, inproj)
            xc, z = jnp.split(xz, 2, axis=-1)
            xc = jax.nn.silu(causal_conv(xc, convw, convb))
            xdbl = jnp.einsum('ble,fe->blf', xc, xproj)
            dt = jax.nn.softplus(jnp.einsum('blr,er->ble', xdbl[..., :R], dtw) + dtb)
            Bm = xdbl[..., R:R + NS]
            Cm = xdbl[..., R + NS:]
            A = -jnp.exp(Alog)
            y = ssm_scan(dt, Bm, Cm, xc, A) + xc * Dp
            y = y * jax.nn.silu(z)
            return jnp.einsum('ble,de->bld', y, outproj)

        def one_direction(x, norm_w, mixer_params, normf):
            residual = x.astype(jnp.float32)
            hidden = mamba(rmsnorm(residual, norm_w), *mixer_params)
            return rmsnorm(hidden + residual, normf)
        fh = one_direction(x, fwd_norm, (fwd_inproj, fwd_convw, fwd_convb, fwd_xproj, fwd_dtw, fwd_dtb, fwd_Alog, fwd_Dp, fwd_outproj), normf)
        bh = one_direction(jnp.flip(x, 1), bwd_norm, (bwd_inproj, bwd_convw, bwd_convb, bwd_xproj, bwd_dtw, bwd_dtb, bwd_Alog, bwd_Dp, bwd_outproj), normf)
        return fh + jnp.flip(bh, 1)

    def _L0_ffn_ref(x, expert_sel, keys, values):
        import jax, jax.numpy as jnp
        import numpy as np
        N_HEADS = 4
        B, S, d = x.shape
        n_experts = keys.shape[0]
        xf = x.reshape(-1, d)
        N = xf.shape[0]
        logits = xf @ expert_sel.T
        sel = jax.nn.sigmoid(logits)
        sel_val, sel_idx = jax.lax.top_k(sel, N_HEADS)
        gates = jnp.zeros((N, n_experts), dtype=x.dtype)
        gates = gates.at[jnp.arange(N)[:, None], sel_idx].set(sel_val)
        h = jnp.einsum('nd,kde->nke', xf, keys)
        scores = jax.nn.relu(h) * gates[:, :, None]
        out = jnp.einsum('nke,kev->nv', scores, values)
        return out.reshape(B, S, -1)
    h = _L0_tok_ref(x, L0_tok_W, L0_tok_b, L0_tok_gamma, L0_tok_beta, L0_tok_running_mean, L0_tok_running_var)
    h = h + _L0_attn_ref(_layernorm(h, axis=-1), L0_attn_fwd_norm, L0_attn_fwd_inproj, L0_attn_fwd_convw, L0_attn_fwd_convb, L0_attn_fwd_xproj, L0_attn_fwd_dtw, L0_attn_fwd_dtb, L0_attn_fwd_Alog, L0_attn_fwd_Dp, L0_attn_fwd_outproj, L0_attn_bwd_norm, L0_attn_bwd_inproj, L0_attn_bwd_convw, L0_attn_bwd_convb, L0_attn_bwd_xproj, L0_attn_bwd_dtw, L0_attn_bwd_dtb, L0_attn_bwd_Alog, L0_attn_bwd_Dp, L0_attn_bwd_outproj, L0_attn_normf)
    h = h + _L0_ffn_ref(_layernorm(h, axis=-1), L0_ffn_expert_sel, L0_ffn_keys, L0_ffn_values)
    return h

_drawn_inputs = setup_inputs


def setup_inputs(seed=0):
    import zlib

    import numpy as np

    out = dict(_drawn_inputs(seed))
    spreads = {'L0_tok_b': (0.0, 0.1),
     'L0_tok_gamma': (1.0, 0.2),
     'L0_tok_beta': (0.0, 0.1),
     'L0_attn_fwd_convb': (0.0, 0.427),
     'L0_attn_fwd_dtb': (-4.600166320800781, 0.6),
     'L0_attn_fwd_Dp': (1.0, 0.2),
     'L0_attn_bwd_convb': (0.0, 0.395),
     'L0_attn_bwd_dtb': (-4.600166320800781, 0.6),
     'L0_attn_bwd_Dp': (1.0, 0.2)}
    factors = {'L0_attn_fwd_norm': 7.513,
     'L0_attn_fwd_dtw': 7.692,
     'L0_attn_fwd_Alog': 3.666,
     'L0_attn_bwd_norm': 7.829,
     'L0_attn_bwd_xproj': 3.109,
     'L0_attn_bwd_dtw': 7.544,
     'L0_attn_bwd_Alog': 5.588,
     'L0_attn_normf': 2.827}
    for name, (base, spread) in spreads.items():
        noise = np.random.default_rng([zlib.crc32(name.encode()), seed]).standard_normal(out[name].shape)
        drawn = base * np.exp(spread * noise) if base else spread * noise
        out[name] = jnp.asarray(drawn.astype(out[name].dtype))
    for name, factor in factors.items():
        out[name] = (out[name] * factor).astype(out[name].dtype)
    return out
```

```python
import numpy as np
import concourse.bass as bass
from concourse import mybir
from contextlib import ExitStack

F32 = mybir.dt.float32
BF16 = mybir.dt.bfloat16
I32 = mybir.dt.int32
U32 = mybir.dt.uint32
ALU = mybir.AluOpType
ACT = mybir.ActivationFunctionType
AX = mybir.AxisListType

B, TIN, DIN = 16, 375, 128
CTX = 5
L = TIN - CTX + 1
D = 256
E = 512
EC = E // 128
NS = 16
R = 64
TAPS = 4
LP = L + 1
TT = [(0, 128), (128, 128), (256, L - 256)]
EPS = 1e-5
POOL_B = (3, 8, 13)
LOG_T = 2.0 ** -5
LOG_C = (0.9999997716733988, -0.4998678486375896, 0.3219470998103213)
EXP_LN = "natural_log_exp_and_others"

N = B * L
NT = (N + 127) // 128
LAST = N - 128 * (NT - 1)
X = 64
HX = 128
TOPK = 4
SATURATED = 16.6355
G = 4
S = 6
PAGES = (NT * 128 * TOPK + 127 * X) // 128
PAGES = (PAGES + S - 1) // S * S


def tower(nc, t, h2_dram, x_dram):
    ctx = ExitStack()
    with ctx:
        def sb(name, shape, dt=F32):
            return ctx.enter_context(nc.sbuf_tensor(name, shape, dt))

        def pb(name, shape):
            return ctx.enter_context(nc.psum_tensor(name, shape, F32))

        def sem(name):
            return ctx.enter_context(nc.semaphore(name))

        tokw = sb("tokw", [128, CTX, D])
        tok_rows = sb("tok_rows", [128, 5, D])
        tok_scale = sb("tok_scale", [128, D])
        tok_shift = sb("tok_shift", [128, D])
        tok_b = sb("tok_b", [1, D])
        ones = sb("ones", [1, 128])
        ident = sb("ident", [128, 128])
        sel = sb("sel", [96, 2 * NS, 128], BF16)
        w_in = [sb(f"w_in{d}", [128, 2, 2 * E]) for d in range(2)]
        w_dt = [sb(f"w_dt{d}", [128, EC, R]) for d in range(2)]
        w_bc = [sb(f"w_bc{d}", [128, EC, 96]) for d in range(2)]
        w_r = [sb(f"w_r{d}", [R, E]) for d in range(2)]
        w_out = [sb(f"w_out{d}", [128, EC, D]) for d in range(2)]
        NV = TAPS + 3 + NS
        vec = [sb(f"vec{d}", [128, EC, NV]) for d in range(2)]
        norm = [sb(f"norm{d}", [128, 2]) for d in range(2)]
        neg_a = [sb(f"neg_a{d}", [128, EC, NS]) for d in range(2)]
        eps_c = sb("eps_c", [128, 3])
        log_t = sb("log_t", [128, 1])

        x_t = sb("x_t", [128, TIN])
        h_new = sb("h_new", [128, 3, D])
        r_new = sb("r_new", [128, 3, D])
        h_cur = sb("h_cur", [128, 3, D])
        r_cur = sb("r_cur", [128, 3, D])
        u_tok = sb("u_tok", [128, 3, D])
        u_t = sb("u_t", [128, 2, L])
        bn = sb("bn", [128, 3, 6])
        mv = sb("mv", [128, 3, 2])
        scales = sb("scales", [128, 2, 3])
        norm_x = sb("norm_x", [128, 2, 3])
        half = sb("half", [128, 6])
        rms = sb("rms", [128, 3])


        xraw = sb("xraw", [128, EC, L + 2 * (TAPS - 1)])
        xc = [sb(f"xc{d}", [128, EC, L]) for d in range(2)]
        sz = [sb(f"sz{d}", [128, EC, L]) for d in range(2)]
        dt_ = [sb(f"dt{d}", [128, EC, L]) for d in range(2)]
        dtx = [sb(f"dtx{d}", [128, EC, L]) for d in range(2)]
        r_sb = sb("r_sb", [R, L])
        bcs = [sb(f"bcs{d}", [96, L], BF16) for d in range(2)]
        mid = sb("mid", [96, L], BF16)
        rest = sb("rest", [96, L])

        NA, NX, NH, NP, NB = 2, 2, 2, 2, 4
        da = [sb(f"da{j}", [128, EC, LP]) for j in range(NA)]
        dbx = [sb(f"dbx{j}", [128, EC, LP]) for j in range(NX)]
        hs = [sb(f"hs{j}", [128, EC, LP]) for j in range(NH)]
        pr = [sb(f"pr{j}", [128, EC, LP]) for j in range(NP)]
        bc = [sb(f"bc{j}", [128, 2, L + 1]) for j in range(NB)]

        y2 = sb("y2", [128, EC, L])
        s_tok = sb("s_tok", [128, 3, D])
        sq = sb("sq", [128, 3, D], BF16)
        ss = sb("ss", [128, 3])
        acc = sb("acc", [128, 3, D])

        tok_x = y2[:, 0, 0:D]
        y_ps = pb("y_ps", [128, EC, 512])
        bc_ps = pb("bc_ps", [128, 2, 512])
        misc = [pb(f"misc{j}", [128, 512]) for j in range(2)]

        loads = sem("loads")
        x_in = sem("x_in")
        setup_a = sem("setup_a")
        setup_v = sem("setup_v")
        setup_done = sem("setup_done")
        full = [sem(f"misc_full{j}") for j in range(2)]
        free = [sem(f"misc_free{j}") for j in range(2)]
        tok_v = sem("tok_v")
        tok_q = sem("tok_q")
        stats_go = sem("stats_go")
        setup_p = sem("setup_p")
        u_done = sem("u_done")
        uT_done = sem("uT_done")
        raw_done = sem("raw_done")
        conv = sem("conv")
        xc_done = sem("xc_done")
        sz_done = sem("sz_done")
        r_done = sem("r_done")
        bc_hi = sem("bc_hi")
        bc_v = sem("bc_v")
        sp_a = sem("sp_a")
        sp_v = sem("sp_v")
        dt_done = sem("dt_done")
        dtx_done = sem("dtx_done")
        bc_mm = sem("bc_mm")
        bc_copied = sem("bc_copied")
        da_done = sem("da_done")
        dbx_v = sem("dbx_v")
        dbx_p = sem("dbx_p")
        h_done = sem("h_done")
        p_done = sem("p_done")
        sum_done = sem("sum_done")
        y_read = sem("y_read")
        y2_done = sem("y2_done")
        out_mm = sem("out_mm")
        s_done = sem("s_done")
        ss_done = sem("ss_done")
        q_done = sem("q_done")
        acc_v = sem("acc_v")
        h2_sent = sem("h2_sent")
        zeroed = sem("zeroed")
        moved = sem("moved")

        NPOOL = len(POOL_B)
        NDVE = NS - NPOOL

        def later(value):
            return not isinstance(value, int) or value > 0

        def cnt(u, per, off=0):
            return u[0] * (2 * per) + (u[1] * per + off)

        def batch(u, per, off=0):
            return u[0] * per + ((u[1] // 2) * per + off)

        def after(u, by=1):
            return (u[0], u[1] + by)

        FIRST = ["x0", "x1", "z0", "z1", "tok", "x", "dt0", "dt1", "tokT"]
        FORWARD = ["x0", "x1", "out", "z0", "z1", "tok", "x", "dt0", "dt1", "tokT"]
        BACKWARD = ["x0", "x1", "out", "z0", "z1", "x", "dt0", "dt1"]
        PROLOGUE = (0, -1)

        def uses(u, what):
            k = u[1]
            if k == -1:
                return ["tok", "tokT", "x0", "x1", "z0", "z1", "x", "dt0", "dt1"].index(what)
            if k == 0:
                return 9 + FIRST.index(what)
            if k >= 2 * B - 1 > 2:
                return 18 * B + (k - (2 * B - 1))
            order = BACKWARD if k % 2 else FORWARD
            return u[0] * 18 + (18 * (k // 2) + (18 if k % 2 else 8) + order.index(what))

        units = lambda i: [(i, 1), (i, 2)]

        block = ctx.enter_context(nc.Block())

        N_LOADS = 0

        @block.sync
        def _(sp):
            nonlocal N_LOADS
            rows = ["tok_gamma", "tok_beta", "tok_mean", "tok_var", "normf"]
            todo = [(tokw[:, :, :], t["tok_w"]), (tok_b[:, :], t["tok_b"].rearrange("(a n) -> a n", a=1)),
                    (ident[:, :], t["ident"]), (sel[:, :, :], t["sel"])]
            for j, n in enumerate(rows):
                todo.append((tok_rows[:, j, :], t[n].rearrange("(a n) -> a n", a=1).to_broadcast([128, D])))
            for d in range(2):
                todo += [(w_in[d][:, :, :], t[f"in{d}"]), (w_dt[d][:, :, :], t[f"xdt{d}"]),
                         (w_bc[d][:, :, :], t[f"xbc{d}"]), (w_r[d][:, :], t[f"dtw{d}"]),
                         (w_out[d][:, :, :], t[f"out{d}"]), (vec[d][:, :, :], t[f"vec{d}"]),
                         (norm[d][:, :], t[f"norm{d}"])]
            sp.dma_start(x_t[:, :], t["x"][0]).then_inc(x_in, 16)
            for dst, src in todo:
                sp.dma_start(dst, src).then_inc(loads, 16)
            N_LOADS = 16 * len(todo)

            def load_x(src, token_products):
                sp.wait_ge(full[1], token_products)
                sp.dma_start(x_t[:, :], src).then_inc(x_in, 16)

            def store_h2(u):
                b = batch(u, 1, -1)
                sp.wait_ge(acc_v, cnt(u, 5, 1))
                for j, (t0, n) in enumerate(TT):
                    if isinstance(b, int):
                        dst = h2_dram[b, t0:t0 + n, :]
                    else:
                        dst = h2_dram[bass.ds(b, 1), t0:t0 + n, :].rearrange("a t d -> (a t) d")
                    sp.dma_start(dst, acc[0:n, j, :]).then_inc(h2_sent, 16)

            sp.sem_inc(h2_sent, 1)
            pages = x_dram.rearrange("(j p) d -> j p d", p=128)
            zeros = t["zeros"].rearrange("p (a d) -> a p d", a=1)
            ZERO = PAGES // (B - 2)
            load_x(t["x"][1], uses(PROLOGUE, "tok") + 1)
            with sp.Fori(0, B - 2) as i:
                sp.dma_start(pages[bass.ds(i * ZERO, ZERO), :, :], zeros.to_broadcast([ZERO, 128, D])).then_inc(zeroed, 16)
                load_x(t["x"][bass.ds(i + 2, 1), :, :].rearrange("a p n -> (a p) n"), i * 18 + (uses((0, 0), "tok") + 1))
                sp.wait_ge(zeroed, i * 16 + 16)
                store_h2((i, 2))
            load_x(t["x"][B - 1], 18 * (B - 2) + (uses((0, 0), "tok") + 1))
            store_h2((0, 2 * B - 2))
            store_h2((0, 2 * B))
            sp.wait_ge(h2_sent, 1 + 48 * B)
            sp.wait_ge(zeroed, 16 * (B - 2))

        @block.tensor
        def _(pe):
            def fill(j, u, what):
                if later(due := uses(u, what)):
                    pe.wait_ge(free[j], due)

            def tokens(u, q):
                pe.wait_ge(x_in, q * 16 + 16)
                for g in range(2):
                    fill(g, u, "tok")
                    for j in ((0, 1) if g == 0 else (2,)):
                        t0, n = TT[j]
                        out = misc[g][0:n, (j % 2) * D:(j % 2) * D + D]
                        for c in range(CTX):
                            nc.tensor.matmul(out, x_t[:, t0 + c:t0 + c + n], tokw[:, c, :], start=(c == 0), stop=False)
                        mm = nc.tensor.matmul(out, ones[0:1, 0:n], tok_b[:, :], start=False, stop=True)
                    mm.then_inc(full[g], 1)

            def tokens_t(u, q):
                pe.wait_ge(u_done, q * 3 + 3)
                for c in range(2):
                    fill(c, u, "tokT")
                    for j, (t0, n) in enumerate(TT):
                        mm = nc.tensor.transpose(misc[c][:, t0:t0 + n], u_tok[0:n, j, c * 128:(c + 1) * 128],
                                                 ident[0:n, 0:n])
                    mm.then_inc(full[c], 1)

            def inproj(u, m):
                p, d = after(u), (u[1] + 1) % 2
                if m == 0:
                    pe.wait_ge(uT_done, batch(p, 2, 2))
                j = m % 2
                fill(j, u, ("x0", "x1", "z0", "z1")[m // 2])
                for c in range(2):
                    mm = nc.tensor.matmul(misc[j][:, 0:L], w_in[d][:, c, m * 128:(m + 1) * 128], u_t[:, c, :],
                                          start=(c == 0), stop=(c == 1))
                mm.then_inc(full[j], 1)

            def xproj(u):
                p, d = after(u), (u[1] + 1) % 2
                pe.wait_ge(xc_done, cnt(p, 1, 1))
                for j, w, n in ((0, w_dt[d], R), (1, w_bc[d], 96)):
                    fill(j, u, "x")
                    for m in range(EC):
                        mm = nc.tensor.matmul(misc[j][0:n, 0:L], w[:, m, :], xc[d][:, m, :],
                                              start=(m == 0), stop=(m == EC - 1))
                    mm.then_inc(full[j], 1)

            def dtproj(u, m):
                p, d = after(u), (u[1] + 1) % 2
                if m == 0:
                    pe.wait_ge(r_done, cnt(p, 1, 1))
                j = m % 2
                fill(j, u, ("dt0", "dt1")[m // 2])
                nc.tensor.matmul(misc[j][:, 0:L], w_r[d][:, m * 128:(m + 1) * 128], r_sb[:, :],
                                 start=True, stop=True).then_inc(full[j], 1)

            def spread(u, n):
                d = u[1] % 2
                if n == 0:
                    pe.wait_ge(bc_v, cnt(u, 4, 4))
                if later(due := cnt(u, NS, n)):
                    pe.wait_ge(bc_copied, due)
                nc.tensor.matmul(bc_ps[:, 0, 0:L], sel[:, n, :], bcs[d][:, :], start=True, stop=True)
                nc.tensor.matmul(bc_ps[:, 1, 0:L], sel[:, NS + n, :], bcs[d][:, :], start=True, stop=True).then_inc(bc_mm, 1)

            def add_state(u, n):
                if n == 0:
                    if later(due := cnt(u, 1)):
                        pe.wait_ge(y_read, due)
                pe.wait_ge(p_done, cnt(u, NS, n + 1))
                for m in range(EC):
                    mm = nc.tensor.matmul(y_ps[:, m, 0:L], ident[:, :], pr[n % NP][:, m, 0:L],
                                          start=(n == 0), stop=(n == NS - 1))
                mm.then_inc(sum_done, 1)

            def outproj(u):
                d = (u[1] + 1) % 2
                pe.wait_ge(y2_done, cnt(u, 1))
                for g in range(2):
                    fill(g, u, "out")
                    for j in ((0, 1) if g == 0 else (2,)):
                        t0, n = TT[j]
                        for m in range(EC):
                            mm = nc.tensor.matmul(misc[g][0:n, (j % 2) * D:(j % 2) * D + D], y2[:, m, t0:t0 + n],
                                                  w_out[d][:, m, :], start=(m == 0), stop=(m == EC - 1))
                    mm.then_inc(full[g], 1)

            def prepare(u, step):
                if step in T_IN:
                    m = 2 * T_IN.index(step)
                    inproj(u, m)
                    inproj(u, m + 1)
                if u[1] % 2 == 0 and step == T_TOK:
                    tokens(u, batch(u, 1, 1))
                if step == T_X:
                    xproj(u)
                if step in T_DT:
                    m = 2 * T_DT.index(step)
                    dtproj(u, m)
                    dtproj(u, m + 1)
                if u[1] % 2 == 0 and step == T_TOKT:
                    tokens_t(u, batch(u, 1, 1))

            def unit(u, before=True, own=True, nxt=True):
                for step in range(NS if own else T_F2 + 1):
                    if own and step + 2 < NS:
                        spread(u, step + 2)
                    elif nxt:
                        spread(after(u), step + 2 - NS)
                    if step >= 2 and own:
                        add_state(u, step - 2)
                    elif step < 2 and before:
                        add_state(after(u, -1), step - 2 + NS)
                    if before and step == T_F2:
                        outproj(u)
                    if nxt:
                        prepare(u, step)

            pe.wait_ge(setup_done, 1)
            tokens(PROLOGUE, 0)
            tokens_t(PROLOGUE, 0)
            for step in range(NS):
                prepare(PROLOGUE, step)
            spread((0, 0), 0)
            spread((0, 0), 1)
            unit((0, 0), before=False)
            with pe.Fori(0, B - 1) as i:
                for u in units(i):
                    unit(u)
            unit((0, 2 * B - 1), nxt=False)
            unit((0, 2 * B), own=False, nxt=False)

        @block.scalar
        def _(act):
            def got(j, u, what):
                act.wait_ge(full[j], uses(u, what) + 1)

            def tokens_t(u, q):
                for c in range(2):
                    got(c, u, "tokT")
                    nc.scalar.activation(u_t[:, c, :], misc[c][:, 0:L], ACT.Copy).then_inc(uT_done, 1)
                    act.wait_ge(uT_done, q * 2 + (c + 1))
                    act.sem_inc(free[c], 1)

            def evacuate(u, m):
                p, d = after(u), (u[1] + 1) % 2
                j = m % 2
                got(j, u, ("x0", "x1", "z0", "z1")[m // 2])
                if m == 0:
                    if later(due := cnt(p, 1, -1)):
                        act.wait_ge(y2_done, due)
                    if later(due := cnt(p, 3 * EC)):
                        act.wait_ge(conv, due)
                if m < EC:
                    nc.scalar.activation(xraw[:, m, TAPS - 1:TAPS - 1 + L], misc[j][:, 0:L], ACT.Copy).then_inc(raw_done, 1)
                    nc.scalar.activation(xc[d][:, m, :], misc[j][:, 0:L], ACT.Identity, scale=vec[d][:, m, TAPS - 1:TAPS],
                                         bias=vec[d][:, m, TAPS:TAPS + 1]).then_inc(free[j], 1)
                else:
                    nc.scalar.activation(sz[d][:, m - EC, :], misc[j][:, 0:L], ACT.Copy).then_inc(free[j], 1)

            def silu_x(u):
                p, d = after(u), (u[1] + 1) % 2
                act.wait_ge(conv, cnt(p, 3 * EC, 3 * EC))
                nc.scalar.activation(xc[d][:, :, :], xc[d][:, :, :], ACT.Silu).then_inc(xc_done, 1)
                for j in range(2):
                    act.wait_ge(free[j], uses(u, "z1") + 1)
                nc.scalar.activation(sz[d][:, :, :], sz[d][:, :, :], ACT.Silu).then_inc(sz_done, 1)
                act.preload_act_table_set(EXP_LN)

            def split_bc(u):
                p, d = after(u), (u[1] + 1) % 2
                got(0, u, "x")
                nc.scalar.activation(r_sb[:, :], misc[0][0:R, 0:L], ACT.Copy).then_inc(r_done, 1)
                act.wait_ge(r_done, cnt(p, 1, 1))
                act.sem_inc(free[0], 1)
                got(1, u, "x")
                nc.scalar.activation(bcs[d][:, :], misc[1][0:96, 0:L], ACT.Copy).then_inc(bc_hi, 1)

            def softplus_in(u, m):
                p, d = after(u), (u[1] + 1) % 2
                j = m % 2
                got(j, u, ("dt0", "dt1")[m // 2])
                b = vec[d][:, m, TAPS + 1:TAPS + 2]
                nc.scalar.activation(dt_[d][:, m, :], misc[j][:, 0:L], ACT.Relu, bias=b)
                nc.scalar.activation(xraw[:, m, TAPS - 1:TAPS - 1 + L], misc[j][:, 0:L], ACT.Abs, bias=b).then_inc(free[j], 1)

            def softplus_exp(u):
                p = after(u)
                v = xraw[:, :, TAPS - 1:TAPS - 1 + L]
                act.wait_ge(free[0], uses(u, "dt1") + 1)
                act.wait_ge(free[1], uses(u, "dt1") + 1)
                nc.scalar.activation(v, v, ACT.Exp, scale=-1.0).then_inc(sp_a, 1)

            def softplus_ln(u):
                p, d = after(u), (u[1] + 1) % 2
                act.wait_ge(sp_v, cnt(p, 6, 1))
                nc.scalar.activation(dtx[d][:, :, :], dtx[d][:, :, :], ACT.Ln).then_inc(sp_a, 1)

            def copy_bc(u, n):
                act.wait_ge(bc_mm, cnt(u, NS, n + 1))
                if later(due := cnt(u, NS, n + 1 - NB)):
                    act.wait_ge(p_done, due)
                dv = sum(1 for x in range(n + 1 - NB + NS) if x % NS not in POOL_B) - NDVE
                if later(due := cnt(u, NDVE, dv)):
                    act.wait_ge(dbx_v, due)
                nc.scalar.activation(bc[n % NB][:, :, 0:L], bc_ps[:, :, 0:L], ACT.Copy).then_inc(bc_copied, 1)

            def decay(u, n):
                d = u[1] % 2
                if n == 0:
                    act.wait_ge(dt_done, cnt(u, 1, 1))
                if later(due := cnt(u, NS, n + 1 - NA)):
                    act.wait_ge(h_done, due)
                for m in range(EC):
                    a = nc.scalar.activation(da[n % NA][:, m, 1:L], dt_[d][:, m, 1 - d:L - d], ACT.Exp,
                                             scale=neg_a[d][:, m, n:n + 1])
                a.then_inc(da_done, 1)

            def squares(u):
                act.wait_ge(s_done, cnt(u, 2))
                act.wait_ge(q_done, cnt(u, 1))
                for j, (t0, n) in enumerate(TT):
                    nc.scalar.activation(sq[0:n, j, :], s_tok[0:n, j, :], ACT.Square, accum_out=ss[0:n, j:j + 1]).then_inc(ss_done, 1)
                act.wait_ge(ss_done, cnt(u, 4, -1))
                nc.scalar.activation(ss[:, :], ss[:, :], ACT.Identity, scale=1.0 / D, bias=eps_c[:, 0:1]).then_inc(ss_done, 1)

            def prepare(u, step):
                if step - 1 in T_IN:
                    m = 2 * T_IN.index(step - 1)
                    evacuate(u, m)
                    evacuate(u, m + 1)
                if step == T_SILU:
                    silu_x(u)
                if step - 1 == T_X:
                    split_bc(u)
                if step - 1 in T_DT:
                    m = 2 * T_DT.index(step - 1)
                    softplus_in(u, m)
                    softplus_in(u, m + 1)
                    if m == 2:
                        softplus_exp(u)
                if step == T_LN:
                    softplus_ln(u)
                if u[1] % 2 == 0 and step - 1 == T_TOKT:
                    tokens_t(u, batch(u, 1, 1))

            def unit(u, before=True, own=True, nxt=True):
                for step in range(NS if own else T_SQ + 1):
                    if before and step == T_SQ:
                        squares(u)
                    if nxt:
                        prepare(u, step)
                    if own and step + 2 < NS:
                        copy_bc(u, step + 2)
                    elif nxt:
                        copy_bc(after(u), step + 2 - NS)
                    if own and step + 1 < NS:
                        decay(u, step + 1)
                    elif nxt:
                        decay(after(u), 0)

            act.preload_act_table_set(EXP_LN)
            act.wait_ge(loads, N_LOADS)
            act.wait_ge(setup_v, 1)
            nc.scalar.activation(log_t[:, :], eps_c[:, 1:2], ACT.Ln).then_inc(setup_a, 1)
            for d in range(2):
                nc.scalar.activation(neg_a[d][:, :, :], vec[d][:, :, TAPS + 3:NV], ACT.Exp).then_inc(setup_a, 1)
            tokens_t(PROLOGUE, 0)
            for step in range(NS):
                prepare(PROLOGUE, step)
            copy_bc((0, 0), 0)
            copy_bc((0, 0), 1)
            decay((0, 0), 0)
            unit((0, 0), before=False)
            with act.Fori(0, B - 1) as i:
                for u in units(i):
                    unit(u)
            unit((0, 2 * B - 1), nxt=False)
            unit((0, 2 * B), own=False, nxt=False)

        @block.vector
        def _(dve):
            def got(j, u, what):
                dve.wait_ge(full[j], uses(u, what) + 1)

            def rows2(x):
                return x.rearrange("p (a n) -> p a n", a=2)

            def tokens(u, q):
                got(0, u, "tok")
                if later(due := q * 2):
                    dve.wait_ge(moved, due)
                nc.vector.scalar_tensor_tensor(h_new[:, 0:2, :], rows2(misc[0][:, :]), 0.0, tok_scale[:, None, :].to_broadcast([128, 2, D]),
                                               ALU.max, ALU.mult).then_inc(free[0], 1)
                got(1, u, "tok")
                n = TT[2][1]
                nc.vector.scalar_tensor_tensor(h_new[0:n, 2, :], misc[1][0:n, 0:D], 0.0, tok_scale[0:n, :],
                                               ALU.max, ALU.mult).then_inc(free[1], 1)
                dve.wait_ge(free[0], uses(u, "tok") + 1)
                nc.vector.tensor_tensor(h_new[:, 0:2, :], h_new[:, 0:2, :], tok_shift[:, None, :].to_broadcast([128, 2, D]),
                                        ALU.add).then_inc(tok_v, 1)
                dve.wait_ge(free[1], uses(u, "tok") + 1)
                nc.vector.tensor_tensor(h_new[0:n, 2, :], h_new[0:n, 2, :], tok_shift[0:n, :], ALU.add).then_inc(tok_v, 1)
                for j, (t0, n) in enumerate(TT):
                    dve.wait_ge(tok_v, q * 10 + (1 if j < 2 else 2))
                    nc.vector.bn_stats(bn[0:n, j, :], h_new[0:n, j, :]).then_inc(tok_v, 1)
                dve.wait_ge(tok_v, q * 10 + 5)
                dve.sem_inc(stats_go, 1)
                for j, (t0, n) in enumerate(TT):
                    nc.vector.bn_aggr(mv[0:n, j, :], bn[0:n, j, :]).then_inc(tok_v, 1)
                dve.wait_ge(tok_v, q * 10 + 8)
                nc.vector.tensor_scalar(norm_x[:, 0, :], mv[:, :, 1], 1.0, EPS, ALU.mult, ALU.add).then_inc(tok_v, 1)
                nc.vector.tensor_scalar(norm_x[:, 1, :], mv[:, :, 1], 1.0 + EPS, EPS * EPS, ALU.mult, ALU.add).then_inc(tok_v, 1)

            def normalise(u, q):
                dve.wait_ge(tok_q, q + 1)
                for j, (t0, n) in enumerate(TT):
                    nc.vector.tensor_scalar(u_tok[0:n, j, :], h_new[0:n, j, :], mv[0:n, j, 0:1], scales[0:n, 1, j:j + 1],
                                            ALU.subtract, ALU.mult).then_inc(u_done, 1)
                for j, (t0, n) in enumerate(TT):
                    a = nc.vector.tensor_scalar(r_new[0:n, j, :], h_new[0:n, j, :], mv[0:n, j, 0:1], scales[0:n, 0, j:j + 1],
                                                ALU.subtract, ALU.mult)
                a.then_inc(moved, 1)

            def take_tokens(u):
                q = batch(u, 1)
                dve.wait_ge(moved, q * 2 + 1)
                nc.vector.tensor_copy(h_cur[:, 0:2, :], h_new[:, 0:2, :])
                nc.vector.tensor_copy(r_cur[:, 0:2, :], r_new[:, 0:2, :])
                n = TT[2][1]
                nc.vector.tensor_copy(h_cur[0:n, 2, :], h_new[0:n, 2, :])
                nc.vector.tensor_copy(r_cur[0:n, 2, :], r_new[0:n, 2, :]).then_inc(moved, 1)

            def convolve(u, k):
                p, d = after(u), (u[1] + 1) % 2
                for m in range(EC):
                    if k == 0:
                        dve.wait_ge(free[m % 2], uses(u, ("x0", "x1")[m // 2]) + 1)
                        if m == 0:
                            dve.wait_ge(raw_done, cnt(p, EC, EC))
                    else:
                        dve.wait_ge(conv, cnt(p, 3 * EC, (k - 1) * EC + m + 1))
                    t0 = k if d == 0 else 2 * (TAPS - 1) - k
                    nc.vector.scalar_tensor_tensor(xc[d][:, m, :], xraw[:, m, t0:t0 + L], vec[d][:, m, k:k + 1], xc[d][:, m, :],
                                                   ALU.mult, ALU.add).then_inc(conv, 1)

            def split_bc(u):
                p, d = after(u), (u[1] + 1) % 2
                dve.wait_ge(bc_hi, cnt(p, 1, 1))
                nc.vector.tensor_tensor(mid[64:96, :], misc[1][64:96, 0:L], bcs[d][64:96, :], ALU.subtract).then_inc(bc_v, 1)
                nc.vector.tensor_tensor(rest[64:96, :], misc[1][64:96, 0:L], bcs[d][64:96, :], ALU.subtract).then_inc(bc_v, 1)
                nc.vector.tensor_tensor(bcs[d][32:64, :], misc[1][32:64, 0:L], bcs[d][32:64, :], ALU.subtract).then_inc(free[1], 1)
                dve.wait_ge(bc_v, cnt(p, 4, 2))
                nc.vector.tensor_tensor(bcs[d][64:96, :], rest[64:96, :], mid[64:96, :], ALU.subtract).then_inc(bc_v, 1)
                dve.wait_ge(free[1], uses(u, "x") + 1)
                dve.sem_inc(bc_v, 1)

            def log1p_small(u):
                p, d = after(u), (u[1] + 1) % 2
                m = xraw[:, :, TAPS - 1:TAPS - 1 + L]
                dve.wait_ge(sp_a, cnt(p, 2, 1))
                if later(due := cnt(p, NPOOL, -NPOOL)):
                    dve.wait_ge(dbx_p, due)
                nc.vector.tensor_scalar(dtx[d][:, :, :], m, LOG_T, 1.0, ALU.max, ALU.add).then_inc(sp_v, 1)
                nc.vector.tensor_scalar(m, m, LOG_T, None, ALU.min).then_inc(sp_v, 1)
                dve.wait_ge(sp_v, cnt(p, 6, 2))
                nc.vector.tensor_scalar(y2[:, :, :], m, LOG_C[2], LOG_C[1], ALU.mult, ALU.add).then_inc(sp_v, 1)
                dve.wait_ge(sp_v, cnt(p, 6, 3))
                nc.vector.tensor_tensor(y2[:, :, :], y2[:, :, :], m, ALU.mult).then_inc(sp_v, 1)
                dve.wait_ge(sp_v, cnt(p, 6, 4))
                nc.vector.scalar_tensor_tensor(y2[:, :, :], y2[:, :, :], LOG_C[0], m, ALU.add, ALU.mult).then_inc(sp_v, 1)

            def add_dt(u):
                p, d = after(u), (u[1] + 1) % 2
                dve.wait_ge(sp_a, cnt(p, 2, 2))
                nc.vector.scalar_tensor_tensor(dt_[d][:, :, :], dtx[d][:, :, :], log_t[:, 0:1], dt_[d][:, :, :],
                                               ALU.subtract, ALU.add).then_inc(sp_v, 1)
                dve.wait_ge(sp_v, cnt(p, 6, 6))
                nc.vector.tensor_tensor(dt_[d][:, :, :], dt_[d][:, :, :], y2[:, :, :], ALU.add).then_inc(dt_done, 1)

            def form_dtx(u):
                p, d = after(u), (u[1] + 1) % 2
                dve.wait_ge(dt_done, cnt(p, 1, 1))
                if later(due := cnt(p, NPOOL, -NPOOL)):
                    dve.wait_ge(dbx_p, due)
                nc.vector.tensor_tensor(dtx[d][:, :, :], dt_[d][:, :, :], xc[d][:, :, :], ALU.mult).then_inc(dtx_done, 1)

            def drive(u, n):
                if n in POOL_B:
                    return
                d = u[1] % 2
                if n == 0:
                    dve.wait_ge(dtx_done, cnt(u, 1, 1))
                dve.wait_ge(bc_copied, cnt(u, NS, n + 1))
                if later(due := cnt(u, NS, n + 1 - NX)):
                    dve.wait_ge(h_done, due)
                nc.vector.tensor_tensor(dbx[n % NX][:, :, d:d + L], dtx[d][:, :, :],
                                        bc[n % NB][:, 0, None, 0:L].to_broadcast([128, EC, L]), ALU.mult).then_inc(dbx_v, 1)

            def scan(u, n):
                d = u[1] % 2
                if n in POOL_B:
                    dve.wait_ge(dbx_p, cnt(u, NPOOL, sum(1 for x in POOL_B if x <= n)))
                else:
                    dve.wait_ge(dbx_v, cnt(u, NDVE, sum(1 for x in range(n + 1) if x not in POOL_B)))
                dve.wait_ge(da_done, cnt(u, NS, n + 1))
                if later(due := cnt(u, NS, n + 1 - NH)):
                    dve.wait_ge(p_done, due)
                flat = lambda x: x[:, :, :].rearrange("p m l -> p (m l)")
                a, b, o = flat(da[n % NA]), flat(dbx[n % NX]), flat(hs[n % NH])
                if d:
                    a, b, o = a[:, ::-1], b[:, ::-1], o[:, ::-1]
                nc.vector.tensor_tensor_scan(o, a, b, 0.0, ALU.mult, ALU.add).then_inc(h_done, 1)

            def gate(u):
                d = (u[1] + 1) % 2
                dve.wait_ge(sum_done, cnt(u, NS))
                dve.wait_ge(sz_done, cnt(u, 1))
                for m in range(EC):
                    a = nc.vector.scalar_tensor_tensor(y2[:, m, :], xc[d][:, m, :], vec[d][:, m, TAPS + 2:TAPS + 3],
                                                       y_ps[:, m, 0:L], ALU.mult, ALU.add)
                a.then_inc(y_read, 1)
                dve.wait_ge(y_read, cnt(u, 1))
                nc.vector.tensor_tensor(y2[:, :, :], y2[:, :, :], sz[d][:, :, :], ALU.mult).then_inc(y2_done, 1)

            def residual(u):
                got(0, u, "out")
                nc.vector.tensor_tensor(s_tok[:, 0:2, :], rows2(misc[0][:, :]), r_cur[:, 0:2, :], ALU.add).then_inc(s_done, 1)
                got(1, u, "out")
                n = TT[2][1]
                nc.vector.tensor_tensor(s_tok[0:n, 2, :], misc[1][0:n, 0:D], r_cur[0:n, 2, :], ALU.add).then_inc(s_done, 1)
                dve.wait_ge(s_done, cnt(u, 2))
                dve.sem_inc(free[0], 1)
                dve.sem_inc(free[1], 1)

            def accumulate(u):
                d = (u[1] + 1) % 2
                dve.wait_ge(q_done, cnt(u, 1, 1))
                for j, (t0, n) in enumerate(TT):
                    nc.vector.scalar_tensor_tensor(s_tok[0:n, j, :], s_tok[0:n, j, :], rms[0:n, j:j + 1], tok_rows[0:n, 4, :],
                                                   ALU.mult, ALU.mult).then_inc(acc_v, 1)
                if d == 0:
                    dve.wait_ge(h2_sent, batch(u, 48, 1))
                other = h_cur if d == 0 else acc
                n = TT[2][1]
                dve.wait_ge(acc_v, cnt(u, 5, 1 - 5 + 3))
                nc.vector.tensor_tensor(acc[:, 0:2, :], s_tok[:, 0:2, :], other[:, 0:2, :], ALU.add).then_inc(acc_v, 1)
                nc.vector.tensor_tensor(acc[0:n, 2, :], s_tok[0:n, 2, :], other[0:n, 2, :], ALU.add).then_inc(acc_v, 1)

            def prepare(u, step):
                if step in T_CONV:
                    convolve(u, T_CONV.index(step))
                if u[1] % 2 == 0 and step == T_TOKV:
                    tokens(u, batch(u, 1, 1))
                if step - 1 == T_X:
                    split_bc(u)
                if u[1] % 2 == 0 and step == T_NORM:
                    normalise(u, batch(u, 1, 1))
                if step == T_SMALL:
                    log1p_small(u)
                if step == T_ADD:
                    add_dt(u)
                    form_dtx(u)

            def unit(u, before=True, own=True, nxt=True):
                for step in range(NS if own else T_F4 + 1):
                    if before and step == T_F1:
                        gate(u)
                    if own and step + 1 < NS:
                        drive(u, step + 1)
                    elif nxt:
                        drive(after(u), 0)
                    if own:
                        scan(u, step)
                    if before and step == T_F3:
                        residual(u)
                    if before and step == T_F4:
                        accumulate(u)
                    if own and u[1] % 2 == 0 and step == T_TAKE:
                        take_tokens(u)
                    if nxt:
                        prepare(u, step)

            dve.sem_inc(acc_v, 1)
            for x in da:
                nc.vector.memset(x[:, :, :], 0.0)
            for x in dbx:
                nc.vector.memset(x[:, :, :], 0.0)
            nc.vector.memset(xraw[:, :, :], 0.0)
            nc.vector.memset(mv[:, :, :], 1.0)
            nc.vector.memset(ss[:, :], 1.0)
            nc.vector.memset(ones[:, :], 1.0)
            nc.vector.memset(eps_c[:, 0:1], EPS)
            nc.vector.memset(eps_c[:, 1:2], 1.0 + LOG_T).then_inc(setup_v, 1)
            dve.wait_ge(setup_v, 1)
            dve.wait_ge(setup_a, 3)
            nc.vector.tensor_scalar(tok_x, tok_rows[:, 3, :], EPS, None, ALU.add).then_inc(setup_v, 1)
            dve.wait_ge(setup_v, 2)
            dve.wait_ge(setup_p, 2)
            nc.vector.tensor_tensor(tok_scale[:, :], tok_scale[:, :], tok_rows[:, 0, :], ALU.mult).then_inc(setup_v, 1)
            dve.wait_ge(setup_v, 3)
            nc.vector.tensor_tensor(tok_rows[:, 2, :], tok_rows[:, 2, :], tok_scale[:, :], ALU.mult).then_inc(setup_v, 1)
            dve.wait_ge(setup_v, 4)
            nc.vector.tensor_tensor(tok_shift[:, :], tok_rows[:, 1, :], tok_rows[:, 2, :], ALU.subtract).then_inc(setup_v, 1)
            for d in range(2):
                nc.vector.tensor_scalar(neg_a[d][:, :, :], neg_a[d][:, :, :], -1.0, None, ALU.mult).then_inc(setup_v, 1)
                for c in range(2):
                    nc.vector.tensor_scalar(w_in[d][:, c, :], w_in[d][:, c, :], norm[d][:, c:c + 1], None, ALU.mult).then_inc(setup_v, 1)
            dve.wait_ge(setup_v, 11)
            dve.sem_inc(setup_done, 1)
            tokens(PROLOGUE, 0)
            normalise(PROLOGUE, 0)
            for step in range(NS):
                prepare(PROLOGUE, step)
            drive((0, 0), 0)
            unit((0, 0), before=False)
            with dve.Fori(0, B - 1) as i:
                for u in units(i):
                    unit(u)
            unit((0, 2 * B - 1), nxt=False)
            unit((0, 2 * B), own=False, nxt=False)

        @block.gpsimd
        def _(pool):
            def drive(u, n):
                if n not in POOL_B:
                    return
                d = u[1] % 2
                if n == POOL_B[0]:
                    pool.wait_ge(dtx_done, cnt(u, 1, 1))
                pool.wait_ge(bc_copied, cnt(u, NS, n + 1))
                pool.wait_ge(h_done, cnt(u, NS, n + 1 - NX))
                nc.gpsimd.tensor_tensor(dbx[n % NX][:, :, d:d + L], dtx[d][:, :, :],
                                        bc[n % NB][:, 0, None, 0:L].to_broadcast([128, EC, L]), ALU.mult).then_inc(dbx_p, 1)

            def weigh(u, n):
                d = u[1] % 2
                pool.wait_ge(h_done, cnt(u, NS, n + 1))
                if later(due := cnt(u, NS, n + 1 - NP)):
                    pool.wait_ge(sum_done, due)
                nc.gpsimd.tensor_tensor(pr[n % NP][:, :, 0:L], hs[n % NH][:, :, d:d + L],
                                        bc[n % NB][:, 1, None, 0:L].to_broadcast([128, EC, L]), ALU.mult).then_inc(p_done, 1)

            def token_power(q):
                pool.wait_ge(tok_v, q * 10 + 10)
                if later(due := q * 2):
                    pool.wait_ge(moved, due)
                nc.gpsimd.tensor_tensor(scales[:, :, :].rearrange("p a b -> p (a b)"), norm_x[:, :, :].rearrange("p a b -> p (a b)"),
                                        half[:, 0:6], ALU.pow).then_inc(tok_q, 1)

            def unit_power(u):
                pool.wait_ge(ss_done, cnt(u, 4))
                pool.wait_ge(acc_v, cnt(u, 5, 1 - 5))
                nc.gpsimd.tensor_tensor(rms[:, :], ss[:, :], half[:, 0:3], ALU.pow).then_inc(q_done, 1)

            def unit(u, before=True, own=True, nxt=True):
                for step in range(NS if own else T_SQ + 1):
                    if own and step + 1 < NS:
                        drive(u, step + 1)
                    elif nxt:
                        drive(after(u), 0)
                    if step >= 1 and own:
                        weigh(u, step - 1)
                    elif step == 0 and before:
                        weigh(after(u, -1), NS - 1)
                    if before and step == T_SQ:
                        unit_power(u)
                    if nxt and u[1] % 2 == 0 and step == T_TOKQ:
                        token_power(batch(u, 1, 1))

            pool.sem_inc(q_done, 1)
            nc.gpsimd.memset(half[:, :], -0.5).then_inc(setup_p, 1)
            pool.wait_ge(setup_p, 1)
            pool.wait_ge(setup_v, 2)
            nc.gpsimd.tensor_tensor(tok_scale[:, :], tok_x, half[:, 0:1].to_broadcast([128, D]), ALU.pow).then_inc(setup_p, 1)
            token_power(0)
            unit((0, 0), before=False)
            with pool.Fori(0, B - 1) as i:
                for u in units(i):
                    unit(u)
            unit((0, 2 * B - 1), nxt=False)
            unit((0, 2 * B), own=False, nxt=False)


T_F1, T_F2, T_F3, T_SQ, T_F4, T_TAKE = 2, 3, 4, 5, 6, 7
T_IN = [0, 1, 4, 5]
T_CONV = [2, 3, 5]
T_SILU = 7
T_X = 7
T_DT = [8, 9]
T_SMALL = 11
T_LN = 12
T_ADD = 13
T_TOK, T_TOKV, T_TOKQ, T_NORM, T_TOKT = 6, 8, 9, 10, 11


def experts(nc, t, h2_dram, x_dram, y_dram, out):
    ctx = ExitStack()
    with ctx:
        def sb(name, shape, dt=F32):
            return ctx.enter_context(nc.sbuf_tensor(name, shape, dt))

        def pb(name, shape):
            return ctx.enter_context(nc.psum_tensor(name, shape, F32))

        def sem(name):
            return ctx.enter_context(nc.semaphore(name))

        def later(value):
            return not isinstance(value, int) or value > 0

        flip_id = sb("flip_id", [128, 128])
        before = sb("before", [128, 128], BF16)
        all_ones = sb("all_ones", [128, 128], BF16)
        one1 = sb("one1", [1, 1])
        w_sel = sb("w_sel", [128, 2, X])
        iota_x = sb("iota_x", [128, X])
        iota_p = sb("iota_p", [X, PAGES])
        index_x = sb("index_x", [X, 128])
        ones_x = sb("ones_x", [128, X])

        h_all = sb("h_all", [128, NT, D])
        stats = [sb(f"stats{j}", [128, 6]) for j in range(2)]
        mv2 = [sb(f"mv2_{j}", [128, 2]) for j in range(2)]
        mean = sb("mean", [128, NT])
        var_x = sb("var_x", [128, NT])
        rstd = sb("rstd", [128, NT])
        shift = sb("shift", [128, NT])
        minus_half = sb("minus_half", [128, NT])
        minus_one = sb("minus_one", [128, NT * TOPK])
        inv_e = sb("inv_e", [128, NT * TOPK])
        vals = sb("vals", [128, NT, TOPK])
        gates = sb("gates", [128, NT, TOPK])
        pos_all = sb("pos_all", [128, NT, TOPK])

        hn = [sb(f"hn{j}", [128, D]) for j in range(G)]
        hn_t = [sb(f"hn_t{j}", [128, 2, 128]) for j in range(2)]
        lg = sb("lg", [128, X])
        top = sb("top", [128, 8])
        top_i = sb("top_i", [128, 8], U32)
        top_f = sb("top_f", [128, TOPK])
        oh = [sb(f"oh{j}", [128, TOPK, X], BF16) for j in range(2)]
        at = sb("at", [128, TOPK, X])
        pos_f = sb("pos_f", [128, TOPK])
        pos = [sb(f"pos{j}", [128, TOPK], I32) for j in range(G)]
        nxt = sb("nxt", [128, X])
        room = sb("room", [128, X])
        end = sb("end", [128, X])
        given = sb("given", [128, 1])
        flag = sb("flag", [128, X])
        upto = sb("upto", [128, X])
        page0 = sb("page0", [128, X])
        jump = sb("jump", [128, X])
        over = sb("over", [128, X])
        slot = sb("slot", [128, X])
        fjump = sb("fjump", [128, X])
        fresh = [sb(f"fresh{j}", [1, X]) for j in range(2)]
        owner = sb("owner", [X, PAGES])
        owner_i = sb("owner_i", [1, PAGES], I32)

        xs = [sb(f"xs{j}", [128, D]) for j in range(S)]
        wx = [sb(f"wx{j}", [128, 2 * HX + D]) for j in range(S)]
        xs_t = [sb(f"xs_t{j}", [128, 2, 128]) for j in range(2)]
        hid = [sb(f"hid{j}", [128, 128]) for j in range(2)]
        ys = [sb(f"ys{j}", [128, D]) for j in range(S)]

        rows = [sb(f"rows{j}", [128, TOPK, D]) for j in range(G)]
        res = [sb(f"res{j}", [128, D]) for j in range(G)]

        tp_ps = [pb(f"tp_ps{j}", [128, 512]) for j in range(2)]
        up_ps = [pb(f"up_ps{j}", [128, 512]) for j in range(2)]
        dn_ps = [pb(f"dn_ps{j}", [128, 512]) for j in range(2)]
        col_ps = pb("col_ps", [128, 512])

        consts = sem("consts")
        h_in = sem("h_in")
        set_v = sem("set_v")
        set_p = sem("set_p")
        stat_v = sem("stat_v")
        power_v = sem("power_v")
        power_p = sem("power_p")
        hn_done = sem("hn_done")
        tp_mm = sem("tp_mm")
        hn_t_done = sem("hn_t_done")
        lg_mm = sem("lg_mm")
        pick = sem("pick")
        cnt_mm = sem("cnt_mm")
        place = sem("place")
        fresh_done = sem("fresh_done")
        col_mm = sem("col_mm")
        owner_v = sem("owner_v")
        pos_done = sem("pos_done")
        pool_go = sem("pool_go")
        scattered = [sem(f"scattered{j}") for j in range(G)]
        owner_mm = sem("owner_mm")
        owner_done = sem("owner_done")
        gate_p = sem("gate_p")
        gate_v = sem("gate_v")
        xs_in = [sem(f"xs_in{j}") for j in range(S)]
        wx_in = [sem(f"wx_in{j}") for j in range(S)]
        xt_mm = sem("xt_mm")
        xt_done = sem("xt_done")
        hid_mm = sem("hid_mm")
        hid_done = sem("hid_done")
        y_mm = sem("y_mm")
        y_done = sem("y_done")
        y_sent = [sem(f"y_sent{j}") for j in range(S)]
        pages_done = sem("pages_done")
        posg_done = sem("posg_done")
        rows_in = [sem(f"rows_in{j}") for j in range(G)]
        sum_v = sem("sum_v")
        out_sent = [sem(f"out_sent{j}") for j in range(G)]

        block = ctx.enter_context(nc.Block())
        h_rows = h2_dram.rearrange("b t d -> (b t) d")
        out_rows = out.rearrange("b t d -> (b t) d")
        pages_x = x_dram.rearrange("(j p) d -> j p d", p=128)
        pages_y = y_dram.rearrange("(j p) d -> j p d", p=128)
        CH = 12
        chunks = [(a, min(a + CH, NT - 1)) for a in range(0, NT - 1, CH)]
        NV_PICK = 6
        NV_PLACE = 18

        def no(r, k, per=G):
            return r * per + k

        def over_all(eng, step, total, per):
            groups = (total - 2 * per) // per
            for k in range(per):
                step(0, k)
            if groups > 0:
                with eng.Fori(1, 1 + groups) as r:
                    for k in range(per):
                        step(r, k)
            for n in range(per * (1 + groups), total):
                step(n // per, n % per)

        def is_last(r, k, ahead, total, per=G):
            return isinstance(r, int) and r * per + k + ahead >= total

        def of_tile(x, i):
            if isinstance(i, int):
                return x[:, i, :]
            return x[:, bass.ds(i, 1), :].rearrange("p a d -> p (a d)")

        def col(x, i):
            return x[:, i:i + 1] if isinstance(i, int) else x[:, bass.ds(i, 1)]

        def page_of(x, j):
            return x[j] if isinstance(j, int) else x[bass.ds(j, 1), :, :].rearrange("a p d -> (a p) d")

        @block.sync
        def _(sp):
            for dst, src in ((flip_id[:, :], t["ident"]), (before[:, :], t["before"]), (all_ones[:, :], t["all_ones"]),
                             (w_sel[:, :, :], t["sel_w"]), (iota_x[:, :], t["iota_x"]),
                             (iota_p[:, :], t["iota_p"]), (index_x[:, :], t["index_x"])):
                sp.dma_start(dst, src).then_inc(consts, 16)
            for c, (a, b) in enumerate(chunks):
                if later(due := 16 * c):
                    sp.wait_ge(h_in, due)
                sp.dma_start(h_all[:, a:b, :], h_rows[a * 128:b * 128, :].rearrange("(i p) d -> p i d", p=128)).then_inc(h_in, 16)
            sp.wait_ge(h_in, 16 * len(chunks))
            sp.wait_ge(set_v, 1)
            sp.dma_start(h_all[0:LAST, NT - 1, :], h_rows[(NT - 1) * 128:N, :]).then_inc(h_in, 16)

            def load(r, k):
                j = no(r, k, S)
                s = k % S
                if later(due := no(r, k + 1 - S, S)):
                    sp.wait_ge(y_mm, due)
                sp.dma_start(xs[s][:, :], page_of(pages_x, j)).then_inc(xs_in[s], 16)
                at_j = owner_i[0:1, j:j + 1] if isinstance(j, int) else owner_i[0:1, bass.ds(j, 1)]
                e = sp.value_load(at_j, min_val=0, max_val=X - 1)
                sp.dma_start(wx[s][:, :], t["experts"][bass.ds(e, 1), :, :].rearrange("a p n -> (a p) n")).then_inc(wx_in[s], 16)

            def page(r, k):
                j = no(r, k, S)
                sp.wait_ge(y_done, j + 1)
                sp.dma_start(page_of(pages_y, j), ys[k % S][:, :]).then_inc(y_sent[k % S], 16)
                if not is_last(r, k, S, PAGES, S):
                    load(r, k + S)

            for s in range(G):
                sp.wait_ge(scattered[s], 64 * len(range(s, NT, G)))
            sp.wait_ge(owner_done, 1)
            for k in range(S):
                load(0, k)
            over_all(sp, page, PAGES, S)
            for s in range(S):
                sp.wait_ge(y_sent[s], 16 * (PAGES // S))
            sp.sem_inc(pages_done, 1)

            def store(r, k):
                i = no(r, k)
                sp.wait_ge(sum_v, i * 5 + 4)
                if isinstance(i, int):
                    n = LAST if i == NT - 1 else 128
                    dst, src = out_rows[i * 128:i * 128 + n, :], res[k][0:n, :]
                else:
                    dst, src = out_rows[bass.ds(i * 128, 128), :], res[k][:, :]
                sp.dma_start(dst, src).then_inc(out_sent[k], 16)

            over_all(sp, store, NT, G)
            for s in range(G):
                sp.wait_ge(out_sent[s], 16 * len(range(s, NT, G)))

        @block.tensor
        def _(pe):
            pe.wait_ge(consts, 16 * 7)
            pe.wait_ge(set_v, 1)

            def logits(r, k):
                i, p = no(r, k), k % 2
                pe.wait_ge(hn_done, i + 1)
                if later(due := i - 1):
                    pe.wait_ge(hn_t_done, due)
                for c in range(2):
                    mm = nc.tensor.transpose(tp_ps[p][:, c * 128:(c + 1) * 128], hn[k % G][:, c * 128:(c + 1) * 128], flip_id[:, :])
                mm.then_inc(tp_mm, 1)
                pe.wait_ge(hn_t_done, i + 1)
                if later(due := (i - 2) * NV_PICK + 1):
                    pe.wait_ge(pick, due)
                for c in range(2):
                    mm = nc.tensor.matmul(up_ps[p][:, 0:X], hn_t[p][:, c, :], w_sel[:, c, :], start=(c == 0), stop=(c == 1))
                mm.then_inc(lg_mm, 1)

            def fresh_column(r, k):
                i, p = no(r, k), k % 2
                pe.wait_ge(fresh_done, i + 1)
                pe.wait_ge(owner_v, i + 1)
                nc.tensor.matmul(col_ps[0:X, p:p + 1], fresh[p][0:1, :], one1[:, :], start=True, stop=True).then_inc(col_mm, 1)

            def tile(r, k):
                i, p = no(r, k), k % 2
                if not is_last(r, k, 2, NT):
                    logits(r, k + 2)
                pe.wait_ge(pick, i * NV_PICK + NV_PICK)
                if later(due := (i - 1) * NV_PLACE):
                    pe.wait_ge(place, due)
                for q in range(TOPK):
                    nc.tensor.matmul(dn_ps[p][:, 0:X], before[:, :], oh[p][:, q, :], start=(q == 0), stop=(q == TOPK - 1))
                for q in range(TOPK):
                    mm = nc.tensor.matmul(dn_ps[p][:, X:2 * X], all_ones[:, :], oh[p][:, q, :], start=(q == 0), stop=(q == TOPK - 1))
                mm.then_inc(cnt_mm, 1)
                if not (isinstance(r, int) and r == 0 and k == 0):
                    fresh_column(r, k - 1)

            logits(0, 0)
            logits(0, 1)
            over_all(pe, tile, NT, G)
            fresh_column(0, NT - 1)
            pe.wait_ge(owner_v, 1 + NT)
            nc.tensor.matmul(col_ps[:, 0:PAGES], index_x[:, :], owner[:, :], start=True, stop=True).then_inc(owner_mm, 1)

            def flip(r, k):
                j, s, p = no(r, k, S), k % S, k % 2
                pe.wait_ge(xs_in[s], (r + (k // S)) * 16 + 16)
                if later(due := j - 1):
                    pe.wait_ge(xt_done, due)
                for c in range(2):
                    mm = nc.tensor.transpose(tp_ps[p][:, c * 128:(c + 1) * 128], xs[s][:, c * 128:(c + 1) * 128], flip_id[:, :])
                mm.then_inc(xt_mm, 1)

            def up(r, k):
                j, s, p = no(r, k, S), k % S, k % 2
                pe.wait_ge(wx_in[s], (r + (k // S)) * 16 + 16)
                if later(due := j - 1):
                    pe.wait_ge(hid_done, due)
                pe.wait_ge(xt_done, j + 1)
                for c in range(2):
                    mm = nc.tensor.matmul(up_ps[p][:, 0:128], wx[s][:, c * HX:(c + 1) * HX], xs_t[p][:, c, :], start=(c == 0), stop=(c == 1))
                mm.then_inc(hid_mm, 1)

            def down(r, k):
                j, s, p = no(r, k, S), k % S, k % 2
                if later(due := j - 1):
                    pe.wait_ge(y_done, due)
                pe.wait_ge(hid_done, j + 1)
                nc.tensor.matmul(dn_ps[p][:, 0:D], hid[p][:, :], wx[s][:, 2 * HX:2 * HX + D], start=True, stop=True).then_inc(y_mm, 1)

            def page(r, k):
                if not is_last(r, k, 2, PAGES, S):
                    flip(r, k + 2)
                if not is_last(r, k, 1, PAGES, S):
                    up(r, k + 1)
                down(r, k)

            flip(0, 0)
            flip(0, 1)
            up(0, 0)
            over_all(pe, page, PAGES, S)

        @block.scalar
        def _(act):
            def normalise(r, k):
                i = no(r, k)
                if later(due := (r + (k // G)) * 64):
                    act.wait_ge(scattered[k % G], due)
                nc.scalar.activation(hn[k % G][:, :], of_tile(h_all, i), ACT.Identity, bias=col(shift, i), scale=col(rstd, i)).then_inc(hn_done, 1)

            def tile(r, k):
                i, p = no(r, k), k % 2
                act.wait_ge(tp_mm, i + 1)
                if later(due := i - 1):
                    act.wait_ge(lg_mm, due)
                nc.scalar.copy(hn_t[p][:, :, :].rearrange("p a b -> p (a b)"), tp_ps[p][:, 0:D]).then_inc(hn_t_done, 1)
                if not is_last(r, k, 1, NT):
                    normalise(r, k + 1)

            act.wait_ge(power_p, 2)
            normalise(0, 0)
            over_all(act, tile, NT, G)

            def page(r, k):
                j, p = no(r, k, S), k % 2
                if not is_last(r, k, 1, PAGES, S):
                    relu(r, k + 1)
                act.wait_ge(y_mm, j + 1)
                if later(due := r * 16):
                    act.wait_ge(y_sent[k % S], due)
                nc.scalar.copy(ys[k % S][:, :], dn_ps[p][:, 0:D]).then_inc(y_done, 1)

            def relu(r, k):
                j, p = no(r, k, S), k % 2
                if later(due := j - 1):
                    act.wait_ge(y_mm, due)
                act.wait_ge(hid_mm, j + 1)
                nc.scalar.activation(hid[p][:, :], up_ps[p][:, 0:128], ACT.Relu).then_inc(hid_done, 1)

            relu(0, 0)
            over_all(act, page, PAGES, S)

        @block.vector
        def _(dve):
            V = nc.vector
            V.memset(h_all[:, NT - 1, :], 0.0)
            V.memset(one1[:, :], 1.0)
            V.memset(ones_x[:, :], 1.0)
            for x in (nxt, room, end):
                V.memset(x[:, :], 0.0)
            V.memset(given[:, :], 0.0)
            V.memset(owner[:, :], 0.0).then_inc(set_v, 1)
            dve.wait_ge(set_v, 1)
            dve.sem_inc(owner_v, 1)

            def measure(r, k):
                i, p = no(r, k), k % 2
                V.bn_stats(stats[p][:, :], of_tile(h_all, i)).then_inc(stat_v, 1)
                dve.wait_ge(stat_v, i * 4 + 1)
                dve.sem_inc(stat_v, 1)
                V.bn_aggr(mv2[p][:, :], stats[p][:, :]).then_inc(stat_v, 1)
                dve.wait_ge(stat_v, i * 4 + 3)
                V.tensor_scalar(col(mean, i), mv2[p][:, 0:1], -1.0, None, ALU.mult)
                V.tensor_scalar(col(var_x, i), mv2[p][:, 1:2], EPS, None, ALU.add).then_inc(stat_v, 1)

            dve.wait_ge(h_in, 16 * (len(chunks) + 1))
            over_all(dve, measure, NT, G)
            dve.wait_ge(stat_v, NT * 4)
            dve.sem_inc(power_v, 1)

            def choose(r, k):
                i, p = no(r, k), k % 2
                c = i * NV_PICK
                dve.wait_ge(lg_mm, i + 1)
                V.tensor_scalar(lg[:, :], up_ps[p][:, 0:X], SATURATED, None, ALU.min).then_inc(pick, 1)
                dve.wait_ge(pick, c + 1)
                dve.sem_inc(pick, 1)
                V.max(top[:, :], lg[:, :]).then_inc(pick, 1)
                dve.wait_ge(pick, c + 3)
                V.tensor_copy(of_tile(vals, i), top[:, 0:TOPK])
                V.max_index(top_i[:, :], top[:, :], lg[:, :]).then_inc(pick, 1)
                dve.wait_ge(pick, c + 4)
                V.tensor_copy(top_f[:, :], top_i[:, 0:TOPK]).then_inc(pick, 1)
                dve.wait_ge(pick, c + 5)
                if later(due := i - 1):
                    dve.wait_ge(cnt_mm, due)
                V.tensor_tensor(oh[p][:, :, :], iota_x[:, None, :].to_broadcast([128, TOPK, X]),
                                top_f[:, :, None].to_broadcast([128, TOPK, X]), ALU.is_equal).then_inc(pick, 1)

            def find_slots(r, k):
                i, p = no(r, k), k % 2
                c = i * NV_PLACE
                pre, tot = dn_ps[p][:, 0:X], dn_ps[p][:, X:2 * X]
                dve.wait_ge(cnt_mm, i + 1)
                if later(due := c):
                    dve.wait_ge(place, due)
                V.tensor_tensor(flag[:, :], tot, room[:, :], ALU.is_gt).then_inc(place, 1)
                V.tensor_tensor(over[:, :], pre, room[:, :], ALU.is_ge).then_inc(place, 1)
                V.tensor_tensor(slot[:, :], pre, nxt[:, :], ALU.add).then_inc(place, 1)
                dve.wait_ge(place, c + 1)
                V.tensor_tensor_scan(upto[:, :], ones_x[:, :], flag[:, :], given[:, 0:1], ALU.mult, ALU.add).then_inc(place, 1)
                V.tensor_tensor(room[:, :], room[:, :], tot, ALU.subtract).then_inc(place, 1)
                dve.wait_ge(place, c + 4)
                V.tensor_tensor(page0[:, :], upto[:, :], flag[:, :], ALU.subtract).then_inc(place, 1)
                V.tensor_copy(given[:, :], upto[:, X - 1:X]).then_inc(place, 1)
                dve.wait_ge(place, c + 6)
                V.scalar_tensor_tensor(jump[:, :], page0[:, :], 128.0, end[:, :], ALU.mult, ALU.subtract).then_inc(place, 1)
                if later(due := i - 1):
                    dve.wait_ge(col_mm, due)
                V.scalar_tensor_tensor(fresh[p][:, :], page0[0:1, :], 1.0, flag[0:1, :], ALU.add, ALU.mult).then_inc(fresh_done, 1)
                V.tensor_tensor(nxt[:, :], nxt[:, :], tot, ALU.add).then_inc(place, 1)
                dve.wait_ge(place, c + 8)
                V.tensor_tensor(over[:, :], over[:, :], jump[:, :], ALU.mult).then_inc(place, 1)
                V.tensor_tensor(fjump[:, :], flag[:, :], jump[:, :], ALU.mult).then_inc(place, 1)
                dve.wait_ge(place, c + 10)
                V.tensor_tensor(slot[:, :], slot[:, :], over[:, :], ALU.add).then_inc(place, 1)
                V.scalar_tensor_tensor(room[:, :], flag[:, :], 128.0, room[:, :], ALU.mult, ALU.add).then_inc(place, 1)
                dve.wait_ge(place, c + 12)
                V.tensor_tensor(at[:, :, :], oh[p][:, :, :], slot[:, None, :].to_broadcast([128, TOPK, X]), ALU.mult).then_inc(place, 1)
                V.tensor_tensor(nxt[:, :], nxt[:, :], fjump[:, :], ALU.add).then_inc(place, 1)
                dve.wait_ge(place, c + 14)
                V.tensor_reduce(pos_f[:, :], at[:, :, :], axis=AX.X, op=ALU.add).then_inc(place, 1)
                dve.wait_ge(place, c + 15)
                V.tensor_tensor(end[:, :], nxt[:, :], room[:, :], ALU.add).then_inc(place, 1)
                dve.wait_ge(place, c + 16)
                V.tensor_copy(of_tile(pos_all, i), pos_f[:, :])
                if later(due := (r + (k // G)) * 64):
                    dve.wait_ge(scattered[k % G], due)
                V.tensor_copy(pos[k % G][:, :], pos_f[:, :]).then_inc(pos_done, 1)
                dve.sem_inc(place, 1)

            def note_owner(r, k):
                i, p = no(r, k), k % 2
                dve.wait_ge(col_mm, i + 1)
                dve.wait_ge(owner_v, i + 1)
                V.scalar_tensor_tensor(owner[:, :], iota_p[:, :], col_ps[0:X, p:p + 1], owner[:, :], ALU.is_equal, ALU.add).then_inc(owner_v, 1)

            def tile(r, k):
                if not is_last(r, k, 1, NT):
                    choose(r, k + 1)
                find_slots(r, k)
                if not (isinstance(r, int) and r == 0 and k == 0):
                    note_owner(r, k - 1)

            dve.wait_ge(consts, 16 * 7)
            choose(0, 0)
            over_all(dve, tile, NT, G)
            note_owner(0, NT - 1)
            dve.wait_ge(owner_mm, 1)
            V.tensor_copy(owner_i[:, :], col_ps[0:1, 0:PAGES]).then_inc(owner_done, 1)
            dve.wait_ge(gate_p, 1)
            V.tensor_scalar(gates[:, :, :], gates[:, :, :], 1.0, None, ALU.add).then_inc(gate_v, 1)

            def page(r, k):
                j, p = no(r, k, S), k % 2
                if later(due := j - 1):
                    dve.wait_ge(hid_mm, due)
                dve.wait_ge(xt_mm, j + 1)
                V.tensor_copy(xs_t[p][:, :, :].rearrange("p a b -> p (a b)"), tp_ps[p][:, 0:D]).then_inc(xt_done, 1)

            over_all(dve, page, PAGES, S)

            def take_slots(r, k):
                V.tensor_copy(pos[k % G][:, :], of_tile(pos_all, no(r, k))).then_inc(posg_done, 1)

            def combine(r, k):
                i, s = no(r, k), k % G
                dve.wait_ge(rows_in[s], r * 64 + 64)
                if later(due := r * 16):
                    dve.wait_ge(out_sent[s], due)
                for q in range(TOPK):
                    if q:
                        dve.wait_ge(sum_v, i * 5 + q)
                    other = res[s][:, :] if q else of_tile(h_all, i)
                    gate = col(gates[:, :, :].rearrange("p i q -> p (i q)"), i * TOPK + q)
                    V.scalar_tensor_tensor(res[s][:, :], rows[s][:, q, :], gate, other, ALU.mult, ALU.add).then_inc(sum_v, 1)
                dve.wait_ge(sum_v, i * 5 + 4)
                dve.sem_inc(sum_v, 1)
                if not is_last(r, k, G, NT):
                    take_slots(r, k + G)

            for k in range(G):
                take_slots(0, k)
            dve.wait_ge(gate_p, 2)
            over_all(dve, combine, NT, G)

        @block.gpsimd
        def _(pool):
            P = nc.gpsimd
            P.memset(minus_half[:, :], -0.5)
            P.memset(minus_one[:, :], -1.0)
            P.memset(inv_e[:, :], float(np.exp(-1.0))).then_inc(set_p, 1)
            pool.wait_ge(set_p, 1)
            pool.wait_ge(power_v, 1)
            P.tensor_tensor(rstd[:, :], var_x[:, :], minus_half[:, :], ALU.pow).then_inc(power_p, 1)
            pool.wait_ge(power_p, 1)
            P.tensor_tensor(shift[:, :], mean[:, :], rstd[:, :], ALU.mult).then_inc(power_p, 1)

            def scatter(r, k):
                i, s = no(r, k), k % G
                pool.wait_ge(pos_done, i + 1)
                pool.sem_inc(pool_go, 1)
                for q in range(TOPK):
                    P.indirect_dma_start(x_dram[:, :], bass.IndirectOffsetOnAxis(ap=pos[s][:, q:q + 1], axis=0),
                                         hn[s][:, :], None).then_inc(scattered[s], 16)

            over_all(pool, scatter, NT, G)
            flat = lambda x: x[:, :, :].rearrange("p i q -> p (i q)")
            P.tensor_tensor(flat(gates), inv_e[:, :], flat(vals), ALU.pow).then_inc(gate_p, 1)
            pool.wait_ge(gate_v, 1)
            P.tensor_tensor(flat(gates), flat(gates), minus_one[:, :], ALU.pow).then_inc(gate_p, 1)

            def gather(r, k):
                i, s = no(r, k), k % G
                pool.wait_ge(posg_done, i + 1)
                pool.sem_inc(pool_go, 1)
                for q in range(TOPK):
                    P.indirect_dma_start(rows[s][:, q, :], None, y_dram[:, :],
                                         bass.IndirectOffsetOnAxis(ap=pos[s][:, q:q + 1], axis=0)).then_inc(rows_in[s], 16)

            pool.wait_ge(pages_done, 1)
            over_all(pool, gather, NT, G)


def scan_arrays(ins):
    n = {k: np.asarray(v) for k, v in ins.items()}
    c = np.ascontiguousarray
    a = {"x": c(n["x"].transpose(0, 2, 1)), "tok_w": c(n["L0_tok_W"].T.reshape(CTX, 128, D).transpose(1, 0, 2)),
         "tok_b": n["L0_tok_b"], "tok_gamma": n["L0_tok_gamma"], "tok_beta": n["L0_tok_beta"],
         "tok_mean": n["L0_tok_running_mean"], "tok_var": n["L0_tok_running_var"], "normf": n["L0_attn_normf"],
         "ident": np.eye(128, dtype=np.float32)}
    s = np.zeros((96, 2 * NS, 128), mybir.dt.np(BF16))
    for j in range(2 * NS):
        for q in range(3):
            s[32 * q + j, j, :] = 1
    a["sel"] = s
    chunks = lambda w: c(w.reshape(-1, 128, *w.shape[1:]).swapaxes(0, 1))
    for d, pre in enumerate(("L0_attn_fwd_", "L0_attn_bwd_")):
        g = lambda k: n[pre + k]
        a[f"in{d}"] = chunks(g("inproj").T)
        a[f"xdt{d}"] = chunks(g("xproj")[:R].T)
        a[f"xbc{d}"] = chunks(np.concatenate([g("xproj")[R:].T] * 3, axis=1))
        a[f"dtw{d}"] = c(g("dtw").T)
        a[f"out{d}"] = chunks(g("outproj").T)
        a[f"vec{d}"] = chunks(np.concatenate([g("convw"), g("convb")[:, None], g("dtb")[:, None], g("Dp")[:, None], g("Alog")], axis=1))
        a[f"norm{d}"] = c(g("norm").reshape(2, 128).T)
    return a


def expert_arrays(ins):
    c = np.ascontiguousarray
    sel, keys, values = (np.asarray(ins["L0_ffn_" + k]) for k in ("expert_sel", "keys", "values"))
    k2 = keys.reshape(X, 2, 128, HX).transpose(0, 2, 1, 3).reshape(X, 128, 2 * HX)
    return {"before": np.triu(np.ones((128, 128)), 1).astype(mybir.dt.np(BF16)),
            "all_ones": np.ones((128, 128), mybir.dt.np(BF16)),
            "sel_w": c(sel.T.reshape(2, 128, X).transpose(1, 0, 2)),
            "iota_x": c(np.broadcast_to(np.arange(X, dtype=np.float32), (128, X))),
            "iota_p": c(np.broadcast_to(np.arange(1, PAGES + 1, dtype=np.float32), (X, PAGES))),
            "index_x": c(np.broadcast_to(np.arange(X, dtype=np.float32)[:, None], (X, 128))),
            "zeros": np.zeros((128, D), np.float32),
            "experts": c(np.concatenate([k2, values], axis=2))}


def build(nc, t, out):
    h2_dram = nc.dram_tensor("h2_dram", [B, L, D], F32).ap()
    x_dram = nc.dram_tensor("x_dram", [PAGES * 128, D], F32).ap()
    y_dram = nc.dram_tensor("y_dram", [PAGES * 128, D], F32).ap()
    tower(nc, t, h2_dram, x_dram)
    experts(nc, t, h2_dram, x_dram, y_dram, out)


def kernel(**inputs):
    import concourse.bacc as bacc
    from concourse.bass_utils import run_bass_kernel_spmd

    arrays = {**scan_arrays(inputs), **expert_arrays(inputs)}
    nc = bacc.Bacc("TRN2", target_bir_lowering=False, num_devices=1)
    t = {k: nc.dram_tensor("in_" + k, a.shape, mybir.dt.from_np(a.dtype), kind="ExternalInput").ap() for k, a in arrays.items()}
    out = nc.dram_tensor("out", [B, L, D], F32, kind="ExternalOutput").ap()
    build(nc, t, out)
    r = run_bass_kernel_spmd(nc, [{"in_" + k: a for k, a in arrays.items()}], core_ids=[0])
    return r.results[0]["out"]
```

```python
import numpy as np
import concourse.bass as bass
from concourse import mybir
from contextlib import ExitStack

F32 = mybir.dt.float32
BF16 = mybir.dt.bfloat16
I32 = mybir.dt.int32
U32 = mybir.dt.uint32
ALU = mybir.AluOpType
ACT = mybir.ActivationFunctionType
AX = mybir.AxisListType

B, TIN, DIN = 16, 375, 128
CTX = 5
L = TIN - CTX + 1
D = 256
E = 512
EC = E // 128
NS = 16
R = 64
TAPS = 4
LP = L + 1
TT = [(0, 128), (128, 128), (256, L - 256)]
EPS = 1e-5
POOL_B = (3, 8, 13)
LOG_T = 2.0 ** -5
LOG_C = (0.9999997716733988, -0.4998678486375896, 0.3219470998103213)
EXP_LN = "natural_log_exp_and_others"

N = B * L
NT = (N + 127) // 128
LAST = N - 128 * (NT - 1)
X = 64
HX = 128
TOPK = 4
SATURATED = 16.6355
GM = 4
GR = 8
G = 4
S = 6
S2 = S // 2
PAGES = (NT * 128 * TOPK + 127 * X) // 128
PAGES = (PAGES + S - 1) // S * S


def tower(nc, t, h2_dram, x_dram):
    ctx = ExitStack()
    with ctx:
        def sb(name, shape, dt=F32):
            return ctx.enter_context(nc.sbuf_tensor(name, shape, dt))

        def pb(name, shape):
            return ctx.enter_context(nc.psum_tensor(name, shape, F32))

        def sem(name):
            return ctx.enter_context(nc.semaphore(name))

        tokw = sb("tokw", [128, CTX, D])
        tok_rows = sb("tok_rows", [128, 5, D])
        tok_scale = sb("tok_scale", [128, D])
        tok_shift = sb("tok_shift", [128, D])
        tok_b = sb("tok_b", [1, D])
        ones = sb("ones", [1, 128])
        ident = sb("ident", [128, 128])
        sel = sb("sel", [96, 2 * NS, 128], BF16)
        w_in = [sb(f"w_in{d}", [128, 2, 2 * E]) for d in range(2)]
        w_dt = [sb(f"w_dt{d}", [128, EC, R]) for d in range(2)]
        w_bc = [sb(f"w_bc{d}", [128, EC, 96]) for d in range(2)]
        w_r = [sb(f"w_r{d}", [R, E]) for d in range(2)]
        w_out = [sb(f"w_out{d}", [128, EC, D]) for d in range(2)]
        NV = TAPS + 3 + NS
        vec = [sb(f"vec{d}", [128, EC, NV]) for d in range(2)]
        norm = [sb(f"norm{d}", [128, 2]) for d in range(2)]
        neg_a = [sb(f"neg_a{d}", [128, EC, NS]) for d in range(2)]
        eps_c = sb("eps_c", [128, 3])
        log_t = sb("log_t", [128, 1])

        x_t = sb("x_t", [128, TIN])
        h_new = sb("h_new", [128, 3, D])
        r_new = sb("r_new", [128, 3, D])
        h_cur = sb("h_cur", [128, 3, D])
        r_cur = sb("r_cur", [128, 3, D])
        u_tok = sb("u_tok", [128, 3, D])
        u_t = sb("u_t", [128, 2, L])
        bn = sb("bn", [128, 3, 6])
        mv = sb("mv", [128, 3, 2])
        scales = sb("scales", [128, 2, 3])
        norm_x = sb("norm_x", [128, 2, 3])
        half = sb("half", [128, 6])
        rms = sb("rms", [128, 3])


        xraw = sb("xraw", [128, EC, L + 2 * (TAPS - 1)])
        xc = [sb(f"xc{d}", [128, EC, L]) for d in range(2)]
        sz = [sb(f"sz{d}", [128, EC, L]) for d in range(2)]
        dt_ = [sb(f"dt{d}", [128, EC, L]) for d in range(2)]
        dtx = [sb(f"dtx{d}", [128, EC, L]) for d in range(2)]
        r_sb = sb("r_sb", [R, L])
        bcs = [sb(f"bcs{d}", [96, L], BF16) for d in range(2)]
        mid = sb("mid", [96, L], BF16)
        rest = sb("rest", [96, L])

        NA, NX, NH, NP, NB = 2, 2, 2, 2, 4
        da = [sb(f"da{j}", [128, EC, LP]) for j in range(NA)]
        dbx = [sb(f"dbx{j}", [128, EC, LP]) for j in range(NX)]
        hs = [sb(f"hs{j}", [128, EC, LP]) for j in range(NH)]
        pr = [sb(f"pr{j}", [128, EC, LP]) for j in range(NP)]
        bc = [sb(f"bc{j}", [128, 2, L + 1]) for j in range(NB)]

        y2 = sb("y2", [128, EC, L])
        s_tok = sb("s_tok", [128, 3, D])
        sq = sb("sq", [128, 3, D], BF16)
        ss = sb("ss", [128, 3])
        acc = sb("acc", [128, 3, D])

        tok_x = y2[:, 0, 0:D]
        y_ps = pb("y_ps", [128, EC, 512])
        bc_ps = pb("bc_ps", [128, 2, 512])
        misc = [pb(f"misc{j}", [128, 512]) for j in range(2)]

        loads = sem("loads")
        x_in = sem("x_in")
        setup_a = sem("setup_a")
        setup_v = sem("setup_v")
        setup_done = sem("setup_done")
        full = [sem(f"misc_full{j}") for j in range(2)]
        free = [sem(f"misc_free{j}") for j in range(2)]
        tok_v = sem("tok_v")
        tok_q = sem("tok_q")
        stats_go = sem("stats_go")
        setup_p = sem("setup_p")
        u_done = sem("u_done")
        uT_done = sem("uT_done")
        raw_done = sem("raw_done")
        conv = sem("conv")
        xc_done = sem("xc_done")
        sz_done = sem("sz_done")
        r_done = sem("r_done")
        bc_hi = sem("bc_hi")
        bc_v = sem("bc_v")
        sp_a = sem("sp_a")
        sp_v = sem("sp_v")
        dt_done = sem("dt_done")
        dtx_done = sem("dtx_done")
        bc_mm = sem("bc_mm")
        bc_copied = sem("bc_copied")
        da_done = sem("da_done")
        dbx_v = sem("dbx_v")
        dbx_p = sem("dbx_p")
        h_done = sem("h_done")
        p_done = sem("p_done")
        sum_done = sem("sum_done")
        y_read = sem("y_read")
        y2_done = sem("y2_done")
        out_mm = sem("out_mm")
        s_done = sem("s_done")
        ss_done = sem("ss_done")
        q_done = sem("q_done")
        acc_v = sem("acc_v")
        h2_sent = sem("h2_sent")
        zeroed = sem("zeroed")
        moved = sem("moved")

        NPOOL = len(POOL_B)
        NDVE = NS - NPOOL

        def later(value):
            return not isinstance(value, int) or value > 0

        def cnt(u, per, off=0):
            return u[0] * (2 * per) + (u[1] * per + off)

        def batch(u, per, off=0):
            return u[0] * per + ((u[1] // 2) * per + off)

        def after(u, by=1):
            return (u[0], u[1] + by)

        FIRST = ["x0", "x1", "z0", "z1", "tok", "x", "dt0", "dt1", "tokT"]
        FORWARD = ["x0", "x1", "out", "z0", "z1", "tok", "x", "dt0", "dt1", "tokT"]
        BACKWARD = ["x0", "x1", "out", "z0", "z1", "x", "dt0", "dt1"]
        PROLOGUE = (0, -1)

        def uses(u, what):
            k = u[1]
            if k == -1:
                return ["tok", "tokT", "x0", "x1", "z0", "z1", "x", "dt0", "dt1"].index(what)
            if k == 0:
                return 9 + FIRST.index(what)
            if k >= 2 * B - 1 > 2:
                return 18 * B + (k - (2 * B - 1))
            order = BACKWARD if k % 2 else FORWARD
            return u[0] * 18 + (18 * (k // 2) + (18 if k % 2 else 8) + order.index(what))

        units = lambda i: [(i, 1), (i, 2)]

        block = ctx.enter_context(nc.Block())

        N_LOADS = 0

        @block.sync
        def _(sp):
            nonlocal N_LOADS
            rows = ["tok_gamma", "tok_beta", "tok_mean", "tok_var", "normf"]
            todo = [(tokw[:, :, :], t["tok_w"]), (tok_b[:, :], t["tok_b"].rearrange("(a n) -> a n", a=1)),
                    (ident[:, :], t["ident"]), (sel[:, :, :], t["sel"])]
            for j, n in enumerate(rows):
                todo.append((tok_rows[:, j, :], t[n].rearrange("(a n) -> a n", a=1).to_broadcast([128, D])))
            for d in range(2):
                todo += [(w_in[d][:, :, :], t[f"in{d}"]), (w_dt[d][:, :, :], t[f"xdt{d}"]),
                         (w_bc[d][:, :, :], t[f"xbc{d}"]), (w_r[d][:, :], t[f"dtw{d}"]),
                         (w_out[d][:, :, :], t[f"out{d}"]), (vec[d][:, :, :], t[f"vec{d}"]),
                         (norm[d][:, :], t[f"norm{d}"])]
            sp.dma_start(x_t[:, :], t["x"][0]).then_inc(x_in, 16)
            for dst, src in todo:
                sp.dma_start(dst, src).then_inc(loads, 16)
            N_LOADS = 16 * len(todo)

            def load_x(src, token_products):
                sp.wait_ge(full[1], token_products)
                sp.dma_start(x_t[:, :], src).then_inc(x_in, 16)

            def store_h2(u):
                b = batch(u, 1, -1)
                sp.wait_ge(acc_v, cnt(u, 5, 1))
                for j, (t0, n) in enumerate(TT):
                    if isinstance(b, int):
                        dst = h2_dram[b, t0:t0 + n, :]
                    else:
                        dst = h2_dram[bass.ds(b, 1), t0:t0 + n, :].rearrange("a t d -> (a t) d")
                    sp.dma_start(dst, acc[0:n, j, :]).then_inc(h2_sent, 16)

            sp.sem_inc(h2_sent, 1)
            pages = x_dram.rearrange("(j p) d -> j p d", p=128)
            zeros = t["zeros"].rearrange("p (a d) -> a p d", a=1)
            ZERO = PAGES // (B - 2)
            load_x(t["x"][1], uses(PROLOGUE, "tok") + 1)
            with sp.Fori(0, B - 2) as i:
                sp.dma_start(pages[bass.ds(i * ZERO, ZERO), :, :], zeros.to_broadcast([ZERO, 128, D])).then_inc(zeroed, 16)
                load_x(t["x"][bass.ds(i + 2, 1), :, :].rearrange("a p n -> (a p) n"), i * 18 + (uses((0, 0), "tok") + 1))
                sp.wait_ge(zeroed, i * 16 + 16)
                store_h2((i, 2))
            load_x(t["x"][B - 1], 18 * (B - 2) + (uses((0, 0), "tok") + 1))
            store_h2((0, 2 * B - 2))
            store_h2((0, 2 * B))
            sp.wait_ge(h2_sent, 1 + 48 * B)
            sp.wait_ge(zeroed, 16 * (B - 2))

        @block.tensor
        def _(pe):
            def fill(j, u, what):
                if later(due := uses(u, what)):
                    pe.wait_ge(free[j], due)

            def tokens(u, q):
                pe.wait_ge(x_in, q * 16 + 16)
                for g in range(2):
                    fill(g, u, "tok")
                    for j in ((0, 1) if g == 0 else (2,)):
                        t0, n = TT[j]
                        out = misc[g][0:n, (j % 2) * D:(j % 2) * D + D]
                        for c in range(CTX):
                            nc.tensor.matmul(out, x_t[:, t0 + c:t0 + c + n], tokw[:, c, :], start=(c == 0), stop=False)
                        mm = nc.tensor.matmul(out, ones[0:1, 0:n], tok_b[:, :], start=False, stop=True)
                    mm.then_inc(full[g], 1)

            def tokens_t(u, q):
                pe.wait_ge(u_done, q * 3 + 3)
                for c in range(2):
                    fill(c, u, "tokT")
                    for j, (t0, n) in enumerate(TT):
                        mm = nc.tensor.transpose(misc[c][:, t0:t0 + n], u_tok[0:n, j, c * 128:(c + 1) * 128],
                                                 ident[0:n, 0:n])
                    mm.then_inc(full[c], 1)

            def inproj(u, m):
                p, d = after(u), (u[1] + 1) % 2
                if m == 0:
                    pe.wait_ge(uT_done, batch(p, 2, 2))
                j = m % 2
                fill(j, u, ("x0", "x1", "z0", "z1")[m // 2])
                for c in range(2):
                    mm = nc.tensor.matmul(misc[j][:, 0:L], w_in[d][:, c, m * 128:(m + 1) * 128], u_t[:, c, :],
                                          start=(c == 0), stop=(c == 1))
                mm.then_inc(full[j], 1)

            def xproj(u):
                p, d = after(u), (u[1] + 1) % 2
                pe.wait_ge(xc_done, cnt(p, 1, 1))
                for j, w, n in ((0, w_dt[d], R), (1, w_bc[d], 96)):
                    fill(j, u, "x")
                    for m in range(EC):
                        mm = nc.tensor.matmul(misc[j][0:n, 0:L], w[:, m, :], xc[d][:, m, :],
                                              start=(m == 0), stop=(m == EC - 1))
                    mm.then_inc(full[j], 1)

            def dtproj(u, m):
                p, d = after(u), (u[1] + 1) % 2
                if m == 0:
                    pe.wait_ge(r_done, cnt(p, 1, 1))
                j = m % 2
                fill(j, u, ("dt0", "dt1")[m // 2])
                nc.tensor.matmul(misc[j][:, 0:L], w_r[d][:, m * 128:(m + 1) * 128], r_sb[:, :],
                                 start=True, stop=True).then_inc(full[j], 1)

            def spread(u, n):
                d = u[1] % 2
                if n == 0:
                    pe.wait_ge(bc_v, cnt(u, 4, 4))
                if later(due := cnt(u, NS, n)):
                    pe.wait_ge(bc_copied, due)
                nc.tensor.matmul(bc_ps[:, 0, 0:L], sel[:, n, :], bcs[d][:, :], start=True, stop=True)
                nc.tensor.matmul(bc_ps[:, 1, 0:L], sel[:, NS + n, :], bcs[d][:, :], start=True, stop=True).then_inc(bc_mm, 1)

            def add_state(u, n):
                if n == 0:
                    if later(due := cnt(u, 1)):
                        pe.wait_ge(y_read, due)
                pe.wait_ge(p_done, cnt(u, NS, n + 1))
                for m in range(EC):
                    mm = nc.tensor.matmul(y_ps[:, m, 0:L], ident[:, :], pr[n % NP][:, m, 0:L],
                                          start=(n == 0), stop=(n == NS - 1))
                mm.then_inc(sum_done, 1)

            def outproj(u):
                d = (u[1] + 1) % 2
                pe.wait_ge(y2_done, cnt(u, 1))
                for g in range(2):
                    fill(g, u, "out")
                    for j in ((0, 1) if g == 0 else (2,)):
                        t0, n = TT[j]
                        for m in range(EC):
                            mm = nc.tensor.matmul(misc[g][0:n, (j % 2) * D:(j % 2) * D + D], y2[:, m, t0:t0 + n],
                                                  w_out[d][:, m, :], start=(m == 0), stop=(m == EC - 1))
                    mm.then_inc(full[g], 1)

            def prepare(u, step):
                if step in T_IN:
                    m = 2 * T_IN.index(step)
                    inproj(u, m)
                    inproj(u, m + 1)
                if u[1] % 2 == 0 and step == T_TOK:
                    tokens(u, batch(u, 1, 1))
                if step == T_X:
                    xproj(u)
                if step in T_DT:
                    m = 2 * T_DT.index(step)
                    dtproj(u, m)
                    dtproj(u, m + 1)
                if u[1] % 2 == 0 and step == T_TOKT:
                    tokens_t(u, batch(u, 1, 1))

            def unit(u, before=True, own=True, nxt=True):
                for step in range(NS if own else T_F2 + 1):
                    if own and step + 2 < NS:
                        spread(u, step + 2)
                    elif nxt:
                        spread(after(u), step + 2 - NS)
                    if step >= 2 and own:
                        add_state(u, step - 2)
                    elif step < 2 and before:
                        add_state(after(u, -1), step - 2 + NS)
                    if before and step == T_F2:
                        outproj(u)
                    if nxt:
                        prepare(u, step)

            pe.wait_ge(setup_done, 1)
            tokens(PROLOGUE, 0)
            tokens_t(PROLOGUE, 0)
            for step in range(NS):
                prepare(PROLOGUE, step)
            spread((0, 0), 0)
            spread((0, 0), 1)
            unit((0, 0), before=False)
            with pe.Fori(0, B - 1) as i:
                for u in units(i):
                    unit(u)
            unit((0, 2 * B - 1), nxt=False)
            unit((0, 2 * B), own=False, nxt=False)

        @block.scalar
        def _(act):
            def got(j, u, what):
                act.wait_ge(full[j], uses(u, what) + 1)

            def tokens_t(u, q):
                for c in range(2):
                    got(c, u, "tokT")
                    nc.scalar.activation(u_t[:, c, :], misc[c][:, 0:L], ACT.Copy).then_inc(uT_done, 1)
                    act.wait_ge(uT_done, q * 2 + (c + 1))
                    act.sem_inc(free[c], 1)

            def evacuate(u, m):
                p, d = after(u), (u[1] + 1) % 2
                j = m % 2
                got(j, u, ("x0", "x1", "z0", "z1")[m // 2])
                if m == 0:
                    if later(due := cnt(p, 1, -1)):
                        act.wait_ge(y2_done, due)
                    if later(due := cnt(p, 3 * EC)):
                        act.wait_ge(conv, due)
                if m < EC:
                    nc.scalar.activation(xraw[:, m, TAPS - 1:TAPS - 1 + L], misc[j][:, 0:L], ACT.Copy).then_inc(raw_done, 1)
                    nc.scalar.activation(xc[d][:, m, :], misc[j][:, 0:L], ACT.Identity, scale=vec[d][:, m, TAPS - 1:TAPS],
                                         bias=vec[d][:, m, TAPS:TAPS + 1]).then_inc(free[j], 1)
                else:
                    nc.scalar.activation(sz[d][:, m - EC, :], misc[j][:, 0:L], ACT.Copy).then_inc(free[j], 1)

            def silu_x(u):
                p, d = after(u), (u[1] + 1) % 2
                act.wait_ge(conv, cnt(p, 3 * EC, 3 * EC))
                nc.scalar.activation(xc[d][:, :, :], xc[d][:, :, :], ACT.Silu).then_inc(xc_done, 1)
                for j in range(2):
                    act.wait_ge(free[j], uses(u, "z1") + 1)
                nc.scalar.activation(sz[d][:, :, :], sz[d][:, :, :], ACT.Silu).then_inc(sz_done, 1)
                act.preload_act_table_set(EXP_LN)

            def split_bc(u):
                p, d = after(u), (u[1] + 1) % 2
                got(0, u, "x")
                nc.scalar.activation(r_sb[:, :], misc[0][0:R, 0:L], ACT.Copy).then_inc(r_done, 1)
                act.wait_ge(r_done, cnt(p, 1, 1))
                act.sem_inc(free[0], 1)
                got(1, u, "x")
                nc.scalar.activation(bcs[d][:, :], misc[1][0:96, 0:L], ACT.Copy).then_inc(bc_hi, 1)

            def softplus_in(u, m):
                p, d = after(u), (u[1] + 1) % 2
                j = m % 2
                got(j, u, ("dt0", "dt1")[m // 2])
                b = vec[d][:, m, TAPS + 1:TAPS + 2]
                nc.scalar.activation(dt_[d][:, m, :], misc[j][:, 0:L], ACT.Relu, bias=b)
                nc.scalar.activation(xraw[:, m, TAPS - 1:TAPS - 1 + L], misc[j][:, 0:L], ACT.Abs, bias=b).then_inc(free[j], 1)

            def softplus_exp(u):
                p = after(u)
                v = xraw[:, :, TAPS - 1:TAPS - 1 + L]
                act.wait_ge(free[0], uses(u, "dt1") + 1)
                act.wait_ge(free[1], uses(u, "dt1") + 1)
                nc.scalar.activation(v, v, ACT.Exp, scale=-1.0).then_inc(sp_a, 1)

            def softplus_ln(u):
                p, d = after(u), (u[1] + 1) % 2
                act.wait_ge(sp_v, cnt(p, 6, 1))
                nc.scalar.activation(dtx[d][:, :, :], dtx[d][:, :, :], ACT.Ln).then_inc(sp_a, 1)

            def copy_bc(u, n):
                act.wait_ge(bc_mm, cnt(u, NS, n + 1))
                if later(due := cnt(u, NS, n + 1 - NB)):
                    act.wait_ge(p_done, due)
                dv = sum(1 for x in range(n + 1 - NB + NS) if x % NS not in POOL_B) - NDVE
                if later(due := cnt(u, NDVE, dv)):
                    act.wait_ge(dbx_v, due)
                nc.scalar.activation(bc[n % NB][:, :, 0:L], bc_ps[:, :, 0:L], ACT.Copy).then_inc(bc_copied, 1)

            def decay(u, n):
                d = u[1] % 2
                if n == 0:
                    act.wait_ge(dt_done, cnt(u, 1, 1))
                if later(due := cnt(u, NS, n + 1 - NA)):
                    act.wait_ge(h_done, due)
                for m in range(EC):
                    a = nc.scalar.activation(da[n % NA][:, m, 1:L], dt_[d][:, m, 1 - d:L - d], ACT.Exp,
                                             scale=neg_a[d][:, m, n:n + 1])
                a.then_inc(da_done, 1)

            def squares(u):
                act.wait_ge(s_done, cnt(u, 2))
                act.wait_ge(q_done, cnt(u, 1))
                for j, (t0, n) in enumerate(TT):
                    nc.scalar.activation(sq[0:n, j, :], s_tok[0:n, j, :], ACT.Square, accum_out=ss[0:n, j:j + 1]).then_inc(ss_done, 1)
                act.wait_ge(ss_done, cnt(u, 4, -1))
                nc.scalar.activation(ss[:, :], ss[:, :], ACT.Identity, scale=1.0 / D, bias=eps_c[:, 0:1]).then_inc(ss_done, 1)

            def prepare(u, step):
                if step - 1 in T_IN:
                    m = 2 * T_IN.index(step - 1)
                    evacuate(u, m)
                    evacuate(u, m + 1)
                if step == T_SILU:
                    silu_x(u)
                if step - 1 == T_X:
                    split_bc(u)
                if step - 1 in T_DT:
                    m = 2 * T_DT.index(step - 1)
                    softplus_in(u, m)
                    softplus_in(u, m + 1)
                    if m == 2:
                        softplus_exp(u)
                if step == T_LN:
                    softplus_ln(u)
                if u[1] % 2 == 0 and step - 1 == T_TOKT:
                    tokens_t(u, batch(u, 1, 1))

            def unit(u, before=True, own=True, nxt=True):
                for step in range(NS if own else T_SQ + 1):
                    if before and step == T_SQ:
                        squares(u)
                    if nxt:
                        prepare(u, step)
                    if own and step + 2 < NS:
                        copy_bc(u, step + 2)
                    elif nxt:
                        copy_bc(after(u), step + 2 - NS)
                    if own and step + 1 < NS:
                        decay(u, step + 1)
                    elif nxt:
                        decay(after(u), 0)

            act.preload_act_table_set(EXP_LN)
            act.wait_ge(loads, N_LOADS)
            act.wait_ge(setup_v, 1)
            nc.scalar.activation(log_t[:, :], eps_c[:, 1:2], ACT.Ln).then_inc(setup_a, 1)
            for d in range(2):
                nc.scalar.activation(neg_a[d][:, :, :], vec[d][:, :, TAPS + 3:NV], ACT.Exp).then_inc(setup_a, 1)
            tokens_t(PROLOGUE, 0)
            for step in range(NS):
                prepare(PROLOGUE, step)
            copy_bc((0, 0), 0)
            copy_bc((0, 0), 1)
            decay((0, 0), 0)
            unit((0, 0), before=False)
            with act.Fori(0, B - 1) as i:
                for u in units(i):
                    unit(u)
            unit((0, 2 * B - 1), nxt=False)
            unit((0, 2 * B), own=False, nxt=False)

        @block.vector
        def _(dve):
            def got(j, u, what):
                dve.wait_ge(full[j], uses(u, what) + 1)

            def rows2(x):
                return x.rearrange("p (a n) -> p a n", a=2)

            def tokens(u, q):
                got(0, u, "tok")
                if later(due := q * 2):
                    dve.wait_ge(moved, due)
                nc.vector.scalar_tensor_tensor(h_new[:, 0:2, :], rows2(misc[0][:, :]), 0.0, tok_scale[:, None, :].to_broadcast([128, 2, D]),
                                               ALU.max, ALU.mult).then_inc(free[0], 1)
                got(1, u, "tok")
                n = TT[2][1]
                nc.vector.scalar_tensor_tensor(h_new[0:n, 2, :], misc[1][0:n, 0:D], 0.0, tok_scale[0:n, :],
                                               ALU.max, ALU.mult).then_inc(free[1], 1)
                dve.wait_ge(free[0], uses(u, "tok") + 1)
                nc.vector.tensor_tensor(h_new[:, 0:2, :], h_new[:, 0:2, :], tok_shift[:, None, :].to_broadcast([128, 2, D]),
                                        ALU.add).then_inc(tok_v, 1)
                dve.wait_ge(free[1], uses(u, "tok") + 1)
                nc.vector.tensor_tensor(h_new[0:n, 2, :], h_new[0:n, 2, :], tok_shift[0:n, :], ALU.add).then_inc(tok_v, 1)
                for j, (t0, n) in enumerate(TT):
                    dve.wait_ge(tok_v, q * 10 + (1 if j < 2 else 2))
                    nc.vector.bn_stats(bn[0:n, j, :], h_new[0:n, j, :]).then_inc(tok_v, 1)
                dve.wait_ge(tok_v, q * 10 + 5)
                dve.sem_inc(stats_go, 1)
                for j, (t0, n) in enumerate(TT):
                    nc.vector.bn_aggr(mv[0:n, j, :], bn[0:n, j, :]).then_inc(tok_v, 1)
                dve.wait_ge(tok_v, q * 10 + 8)
                nc.vector.tensor_scalar(norm_x[:, 0, :], mv[:, :, 1], 1.0, EPS, ALU.mult, ALU.add).then_inc(tok_v, 1)
                nc.vector.tensor_scalar(norm_x[:, 1, :], mv[:, :, 1], 1.0 + EPS, EPS * EPS, ALU.mult, ALU.add).then_inc(tok_v, 1)

            def normalise(u, q):
                dve.wait_ge(tok_q, q + 1)
                for j, (t0, n) in enumerate(TT):
                    nc.vector.tensor_scalar(u_tok[0:n, j, :], h_new[0:n, j, :], mv[0:n, j, 0:1], scales[0:n, 1, j:j + 1],
                                            ALU.subtract, ALU.mult).then_inc(u_done, 1)
                for j, (t0, n) in enumerate(TT):
                    a = nc.vector.tensor_scalar(r_new[0:n, j, :], h_new[0:n, j, :], mv[0:n, j, 0:1], scales[0:n, 0, j:j + 1],
                                                ALU.subtract, ALU.mult)
                a.then_inc(moved, 1)

            def take_tokens(u):
                q = batch(u, 1)
                dve.wait_ge(moved, q * 2 + 1)
                nc.vector.tensor_copy(h_cur[:, 0:2, :], h_new[:, 0:2, :])
                nc.vector.tensor_copy(r_cur[:, 0:2, :], r_new[:, 0:2, :])
                n = TT[2][1]
                nc.vector.tensor_copy(h_cur[0:n, 2, :], h_new[0:n, 2, :])
                nc.vector.tensor_copy(r_cur[0:n, 2, :], r_new[0:n, 2, :]).then_inc(moved, 1)

            def convolve(u, k):
                p, d = after(u), (u[1] + 1) % 2
                for m in range(EC):
                    if k == 0:
                        dve.wait_ge(free[m % 2], uses(u, ("x0", "x1")[m // 2]) + 1)
                        if m == 0:
                            dve.wait_ge(raw_done, cnt(p, EC, EC))
                    else:
                        dve.wait_ge(conv, cnt(p, 3 * EC, (k - 1) * EC + m + 1))
                    t0 = k if d == 0 else 2 * (TAPS - 1) - k
                    nc.vector.scalar_tensor_tensor(xc[d][:, m, :], xraw[:, m, t0:t0 + L], vec[d][:, m, k:k + 1], xc[d][:, m, :],
                                                   ALU.mult, ALU.add).then_inc(conv, 1)

            def split_bc(u):
                p, d = after(u), (u[1] + 1) % 2
                dve.wait_ge(bc_hi, cnt(p, 1, 1))
                nc.vector.tensor_tensor(mid[64:96, :], misc[1][64:96, 0:L], bcs[d][64:96, :], ALU.subtract).then_inc(bc_v, 1)
                nc.vector.tensor_tensor(rest[64:96, :], misc[1][64:96, 0:L], bcs[d][64:96, :], ALU.subtract).then_inc(bc_v, 1)
                nc.vector.tensor_tensor(bcs[d][32:64, :], misc[1][32:64, 0:L], bcs[d][32:64, :], ALU.subtract).then_inc(free[1], 1)
                dve.wait_ge(bc_v, cnt(p, 4, 2))
                nc.vector.tensor_tensor(bcs[d][64:96, :], rest[64:96, :], mid[64:96, :], ALU.subtract).then_inc(bc_v, 1)
                dve.wait_ge(free[1], uses(u, "x") + 1)
                dve.sem_inc(bc_v, 1)

            def log1p_small(u):
                p, d = after(u), (u[1] + 1) % 2
                m = xraw[:, :, TAPS - 1:TAPS - 1 + L]
                dve.wait_ge(sp_a, cnt(p, 2, 1))
                if later(due := cnt(p, NPOOL, -NPOOL)):
                    dve.wait_ge(dbx_p, due)
                nc.vector.tensor_scalar(dtx[d][:, :, :], m, LOG_T, 1.0, ALU.max, ALU.add).then_inc(sp_v, 1)
                nc.vector.tensor_scalar(m, m, LOG_T, None, ALU.min).then_inc(sp_v, 1)
                dve.wait_ge(sp_v, cnt(p, 6, 2))
                nc.vector.tensor_scalar(y2[:, :, :], m, LOG_C[2], LOG_C[1], ALU.mult, ALU.add).then_inc(sp_v, 1)
                dve.wait_ge(sp_v, cnt(p, 6, 3))
                nc.vector.tensor_tensor(y2[:, :, :], y2[:, :, :], m, ALU.mult).then_inc(sp_v, 1)
                dve.wait_ge(sp_v, cnt(p, 6, 4))
                nc.vector.scalar_tensor_tensor(y2[:, :, :], y2[:, :, :], LOG_C[0], m, ALU.add, ALU.mult).then_inc(sp_v, 1)

            def add_dt(u):
                p, d = after(u), (u[1] + 1) % 2
                dve.wait_ge(sp_a, cnt(p, 2, 2))
                nc.vector.scalar_tensor_tensor(dt_[d][:, :, :], dtx[d][:, :, :], log_t[:, 0:1], dt_[d][:, :, :],
                                               ALU.subtract, ALU.add).then_inc(sp_v, 1)
                dve.wait_ge(sp_v, cnt(p, 6, 6))
                nc.vector.tensor_tensor(dt_[d][:, :, :], dt_[d][:, :, :], y2[:, :, :], ALU.add).then_inc(dt_done, 1)

            def form_dtx(u):
                p, d = after(u), (u[1] + 1) % 2
                dve.wait_ge(dt_done, cnt(p, 1, 1))
                if later(due := cnt(p, NPOOL, -NPOOL)):
                    dve.wait_ge(dbx_p, due)
                nc.vector.tensor_tensor(dtx[d][:, :, :], dt_[d][:, :, :], xc[d][:, :, :], ALU.mult).then_inc(dtx_done, 1)

            def drive(u, n):
                if n in POOL_B:
                    return
                d = u[1] % 2
                if n == 0:
                    dve.wait_ge(dtx_done, cnt(u, 1, 1))
                dve.wait_ge(bc_copied, cnt(u, NS, n + 1))
                if later(due := cnt(u, NS, n + 1 - NX)):
                    dve.wait_ge(h_done, due)
                nc.vector.tensor_tensor(dbx[n % NX][:, :, d:d + L], dtx[d][:, :, :],
                                        bc[n % NB][:, 0, None, 0:L].to_broadcast([128, EC, L]), ALU.mult).then_inc(dbx_v, 1)

            def scan(u, n):
                d = u[1] % 2
                if n in POOL_B:
                    dve.wait_ge(dbx_p, cnt(u, NPOOL, sum(1 for x in POOL_B if x <= n)))
                else:
                    dve.wait_ge(dbx_v, cnt(u, NDVE, sum(1 for x in range(n + 1) if x not in POOL_B)))
                dve.wait_ge(da_done, cnt(u, NS, n + 1))
                if later(due := cnt(u, NS, n + 1 - NH)):
                    dve.wait_ge(p_done, due)
                flat = lambda x: x[:, :, :].rearrange("p m l -> p (m l)")
                a, b, o = flat(da[n % NA]), flat(dbx[n % NX]), flat(hs[n % NH])
                if d:
                    a, b, o = a[:, ::-1], b[:, ::-1], o[:, ::-1]
                nc.vector.tensor_tensor_scan(o, a, b, 0.0, ALU.mult, ALU.add).then_inc(h_done, 1)

            def gate(u):
                d = (u[1] + 1) % 2
                dve.wait_ge(sum_done, cnt(u, NS))
                dve.wait_ge(sz_done, cnt(u, 1))
                for m in range(EC):
                    a = nc.vector.scalar_tensor_tensor(y2[:, m, :], xc[d][:, m, :], vec[d][:, m, TAPS + 2:TAPS + 3],
                                                       y_ps[:, m, 0:L], ALU.mult, ALU.add)
                a.then_inc(y_read, 1)
                dve.wait_ge(y_read, cnt(u, 1))
                nc.vector.tensor_tensor(y2[:, :, :], y2[:, :, :], sz[d][:, :, :], ALU.mult).then_inc(y2_done, 1)

            def residual(u):
                got(0, u, "out")
                nc.vector.tensor_tensor(s_tok[:, 0:2, :], rows2(misc[0][:, :]), r_cur[:, 0:2, :], ALU.add).then_inc(s_done, 1)
                got(1, u, "out")
                n = TT[2][1]
                nc.vector.tensor_tensor(s_tok[0:n, 2, :], misc[1][0:n, 0:D], r_cur[0:n, 2, :], ALU.add).then_inc(s_done, 1)
                dve.wait_ge(s_done, cnt(u, 2))
                dve.sem_inc(free[0], 1)
                dve.sem_inc(free[1], 1)

            def accumulate(u):
                d = (u[1] + 1) % 2
                dve.wait_ge(q_done, cnt(u, 1, 1))
                for j, (t0, n) in enumerate(TT):
                    nc.vector.scalar_tensor_tensor(s_tok[0:n, j, :], s_tok[0:n, j, :], rms[0:n, j:j + 1], tok_rows[0:n, 4, :],
                                                   ALU.mult, ALU.mult).then_inc(acc_v, 1)
                if d == 0:
                    dve.wait_ge(h2_sent, batch(u, 48, 1))
                other = h_cur if d == 0 else acc
                n = TT[2][1]
                dve.wait_ge(acc_v, cnt(u, 5, 1 - 5 + 3))
                nc.vector.tensor_tensor(acc[:, 0:2, :], s_tok[:, 0:2, :], other[:, 0:2, :], ALU.add).then_inc(acc_v, 1)
                nc.vector.tensor_tensor(acc[0:n, 2, :], s_tok[0:n, 2, :], other[0:n, 2, :], ALU.add).then_inc(acc_v, 1)

            def prepare(u, step):
                if step in T_CONV:
                    convolve(u, T_CONV.index(step))
                if u[1] % 2 == 0 and step == T_TOKV:
                    tokens(u, batch(u, 1, 1))
                if step - 1 == T_X:
                    split_bc(u)
                if u[1] % 2 == 0 and step == T_NORM:
                    normalise(u, batch(u, 1, 1))
                if step == T_SMALL:
                    log1p_small(u)
                if step == T_ADD:
                    add_dt(u)
                    form_dtx(u)

            def unit(u, before=True, own=True, nxt=True):
                for step in range(NS if own else T_F4 + 1):
                    if before and step == T_F1:
                        gate(u)
                    if own and step + 1 < NS:
                        drive(u, step + 1)
                    elif nxt:
                        drive(after(u), 0)
                    if own:
                        scan(u, step)
                    if before and step == T_F3:
                        residual(u)
                    if before and step == T_F4:
                        accumulate(u)
                    if own and u[1] % 2 == 0 and step == T_TAKE:
                        take_tokens(u)
                    if nxt:
                        prepare(u, step)

            dve.sem_inc(acc_v, 1)
            for x in da:
                nc.vector.memset(x[:, :, :], 0.0)
            for x in dbx:
                nc.vector.memset(x[:, :, :], 0.0)
            nc.vector.memset(xraw[:, :, :], 0.0)
            nc.vector.memset(mv[:, :, :], 1.0)
            nc.vector.memset(ss[:, :], 1.0)
            nc.vector.memset(ones[:, :], 1.0)
            nc.vector.memset(eps_c[:, 0:1], EPS)
            nc.vector.memset(eps_c[:, 1:2], 1.0 + LOG_T).then_inc(setup_v, 1)
            dve.wait_ge(setup_v, 1)
            dve.wait_ge(setup_a, 3)
            nc.vector.tensor_scalar(tok_x, tok_rows[:, 3, :], EPS, None, ALU.add).then_inc(setup_v, 1)
            dve.wait_ge(setup_v, 2)
            dve.wait_ge(setup_p, 2)
            nc.vector.tensor_tensor(tok_scale[:, :], tok_scale[:, :], tok_rows[:, 0, :], ALU.mult).then_inc(setup_v, 1)
            dve.wait_ge(setup_v, 3)
            nc.vector.tensor_tensor(tok_rows[:, 2, :], tok_rows[:, 2, :], tok_scale[:, :], ALU.mult).then_inc(setup_v, 1)
            dve.wait_ge(setup_v, 4)
            nc.vector.tensor_tensor(tok_shift[:, :], tok_rows[:, 1, :], tok_rows[:, 2, :], ALU.subtract).then_inc(setup_v, 1)
            for d in range(2):
                nc.vector.tensor_scalar(neg_a[d][:, :, :], neg_a[d][:, :, :], -1.0, None, ALU.mult).then_inc(setup_v, 1)
                for c in range(2):
                    nc.vector.tensor_scalar(w_in[d][:, c, :], w_in[d][:, c, :], norm[d][:, c:c + 1], None, ALU.mult).then_inc(setup_v, 1)
            dve.wait_ge(setup_v, 11)
            dve.sem_inc(setup_done, 1)
            tokens(PROLOGUE, 0)
            normalise(PROLOGUE, 0)
            for step in range(NS):
                prepare(PROLOGUE, step)
            drive((0, 0), 0)
            unit((0, 0), before=False)
            with dve.Fori(0, B - 1) as i:
                for u in units(i):
                    unit(u)
            unit((0, 2 * B - 1), nxt=False)
            unit((0, 2 * B), own=False, nxt=False)

        @block.gpsimd
        def _(pool):
            def drive(u, n):
                if n not in POOL_B:
                    return
                d = u[1] % 2
                if n == POOL_B[0]:
                    pool.wait_ge(dtx_done, cnt(u, 1, 1))
                pool.wait_ge(bc_copied, cnt(u, NS, n + 1))
                pool.wait_ge(h_done, cnt(u, NS, n + 1 - NX))
                nc.gpsimd.tensor_tensor(dbx[n % NX][:, :, d:d + L], dtx[d][:, :, :],
                                        bc[n % NB][:, 0, None, 0:L].to_broadcast([128, EC, L]), ALU.mult).then_inc(dbx_p, 1)

            def weigh(u, n):
                d = u[1] % 2
                pool.wait_ge(h_done, cnt(u, NS, n + 1))
                if later(due := cnt(u, NS, n + 1 - NP)):
                    pool.wait_ge(sum_done, due)
                nc.gpsimd.tensor_tensor(pr[n % NP][:, :, 0:L], hs[n % NH][:, :, d:d + L],
                                        bc[n % NB][:, 1, None, 0:L].to_broadcast([128, EC, L]), ALU.mult).then_inc(p_done, 1)

            def token_power(q):
                pool.wait_ge(tok_v, q * 10 + 10)
                if later(due := q * 2):
                    pool.wait_ge(moved, due)
                nc.gpsimd.tensor_tensor(scales[:, :, :].rearrange("p a b -> p (a b)"), norm_x[:, :, :].rearrange("p a b -> p (a b)"),
                                        half[:, 0:6], ALU.pow).then_inc(tok_q, 1)

            def unit_power(u):
                pool.wait_ge(ss_done, cnt(u, 4))
                pool.wait_ge(acc_v, cnt(u, 5, 1 - 5))
                nc.gpsimd.tensor_tensor(rms[:, :], ss[:, :], half[:, 0:3], ALU.pow).then_inc(q_done, 1)

            def unit(u, before=True, own=True, nxt=True):
                for step in range(NS if own else T_SQ + 1):
                    if own and step + 1 < NS:
                        drive(u, step + 1)
                    elif nxt:
                        drive(after(u), 0)
                    if step >= 1 and own:
                        weigh(u, step - 1)
                    elif step == 0 and before:
                        weigh(after(u, -1), NS - 1)
                    if before and step == T_SQ:
                        unit_power(u)
                    if nxt and u[1] % 2 == 0 and step == T_TOKQ:
                        token_power(batch(u, 1, 1))

            pool.sem_inc(q_done, 1)
            nc.gpsimd.memset(half[:, :], -0.5).then_inc(setup_p, 1)
            pool.wait_ge(setup_p, 1)
            pool.wait_ge(setup_v, 2)
            nc.gpsimd.tensor_tensor(tok_scale[:, :], tok_x, half[:, 0:1].to_broadcast([128, D]), ALU.pow).then_inc(setup_p, 1)
            token_power(0)
            unit((0, 0), before=False)
            with pool.Fori(0, B - 1) as i:
                for u in units(i):
                    unit(u)
            unit((0, 2 * B - 1), nxt=False)
            unit((0, 2 * B), own=False, nxt=False)


T_F1, T_F2, T_F3, T_SQ, T_F4, T_TAKE = 2, 3, 4, 5, 6, 7
T_IN = [0, 1, 4, 5]
T_CONV = [2, 3, 5]
T_SILU = 7
T_X = 7
T_DT = [8, 9]
T_SMALL = 11
T_LN = 12
T_ADD = 13
T_TOK, T_TOKV, T_TOKQ, T_NORM, T_TOKT = 6, 8, 9, 10, 11


def experts(nc, t, h2_dram, x_dram, y_dram, out):
    ctx = ExitStack()
    with ctx:
        def sb(name, shape, dt=F32):
            return ctx.enter_context(nc.sbuf_tensor(name, shape, dt))

        def pb(name, shape):
            return ctx.enter_context(nc.psum_tensor(name, shape, F32))

        def sem(name):
            return ctx.enter_context(nc.semaphore(name))

        def later(value):
            return not isinstance(value, int) or value > 0

        flip_id = sb("flip_id", [128, 128])
        before = sb("before", [128, 128], BF16)
        all_ones = sb("all_ones", [128, 128], BF16)
        one1 = sb("one1", [1, 1])
        w_sel = sb("w_sel", [128, 2, X])
        iota_x = sb("iota_x", [128, X])
        iota_p = sb("iota_p", [X, PAGES])
        index_x = sb("index_x", [X, 128])
        ones_x = sb("ones_x", [128, X])

        h_all = sb("h_all", [128, NT, D])
        stats = sb("stats", [128, GM, 6])
        mv = sb("mv_x", [128, GM, 2])
        mean = sb("mean", [128, NT])
        var_x = sb("var_x", [128, NT])
        rstd = sb("rstd", [128, NT])
        shift = sb("shift", [128, NT])
        minus_half = sb("minus_half", [128, NT])
        vals = sb("vals", [128, NT, TOPK])
        gates = sb("gates", [128, NT, TOPK])
        pos_all = sb("pos_all", [128, NT, TOPK])

        hn_all = sb("hn_all", [128, GR, D])
        hn = [hn_all[:, j, :] for j in range(GR)]
        hn_t = [sb(f"hn_t{j}", [128, 2, 128]) for j in range(2)]
        lg = sb("lg", [128, X])
        top = sb("top", [128, 8])
        top_i = sb("top_i", [128, 8], U32)
        top_f = sb("top_f", [128, TOPK])
        oh = [sb(f"oh{j}", [128, TOPK, X], BF16) for j in range(2)]
        at = sb("at", [128, TOPK, X])
        pos_f = sb("pos_f", [128, TOPK])
        pos = [sb(f"pos{j}", [128, TOPK], I32) for j in range(GR)]
        lack = sb("lack", [128, X])
        end128 = sb("end128", [128, X])
        given = [sb(f"given{j}", [128, X]) for j in range(2)]
        need = sb("need", [128, X])
        flag = sb("flag", [128, X])
        jump = sb("jump", [128, X])
        step_ = sb("step_", [128, X])
        rel = sb("rel", [128, X])
        rel_jump = sb("rel_jump", [128, X])
        slot = sb("slot", [128, X])
        fresh = [sb(f"fresh{j}", [1, X]) for j in range(2)]
        owner = sb("owner", [X, PAGES])
        owner_i = sb("owner_i", [1, PAGES], I32)

        w_all = sb("w_all", [128, X, 2 * HX + D])
        xs = [hn_all[:, S2 * j:S2 * j + S2, :] for j in range(2)]
        vals_x = [hn_all[:, 2 * S2 + j, :] for j in range(2)]
        xs_t = hn_t
        hid = [at[:, 2 * j:2 * j + 2, :].rearrange("p a b -> p (a b)") for j in range(2)]
        keys = [sb(f"keys{j}", [128, 2 * HX]) for j in range(2)]
        ys = [sb(f"ys{j}", [128, S2, D]) for j in range(2)]

        part = lambda x, n: w_all[:, x:x + n, :].rearrange("p a (b d) -> p (a b) d", b=2)
        rows = [part(2 * j, 2) for j in range(G)]
        res = [part(2 * G + j // 2, 1)[:, j % 2, :] for j in range(G)]

        tp_ps = [pb(f"tp_ps{j}", [128, 512]) for j in range(2)]
        up_ps = [pb(f"up_ps{j}", [128, 512]) for j in range(2)]
        dn_ps = [pb(f"dn_ps{j}", [128, 512]) for j in range(2)]
        col_ps = pb("col_ps", [128, 512])

        consts = sem("consts")
        h_in = sem("h_in")
        set_v = sem("set_v")
        set_p = sem("set_p")
        stat_v = sem("stat_v")
        power_v = sem("power_v")
        power_p = sem("power_p")
        hn_done = sem("hn_done")
        tp_mm = sem("tp_mm")
        hn_t_done = sem("hn_t_done")
        lg_mm = sem("lg_mm")
        pick = sem("pick")
        cnt_mm = sem("cnt_mm")
        place = sem("place")
        fresh_done = sem("fresh_done")
        col_mm = sem("col_mm")
        owner_v = sem("owner_v")
        pos_done = sem("pos_done")
        pool_go = sem("pool_go")
        scattered = [sem(f"scattered{j}") for j in range(GR)]
        owner_mm = sem("owner_mm")
        owner_done = sem("owner_done")
        gates_done = sem("gates_done")
        xs_in = [sem(f"xs_in{j}") for j in range(2)]
        w_in = sem("w_in")
        keys_done = sem("keys_done")
        vals_done = sem("vals_done")
        xt_mm = sem("xt_mm")
        xt_done = sem("xt_done")
        hid_mm = sem("hid_mm")
        hid_done = sem("hid_done")
        y_mm = sem("y_mm")
        y_done = sem("y_done")
        y_sent = [sem(f"y_sent{j}") for j in range(2)]
        pages_done = sem("pages_done")
        posg_done = sem("posg_done")
        rows_in = [sem(f"rows_in{j}") for j in range(G)]
        sum_v = sem("sum_v")
        out_sent = [sem(f"out_sent{j}") for j in range(G)]

        block = ctx.enter_context(nc.Block())
        h_rows = h2_dram.rearrange("b t d -> (b t) d")
        out_rows = out.rearrange("b t d -> (b t) d")
        pages_x = x_dram.rearrange("(j p) d -> j p d", p=128)
        pages_y = y_dram.rearrange("(j p) d -> j p d", p=128)
        CH = 12
        chunks = [(a, min(a + CH, NT - 1)) for a in range(0, NT - 1, CH)]
        spans = chunks[:-1] + [(chunks[-1][0], NT)]
        XW = 8
        NV_PICK = 6
        NV_PLACE = 15

        def over_all(eng, step, total, per, ahead=0):
            for k in range(per):
                step(0, k)
            groups = max(0, (total - ahead - per) // per)
            if groups > 0:
                with eng.Fori(1, 1 + groups) as r:
                    for k in range(per):
                        step(r, k)
            for n in range(per * (1 + groups), total):
                step(n // per, n % per)

        def is_last(r, k, ahead, total, per):
            return isinstance(r, int) and r * per + k + ahead >= total

        def first(r, k):
            return isinstance(r, int) and r == 0 and k == 0

        def of_tile(x, i):
            if isinstance(i, int):
                return x[:, i, :]
            return x[:, bass.ds(i, 1), :].rearrange("p a d -> p (a d)")

        def col(x, i):
            return x[:, i:i + 1] if isinstance(i, int) else x[:, bass.ds(i, 1)]

        def cols(x, i, n):
            return x[:, i:i + n] if isinstance(i, int) else x[:, bass.ds(i, n)]

        def half_of(pages, j):
            if isinstance(j, int):
                return pages[j * S2:j * S2 + S2].rearrange("j p d -> p j d")
            return pages[bass.ds(j * S2, S2), :, :].rearrange("j p d -> p j d")

        def at_page(j):
            return owner_i[0:1, j:j + 1] if isinstance(j, int) else owner_i[0:1, bass.ds(j, 1)]

        def of_expert(x, start, n):
            return w_all[:, bass.ds(x, 1), start:start + n].rearrange("p a n -> p (a n)")

        @block.sync
        def _(sp):
            for dst, src in ((flip_id[:, :], t["ident"]), (before[:, :], t["before"]), (all_ones[:, :], t["all_ones"]),
                             (w_sel[:, :, :], t["sel_w"]), (iota_x[:, :], t["iota_x"]),
                             (iota_p[:, :], t["iota_p"]), (index_x[:, :], t["index_x"])):
                sp.dma_start(dst, src).then_inc(consts, 16)
            for c, (a, b) in enumerate(chunks):
                if later(due := 16 * c):
                    sp.wait_ge(h_in, due)
                src = h_rows[a * 128:b * 128, :].rearrange("(i p) d -> p i d", p=128)
                sp.dma_start(h_all[:, a:b, :], src).then_inc(h_in, 16)
            sp.wait_ge(h_in, 16 * len(chunks))
            sp.dma_start(h_all[0:LAST, NT - 1, :], h_rows[(NT - 1) * 128:N, :]).then_inc(h_in, 16)
            sp.wait_ge(h_in, 16 * (len(chunks) + 1))
            sp.dma_start(h_all[LAST:128, NT - 1, :], h_rows[0:128 - LAST, :]).then_inc(h_in, 16)
            for x in range(0, X, XW):
                sp.dma_start(w_all[:, x:x + XW, :], t["experts"][x:x + XW].rearrange("x p n -> p x n")).then_inc(w_in, 16)

            def load(r, k):
                if later(due := r * S + (k - 1) * S2):
                    sp.wait_ge(xt_mm, due)
                sp.dma_start(xs[k % 2][:, :, :], half_of(pages_x, r * 2 + k)).then_inc(xs_in[k % 2], 16)

            def half(r, k):
                if not is_last(r, k, 2, PAGES // S2, 2):
                    load(r, k + 2)
                sp.wait_ge(y_done, r * S + (k * S2 + S2))
                sp.dma_start(half_of(pages_y, r * 2 + k), ys[k][:, :, :]).then_inc(y_sent[k], 16)

            for s in range(GR):
                sp.wait_ge(scattered[s], 64 * len(range(s, NT, GR)))
            load(0, 0)
            load(0, 1)
            over_all(sp, half, PAGES // S2, 2, 2)
            for k in range(2):
                sp.wait_ge(y_sent[k], 16 * (PAGES // S))
            sp.sem_inc(pages_done, 1)

            def store(r, k):
                i = r * G + k
                sp.wait_ge(sum_v, i * 5 + 4)
                if isinstance(i, int):
                    n = LAST if i == NT - 1 else 128
                    dst, src = out_rows[i * 128:i * 128 + n, :], res[k][0:n, :]
                else:
                    dst, src = out_rows[bass.ds(i * 128, 128), :], res[k]
                sp.dma_start(dst, src).then_inc(out_sent[k], 16)

            over_all(sp, store, NT, G, 1)
            for s in range(G):
                sp.wait_ge(out_sent[s], 16 * len(range(s, NT, G)))

        @block.tensor
        def _(pe):
            pe.wait_ge(consts, 16 * 7)
            pe.wait_ge(set_v, 1)

            def logits(r, k):
                i, p = r * GR + k, k % 2
                pe.wait_ge(hn_done, i + 1)
                if later(due := i - 1):
                    pe.wait_ge(hn_t_done, due)
                for c in range(2):
                    mm = nc.tensor.transpose(tp_ps[p][:, c * 128:(c + 1) * 128], hn[k % GR][:, c * 128:(c + 1) * 128], flip_id[:, :])
                mm.then_inc(tp_mm, 1)
                pe.wait_ge(hn_t_done, i + 1)
                if later(due := (i - 2) * NV_PICK + 1):
                    pe.wait_ge(pick, due)
                for c in range(2):
                    mm = nc.tensor.matmul(up_ps[p][:, 0:X], hn_t[p][:, c, :], w_sel[:, c, :], start=(c == 0), stop=(c == 1))
                mm.then_inc(lg_mm, 1)

            def fresh_column(r, k):
                i, p = r * GR + k, k % 2
                pe.wait_ge(fresh_done, i + 1)
                pe.wait_ge(owner_v, i + 1)
                nc.tensor.matmul(col_ps[0:X, 0:1], fresh[p][0:1, :], one1[:, :], start=True, stop=True).then_inc(col_mm, 1)

            def tile(r, k):
                i, p = r * GR + k, k % 2
                if not is_last(r, k, 2, NT, GR):
                    logits(r, k + 2)
                pe.wait_ge(pick, i * NV_PICK + NV_PICK)
                if later(due := (i - 1) * NV_PLACE):
                    pe.wait_ge(place, due)
                for q in range(TOPK):
                    nc.tensor.matmul(dn_ps[p][:, X:2 * X], all_ones[:, :], oh[p][:, q, :], start=(q == 0), stop=(q == TOPK - 1))
                for q in range(TOPK):
                    mm = nc.tensor.matmul(dn_ps[p][:, 0:X], before[:, :], oh[p][:, q, :], start=(q == 0), stop=(q == TOPK - 1))
                mm.then_inc(cnt_mm, 1)
                if not first(r, k):
                    fresh_column(r, k - 1)

            logits(0, 0)
            logits(0, 1)
            over_all(pe, tile, NT, GR, 2)
            fresh_column(NT // GR, NT % GR - 1)
            pe.wait_ge(owner_v, 1 + NT)
            nc.tensor.matmul(col_ps[:, 0:PAGES], index_x[:, :], owner[:, :], start=True, stop=True).then_inc(owner_mm, 1)

            def flip(r, k):
                j, s, p = r * S + k, (k // S2) % 2, k % 2
                pe.wait_ge(xs_in[s], (r + k // S) * 16 + 16)
                if later(due := j - 1):
                    pe.wait_ge(xt_done, due)
                for c in range(2):
                    mm = nc.tensor.transpose(tp_ps[p][:, c * 128:(c + 1) * 128], xs[s][:, k % S2, c * 128:(c + 1) * 128], flip_id[:, :])
                mm.then_inc(xt_mm, 1)

            def up(r, k):
                j, p = r * S + k, k % 2
                pe.wait_ge(keys_done, j + 1)
                if later(due := j - 1):
                    pe.wait_ge(hid_done, due)
                pe.wait_ge(xt_done, j + 1)
                for c in range(2):
                    mm = nc.tensor.matmul(up_ps[p][:, 0:128], keys[p][:, c * HX:(c + 1) * HX], xs_t[p][:, c, :], start=(c == 0), stop=(c == 1))
                mm.then_inc(hid_mm, 1)

            def down(r, k):
                j, p = r * S + k, k % 2
                pe.wait_ge(vals_done, j + 1)
                if later(due := j - 1):
                    pe.wait_ge(y_done, due)
                pe.wait_ge(hid_done, j + 1)
                nc.tensor.matmul(dn_ps[p][:, 0:D], hid[p], vals_x[p], start=True, stop=True).then_inc(y_mm, 1)

            def page(r, k):
                if not is_last(r, k, 2, PAGES, S):
                    flip(r, k + 2)
                if not is_last(r, k, 1, PAGES, S):
                    up(r, k + 1)
                down(r, k)

            flip(0, 0)
            flip(0, 1)
            up(0, 0)
            over_all(pe, page, PAGES, S, 2)

        @block.scalar
        def _(act):
            def normalise(r, k):
                i = r * GR + k
                if later(due := (r + k // GR) * 64):
                    act.wait_ge(scattered[k % GR], due)
                nc.scalar.activation(hn[k % GR], of_tile(h_all, i), ACT.Identity, bias=col(shift, i), scale=col(rstd, i)).then_inc(hn_done, 1)

            def tile(r, k):
                i, p = r * GR + k, k % 2
                act.wait_ge(tp_mm, i + 1)
                if later(due := i - 1):
                    act.wait_ge(lg_mm, due)
                nc.scalar.copy(hn_t[p][:, :, :].rearrange("p a b -> p (a b)"), tp_ps[p][:, 0:D]).then_inc(hn_t_done, 1)
                if not is_last(r, k, 2, NT, GR):
                    normalise(r, k + 2)

            act.wait_ge(power_p, 2 * len(chunks))
            normalise(0, 0)
            normalise(0, 1)
            over_all(act, tile, NT, GR, 2)
            act.wait_ge(pick, NT * NV_PICK)
            nc.scalar.activation(gates[:, :, :], vals[:, :, :], ACT.Sigmoid).then_inc(gates_done, 1)

            def relu(r, k):
                j, p = r * S + k, k % 2
                if later(due := j - 1):
                    act.wait_ge(y_mm, due)
                act.wait_ge(hid_mm, j + 1)
                nc.scalar.activation(hid[p], up_ps[p][:, 0:128], ACT.Relu).then_inc(hid_done, 1)

            def page(r, k):
                j, p = r * S + k, k % 2
                if not is_last(r, k, 1, PAGES, S):
                    relu(r, k + 1)
                act.wait_ge(y_mm, j + 1)
                if later(due := r * 16):
                    act.wait_ge(y_sent[k // S2], due)
                nc.scalar.copy(ys[k // S2][:, k % S2, :], dn_ps[p][:, 0:D]).then_inc(y_done, 1)

            relu(0, 0)
            over_all(act, page, PAGES, S, 1)

        @block.vector
        def _(dve):
            V = nc.vector
            V.memset(one1[:, :], 1.0)
            V.memset(ones_x[:, :], 1.0)
            V.memset(lack[:, :], 0.0)
            V.memset(end128[:, :], 128.0)
            V.memset(given[1][:, :], 0.0)
            V.memset(owner[:, :], 0.0).then_inc(set_v, 1)
            dve.wait_ge(set_v, 1)
            dve.sem_inc(owner_v, 1)

            def measure(g, i, n):
                for q in range(n):
                    a = V.bn_stats(stats[:, q, :], of_tile(h_all, i + q))
                a.then_inc(stat_v, 1)
                dve.wait_ge(stat_v, g * 4 + 1)
                dve.sem_inc(stat_v, 1)
                for q in range(n):
                    a = V.bn_aggr(mv[:, q, :], stats[:, q, :])
                a.then_inc(stat_v, 1)
                dve.wait_ge(stat_v, g * 4 + 3)
                V.tensor_scalar(cols(mean, i, n), mv[:, 0:n, 0], -1.0, None, ALU.mult)
                V.tensor_scalar(cols(var_x, i, n), mv[:, 0:n, 1], EPS, None, ALU.add).then_inc(stat_v, 1)

            for c, (a, b) in enumerate(spans):
                dve.wait_ge(h_in, 16 * (c + 1 + (2 if b == NT else 0)))
                groups = (b - a) // GM
                if groups:
                    with dve.Fori(0, groups) as r:
                        measure(r + a // GM, r * GM + a, GM)
                if b - a > groups * GM:
                    measure(a // GM + groups, a + groups * GM, b - a - groups * GM)
                dve.wait_ge(stat_v, (b + GM - 1) // GM * 4)
                dve.sem_inc(power_v, 1)

            def choose(r, k):
                i, p = r * GR + k, k % 2
                c = i * NV_PICK
                dve.wait_ge(lg_mm, i + 1)
                V.tensor_scalar(lg[:, :], up_ps[p][:, 0:X], SATURATED, None, ALU.min).then_inc(pick, 1)
                dve.wait_ge(pick, c + 1)
                dve.sem_inc(pick, 1)
                V.max(top[:, :], lg[:, :]).then_inc(pick, 1)
                dve.wait_ge(pick, c + 3)
                V.tensor_copy(of_tile(vals, i), top[:, 0:TOPK])
                V.max_index(top_i[:, :], top[:, :], lg[:, :]).then_inc(pick, 1)
                dve.wait_ge(pick, c + 4)
                V.tensor_copy(top_f[:, :], top_i[:, 0:TOPK]).then_inc(pick, 1)
                dve.wait_ge(pick, c + 5)
                if later(due := i - 1):
                    dve.wait_ge(cnt_mm, due)
                V.tensor_tensor(oh[p][:, :, :], iota_x[:, None, :].to_broadcast([128, TOPK, X]),
                                top_f[:, :, None].to_broadcast([128, TOPK, X]), ALU.is_equal).then_inc(pick, 1)

            def find_slots(r, k):
                i, p = r * GR + k, k % 2
                c = i * NV_PLACE
                pre, tot = dn_ps[p][:, 0:X], dn_ps[p][:, X:2 * X]
                dve.wait_ge(cnt_mm, i + 1)
                if later(due := c):
                    dve.wait_ge(place, due)
                V.tensor_tensor(need[:, :], tot, lack[:, :], ALU.add).then_inc(place, 1)
                V.tensor_tensor(rel[:, :], pre, lack[:, :], ALU.add).then_inc(place, 1)
                dve.wait_ge(place, c + 1)
                V.tensor_scalar(flag[:, :], need[:, :], 0.0, None, ALU.is_gt).then_inc(place, 1)
                dve.wait_ge(place, c + 3)
                V.tensor_tensor_scan(given[p][:, :], ones_x[:, :], flag[:, :], given[1 - p][:, X - 1:X], ALU.mult, ALU.add).then_inc(place, 1)
                V.scalar_tensor_tensor(lack[:, :], flag[:, :], -128.0, need[:, :], ALU.mult, ALU.add).then_inc(place, 1)
                dve.wait_ge(place, c + 4)
                V.scalar_tensor_tensor(jump[:, :], given[p][:, :], 128.0, end128[:, :], ALU.mult, ALU.subtract).then_inc(place, 1)
                if later(due := i - 1):
                    dve.wait_ge(col_mm, due)
                V.tensor_tensor(fresh[p][:, :], given[p][0:1, :], flag[0:1, :], ALU.mult).then_inc(fresh_done, 1)
                dve.wait_ge(place, c + 6)
                V.scalar_tensor_tensor(rel_jump[:, :], rel[:, :], 0.0, jump[:, :], ALU.is_ge, ALU.mult).then_inc(place, 1)
                V.scalar_tensor_tensor(step_[:, :], jump[:, :], 128.0, flag[:, :], ALU.add, ALU.mult).then_inc(place, 1)
                V.scalar_tensor_tensor(slot[:, :], rel[:, :], -128.0, end128[:, :], ALU.add, ALU.add).then_inc(place, 1)
                dve.wait_ge(place, c + 9)
                V.tensor_tensor(slot[:, :], slot[:, :], rel_jump[:, :], ALU.add).then_inc(place, 1)
                V.tensor_tensor(end128[:, :], end128[:, :], step_[:, :], ALU.add).then_inc(place, 1)
                dve.wait_ge(place, c + 10)
                V.tensor_tensor(at[:, :, :], oh[p][:, :, :], slot[:, None, :].to_broadcast([128, TOPK, X]), ALU.mult).then_inc(place, 1)
                dve.wait_ge(place, c + 12)
                V.tensor_reduce(pos_f[:, :], at[:, :, :], axis=AX.X, op=ALU.add).then_inc(place, 1)
                dve.wait_ge(place, c + 13)
                if later(due := (r + k // GR) * 64):
                    dve.wait_ge(scattered[k % GR], due)
                V.tensor_copy(pos[k % GR][:, :], pos_f[:, :]).then_inc(pos_done, 1)
                V.tensor_copy(of_tile(pos_all, i), pos_f[:, :]).then_inc(place, 1)
                dve.sem_inc(place, 1)

            def note_owner(r, k):
                i = r * GR + k
                dve.wait_ge(col_mm, i + 1)
                dve.wait_ge(owner_v, i + 1)
                V.scalar_tensor_tensor(owner[:, :], iota_p[:, :], col_ps[0:X, 0:1], owner[:, :], ALU.is_equal, ALU.add).then_inc(owner_v, 1)

            def tile(r, k):
                if not is_last(r, k, 1, NT, GR):
                    choose(r, k + 1)
                find_slots(r, k)
                if not first(r, k):
                    note_owner(r, k - 1)

            dve.wait_ge(consts, 16 * 7)
            choose(0, 0)
            over_all(dve, tile, NT, GR, 1)
            note_owner(NT // GR, NT % GR - 1)
            dve.wait_ge(owner_mm, 1)
            V.tensor_copy(owner_i[:, :], col_ps[0:1, 0:PAGES]).then_inc(owner_done, 1)
            dve.wait_ge(owner_done, 1)
            dve.wait_ge(w_in, 16 * (X // XW))

            def values(r, k):
                j, p = r * S + k, k % 2
                x = dve.value_load(at_page(j), min_val=0, max_val=X - 1)
                if later(due := j - 1):
                    dve.wait_ge(y_mm, due)
                V.tensor_copy(vals_x[p], of_expert(x, 2 * HX, D)).then_inc(vals_done, 1)

            def page(r, k):
                j, p = r * S + k, k % 2
                if later(due := j - 1):
                    dve.wait_ge(hid_mm, due)
                dve.wait_ge(xt_mm, j + 1)
                V.tensor_copy(xs_t[p][:, :, :].rearrange("p a b -> p (a b)"), tp_ps[p][:, 0:D]).then_inc(xt_done, 1)
                values(r, k)

            over_all(dve, page, PAGES, S, 1)

            def take_slots(r, k):
                V.tensor_copy(pos[k % G][:, :], of_tile(pos_all, r * G + k)).then_inc(posg_done, 1)

            def combine(r, k):
                i = r * G + k
                dve.wait_ge(rows_in[k], r * 64 + 64)
                if later(due := r * 16):
                    dve.wait_ge(out_sent[k], due)
                for q in range(TOPK):
                    if q:
                        dve.wait_ge(sum_v, i * 5 + q)
                    other = res[k] if q else of_tile(h_all, i)
                    gate = col(gates[:, :, :].rearrange("p i q -> p (i q)"), i * TOPK + q)
                    V.scalar_tensor_tensor(res[k], rows[k][:, q, :], gate, other, ALU.mult, ALU.add).then_inc(sum_v, 1)
                dve.wait_ge(sum_v, i * 5 + 4)
                dve.sem_inc(sum_v, 1)
                if not is_last(r, k, G, NT, G):
                    take_slots(r, k + G)

            for k in range(G):
                take_slots(0, k)
            dve.wait_ge(gates_done, 1)
            over_all(dve, combine, NT, G, G)

        @block.gpsimd
        def _(pool):
            P = nc.gpsimd
            P.memset(minus_half[:, :], -0.5).then_inc(set_p, 1)
            pool.wait_ge(set_p, 1)
            for c, (a, b) in enumerate(spans):
                pool.wait_ge(power_v, c + 1)
                P.tensor_tensor(rstd[:, a:b], var_x[:, a:b], minus_half[:, a:b], ALU.pow).then_inc(power_p, 1)
                pool.wait_ge(power_p, 2 * c + 1)
                P.tensor_tensor(shift[:, a:b], mean[:, a:b], rstd[:, a:b], ALU.mult).then_inc(power_p, 1)

            def scatter(r, k):
                pool.wait_ge(pos_done, r * GR + (k + 1))
                pool.sem_inc(pool_go, 1)
                for q in range(TOPK):
                    P.indirect_dma_start(x_dram[:, :], bass.IndirectOffsetOnAxis(ap=pos[k][:, q:q + 1], axis=0),
                                         hn[k], None).then_inc(scattered[k], 16)

            over_all(pool, scatter, NT, GR, 1)

            def page_keys(r, k):
                j, p = r * S + k, k % 2
                x = pool.value_load(at_page(j), min_val=0, max_val=X - 1)
                if later(due := j - 1):
                    pool.wait_ge(hid_mm, due)
                pool.sem_inc(pool_go, 1)
                P.tensor_copy(keys[p][:, :], of_expert(x, 0, 2 * HX)).then_inc(keys_done, 1)

            pool.wait_ge(owner_done, 1)
            pool.wait_ge(w_in, 16 * (X // XW))
            over_all(pool, page_keys, PAGES, S, 1)

            def gather(r, k):
                pool.wait_ge(posg_done, r * G + (k + 1))
                pool.sem_inc(pool_go, 1)
                for q in range(TOPK):
                    P.indirect_dma_start(rows[k][:, q, :], None, y_dram[:, :],
                                         bass.IndirectOffsetOnAxis(ap=pos[k][:, q:q + 1], axis=0)).then_inc(rows_in[k], 16)

            pool.wait_ge(pages_done, 1)
            over_all(pool, gather, NT, G, 1)


def scan_arrays(ins):
    n = {k: np.asarray(v) for k, v in ins.items()}
    c = np.ascontiguousarray
    a = {"x": c(n["x"].transpose(0, 2, 1)), "tok_w": c(n["L0_tok_W"].T.reshape(CTX, 128, D).transpose(1, 0, 2)),
         "tok_b": n["L0_tok_b"], "tok_gamma": n["L0_tok_gamma"], "tok_beta": n["L0_tok_beta"],
         "tok_mean": n["L0_tok_running_mean"], "tok_var": n["L0_tok_running_var"], "normf": n["L0_attn_normf"],
         "ident": np.eye(128, dtype=np.float32)}
    s = np.zeros((96, 2 * NS, 128), mybir.dt.np(BF16))
    for j in range(2 * NS):
        for q in range(3):
            s[32 * q + j, j, :] = 1
    a["sel"] = s
    chunks = lambda w: c(w.reshape(-1, 128, *w.shape[1:]).swapaxes(0, 1))
    for d, pre in enumerate(("L0_attn_fwd_", "L0_attn_bwd_")):
        g = lambda k: n[pre + k]
        a[f"in{d}"] = chunks(g("inproj").T)
        a[f"xdt{d}"] = chunks(g("xproj")[:R].T)
        a[f"xbc{d}"] = chunks(np.concatenate([g("xproj")[R:].T] * 3, axis=1))
        a[f"dtw{d}"] = c(g("dtw").T)
        a[f"out{d}"] = chunks(g("outproj").T)
        a[f"vec{d}"] = chunks(np.concatenate([g("convw"), g("convb")[:, None], g("dtb")[:, None], g("Dp")[:, None], g("Alog")], axis=1))
        a[f"norm{d}"] = c(g("norm").reshape(2, 128).T)
    return a


def expert_arrays(ins):
    c = np.ascontiguousarray
    sel, keys, values = (np.asarray(ins["L0_ffn_" + k]) for k in ("expert_sel", "keys", "values"))
    k2 = keys.reshape(X, 2, 128, HX).transpose(0, 2, 1, 3).reshape(X, 128, 2 * HX)
    return {"before": np.triu(np.ones((128, 128)), 1).astype(mybir.dt.np(BF16)),
            "all_ones": np.ones((128, 128), mybir.dt.np(BF16)),
            "sel_w": c(sel.T.reshape(2, 128, X).transpose(1, 0, 2)),
            "iota_x": c(np.broadcast_to(np.arange(X, dtype=np.float32), (128, X))),
            "iota_p": c(np.broadcast_to(np.arange(1, PAGES + 1, dtype=np.float32), (X, PAGES))),
            "index_x": c(np.broadcast_to(np.arange(X, dtype=np.float32)[:, None], (X, 128))),
            "zeros": np.zeros((128, D), np.float32),
            "experts": c(np.concatenate([k2, values], axis=2))}


def build(nc, t, out):
    h2_dram = nc.dram_tensor("h2_dram", [B, L, D], F32).ap()
    x_dram = nc.dram_tensor("x_dram", [PAGES * 128, D], F32).ap()
    y_dram = nc.dram_tensor("y_dram", [PAGES * 128, D], F32).ap()
    tower(nc, t, h2_dram, x_dram)
    experts(nc, t, h2_dram, x_dram, y_dram, out)


def kernel(**inputs):
    import concourse.bacc as bacc
    from concourse.bass_utils import run_bass_kernel_spmd

    arrays = {**scan_arrays(inputs), **expert_arrays(inputs)}
    nc = bacc.Bacc("TRN2", target_bir_lowering=False, num_devices=1)
    t = {k: nc.dram_tensor("in_" + k, a.shape, mybir.dt.from_np(a.dtype), kind="ExternalInput").ap() for k, a in arrays.items()}
    out = nc.dram_tensor("out", [B, L, D], F32, kind="ExternalOutput").ap()
    build(nc, t, out)
    r = run_bass_kernel_spmd(nc, [{"in_" + k: a for k, a in arrays.items()}], core_ids=[0])
    return r.results[0]["out"]
```

```python
import numpy as np
import concourse.bass as bass
from concourse import mybir
from contextlib import ExitStack

F32 = mybir.dt.float32
BF16 = mybir.dt.bfloat16
I32 = mybir.dt.int32
U32 = mybir.dt.uint32
ALU = mybir.AluOpType
ACT = mybir.ActivationFunctionType
AX = mybir.AxisListType

B, TIN, DIN = 16, 375, 128
CTX = 5
L = TIN - CTX + 1
D = 256
E = 512
EC = E // 128
NS = 16
R = 64
TAPS = 4
LP = L + 1
TT = [(0, 128), (128, 128), (256, L - 256)]
EPS = 1e-5
N_SKIP = (11, 13)
AHEAD_BC, AHEAD_DECAY = 2, 1
POOL_B = (6, 8, 10, 12, 14)
LOG_T = 2.0 ** -5
LOG_C = (0.9999997716733988, -0.4998678486375896, 0.3219470998103213)
SQUARE = (LOG_C[2] ** 0.5, LOG_C[1] / (2 * LOG_C[2] ** 0.5), LOG_C[0] - LOG_C[1] ** 2 / (4 * LOG_C[2]))
T_F1, T_F2, T_F3, T_SQ, T_F4, T_TAKE = 2, [4, 4], 5, 6, 7, 8
T_IN, T_EVAC, T_CONV, T_SILU, T_X = [1, 3, 5, 7], [3, 4, 7, 8], [4, 5, 6], 8, [8, 8]
T_DT, T_LN, T_LIMIT, T_SQUARE, T_SMALL, T_ADD, T_DTX = [9, 10], 11, 11, 12, 12, 12, 13
T_TOK, T_TOKV, T_TOKQ, T_NORM, T_TOKT = [9, 9], 10, 11, 11, 12
EXP_LN = "natural_log_exp_and_others"

N = B * L
NT = (N + 127) // 128
LAST = N - 128 * (NT - 1)
X = 64
HX = 128
TOPK = 4
SATURATED = 16.6355
GM = 4
GR = 8
S = 6
S2 = S // 2
DEEP = 3
ACT_PAGES = (1, 2, 4, 5)


def pages_after(tiles):
    return (tiles * 128 * TOPK + 127 * X) // 128


TS = 3
TP = TS * TOPK
LAG = (pages_after(1) + TP - 1) // TP + 1
TRIPS = (pages_after(NT) + TP - 1) // TP
PAGES = TRIPS * TP
LOADS = TP // S2
XS0 = 6 * TS + S + 2 * DEEP


def tower(nc, t, h2_dram, x_dram):
    ctx = ExitStack()
    with ctx:
        def sb(name, shape, dt=F32):
            return ctx.enter_context(nc.sbuf_tensor(name, shape, dt))

        def pb(name, shape):
            return ctx.enter_context(nc.psum_tensor(name, shape, F32))

        def sem(name):
            return ctx.enter_context(nc.semaphore(name))

        tokw = sb("tokw", [128, CTX, D])
        tok_rows = sb("tok_rows", [128, 5, D])
        tok_scale, tok_shift, tok_power = tok_rows[:, 0, :], tok_rows[:, 1, :], tok_rows[:, 3, :]
        tok_b = sb("tok_b", [1, D])
        ones = sb("ones", [1, 128])
        ident = sb("ident", [128, 128])
        sel = sb("sel", [96, 2 * NS, 128], BF16)
        w_in = [sb(f"w_in{d}", [128, 2, 2 * E]) for d in range(2)]
        w_dt = [sb(f"w_dt{d}", [128, EC, R]) for d in range(2)]
        w_bc = [sb(f"w_bc{d}", [128, EC, 96]) for d in range(2)]
        w_r = [sb(f"w_r{d}", [R, E]) for d in range(2)]
        w_out = [sb(f"w_out{d}", [128, EC, D]) for d in range(2)]
        NV = TAPS + 3 + NS
        vec = [sb(f"vec{d}", [128, EC, NV]) for d in range(2)]
        norm = [sb(f"norm{d}", [128, 2]) for d in range(2)]
        neg_a = [sb(f"neg_a{d}", [128, EC, NS]) for d in range(2)]
        skip = [sb(f"skip{d}", [128, EC, 128]) for d in range(2)]
        eps_c = sb("eps_c", [128, 4])
        log_t = sb("log_t", [128, 1])

        x_t = sb("x_t", [128, TIN])
        h_new = sb("h_new", [128, 3, D])
        r_new = sb("r_new", [128, 3, D])
        h_cur = sb("h_cur", [128, 3, D])
        r_cur = sb("r_cur", [128, 3, D])
        u_tok = sb("u_tok", [128, 3, D])
        u_t = sb("u_t", [128, 2, L])
        bn = sb("bn", [128, 3, 6])
        mv = sb("mv", [128, 3, 2])
        scales = sb("scales", [128, 2, 3])
        norm_x = sb("norm_x", [128, 2, 3])
        half = sb("half", [128, 6])
        rms = sb("rms", [128, 3])


        xraw = sb("xraw", [128, EC, L + 2 * (TAPS - 1)])
        xc = [sb(f"xc{d}", [128, EC, L]) for d in range(2)]
        sz = [sb(f"sz{d}", [128, EC, L]) for d in range(2)]
        dt_ = [sb(f"dt{d}", [128, EC, L]) for d in range(2)]
        dtx = [sb(f"dtx{d}", [128, EC, L]) for d in range(2)]
        bcs = [sb(f"bcs{d}", [96, L], BF16) for d in range(2)]
        mid = sb("mid", [96, L], BF16)
        rest = sb("rest", [96, L])
        r_sb = rest[0:R, :]

        NA, NX, NH, NP, NB = 2, 2, 2, 2, 4
        da = [sb(f"da{j}", [128, EC, LP]) for j in range(NA)]
        dbx = [sb(f"dbx{j}", [128, EC, LP]) for j in range(NX)]
        hs = [sb(f"hs{j}", [128, EC, LP]) for j in range(NH)]
        pr = [sb(f"pr{j}", [128, EC, LP]) for j in range(NP)]
        bc = [sb(f"bc{j}", [128, 2, L + 1]) for j in range(NB)]

        y2 = sb("y2", [128, EC, L])
        s_tok = sb("s_tok", [128, 3, D])
        ss = sb("ss", [128, 3])
        acc = sb("acc", [128, 3, D])

        tok_x = y2[:, 0, 0:D]
        y_ps = pb("y_ps", [128, EC, 512])
        bc_ps = pb("bc_ps", [128, 2, 512])
        misc = [pb(f"misc{j}", [128, 512]) for j in range(2)]

        loads = sem("loads")
        x_in = sem("x_in")
        setup_a = sem("setup_a")
        setup_v = sem("setup_v")
        setup_done = sem("setup_done")
        full = [sem(f"misc_full{j}") for j in range(2)]
        free = [sem(f"misc_free{j}") for j in range(2)]
        tok_v = sem("tok_v")
        tok_q = sem("tok_q")
        stats_go = sem("stats_go")
        setup_p = sem("setup_p")
        u_done = sem("u_done")
        uT_done = sem("uT_done")
        raw_done = sem("raw_done")
        conv = sem("conv")
        xc_done = sem("xc_done")
        sz_done = sem("sz_done")
        r_done = sem("r_done")
        bc_hi = sem("bc_hi")
        bc_v = sem("bc_v")
        sp_a = sem("sp_a")
        sp_v = sem("sp_v")
        dt_done = sem("dt_done")
        dtx_done = sem("dtx_done")
        bc_mm = sem("bc_mm")
        bc_copied = sem("bc_copied")
        da_done = sem("da_done")
        dbx_v = sem("dbx_v")
        dbx_p = sem("dbx_p")
        h_done = sem("h_done")
        p_done = sem("p_done")
        sum_done = sem("sum_done")
        y2_done = sem("y2_done")
        s_done = sem("s_done")
        ss_done = sem("ss_done")
        q_done = sem("q_done")
        acc_v = sem("acc_v")
        h2_sent = sem("h2_sent")
        zeroed = sem("zeroed")
        moved = sem("moved")

        def ring(n):
            return [k % n for k in range(NS - NS % n)] + list(range(n - NS % n, n))

        A_SLOT, X_SLOT, H_SLOT, B_SLOT = ring(NA), ring(NX), ring(NH), ring(NB)

        def last_in(slots, n):
            return max(m for m in range(-NS, n) if slots[m] == slots[n])

        NPOOL = len(POOL_B)
        NDVE = NS - NPOOL

        def later(value):
            return not isinstance(value, int) or value > 0

        def cnt(u, per, off=0):
            return u[0] * (2 * per) + (u[1] * per + off)

        def batch(u, per, off=0):
            return u[0] * per + ((u[1] // 2) * per + off)

        def after(u, by=1):
            return (u[0], u[1] + by)

        def fills(j, finish, tokens):
            stages = [("out", T_F2[j])] if finish else []
            stages += list(zip(("x0", "x1", "z0", "z1"), T_IN))
            stages += [("tok", T_TOK[j])] if tokens else []
            stages += [("x", T_X[j])] + list(zip(("dt0", "dt1"), T_DT))
            stages += [("tokT", T_TOKT)] if tokens else []
            return [name for name, step in sorted(stages, key=lambda x: x[1])]

        PROLOGUE = (0, -1)
        FIRST, FORWARD, BACKWARD = ([fills(j, *which) for j in range(2)]
                                    for which in ((False, True), (True, True), (True, False)))

        def uses(j, u, what):
            k = u[1]
            if k == -1:
                return (["tok", "tokT"] + fills(j, False, False)).index(what)
            if k == 0:
                return 9 + FIRST[j].index(what)
            if k >= 2 * B - 1 > 2:
                return 18 * B + (k - (2 * B - 1))
            order = (BACKWARD if k % 2 else FORWARD)[j]
            return u[0] * 18 + (18 * (k // 2) + (18 if k % 2 else 8) + order.index(what))

        units = lambda i: [(i, 1), (i, 2)]

        block = ctx.enter_context(nc.Block())

        N_LOADS = 0

        @block.sync
        def _(sp):
            nonlocal N_LOADS
            rows = ["tok_gamma", "tok_beta", "tok_mean", "tok_var", "normf"]
            todo = [(tokw[:, :, :], t["tok_w"]), (tok_b[:, :], t["tok_b"].rearrange("(a n) -> a n", a=1)),
                    (ident[:, :], t["ident"]), (sel[:, :, :], t["sel"])]
            for j, n in enumerate(rows):
                todo.append((tok_rows[:, j, :], t[n].rearrange("(a n) -> a n", a=1).to_broadcast([128, D])))
            for d in range(2):
                todo += [(w_in[d][:, :, :], t[f"in{d}"]), (w_dt[d][:, :, :], t[f"xdt{d}"]),
                         (w_bc[d][:, :, :], t[f"xbc{d}"]), (w_r[d][:, :], t[f"dtw{d}"]),
                         (w_out[d][:, :, :], t[f"out{d}"]), (vec[d][:, :, :], t[f"vec{d}"]),
                         (norm[d][:, :], t[f"norm{d}"])]
            sp.dma_start(x_t[:, :], t["x"][0]).then_inc(x_in, 16)
            for dst, src in todo:
                sp.dma_start(dst, src).then_inc(loads, 16)
            N_LOADS = 16 * len(todo)

            def load_x(src, token_products):
                sp.wait_ge(full[1], token_products)
                sp.dma_start(x_t[:, :], src).then_inc(x_in, 16)

            def store_h2(u):
                b = batch(u, 1, -1)
                sp.wait_ge(acc_v, cnt(u, 5, 1))
                for j, (t0, n) in enumerate(TT):
                    if isinstance(b, int):
                        dst = h2_dram[b, t0:t0 + n, :]
                    else:
                        dst = h2_dram[bass.ds(b, 1), t0:t0 + n, :].rearrange("a t d -> (a t) d")
                    sp.dma_start(dst, acc[0:n, j, :]).then_inc(h2_sent, 16)

            sp.sem_inc(h2_sent, 1)
            pages = x_dram.rearrange("(j p) d -> j p d", p=128)
            zeros = t["zeros"].rearrange("p (a d) -> a p d", a=1)
            ZERO = PAGES // (B - 2)
            load_x(t["x"][1], uses(1, PROLOGUE, "tok") + 1)
            with sp.Fori(0, B - 2) as i:
                sp.dma_start(pages[bass.ds(i * ZERO, ZERO), :, :], zeros.to_broadcast([ZERO, 128, D])).then_inc(zeroed, 16)
                load_x(t["x"][bass.ds(i + 2, 1), :, :].rearrange("a p n -> (a p) n"), i * 18 + (uses(1, (0, 0), "tok") + 1))
                sp.wait_ge(zeroed, i * 16 + 16)
                store_h2((i, 2))
            load_x(t["x"][B - 1], 18 * (B - 2) + (uses(1, (0, 0), "tok") + 1))
            store_h2((0, 2 * B - 2))
            store_h2((0, 2 * B))
            sp.wait_ge(h2_sent, 1 + 48 * B)
            sp.wait_ge(zeroed, 16 * (B - 2))

        @block.tensor
        def _(pe):
            def fill(j, u, what):
                if later(due := uses(j, u, what)):
                    pe.wait_ge(free[j], due)

            def tokens(u, q, banks=(0, 1)):
                pe.wait_ge(x_in, q * 16 + 16)
                for g in banks:
                    fill(g, u, "tok")
                    for j in ((0, 1) if g == 0 else (2,)):
                        t0, n = TT[j]
                        out = misc[g][0:n, (j % 2) * D:(j % 2) * D + D]
                        for c in range(CTX):
                            nc.tensor.matmul(out, x_t[:, t0 + c:t0 + c + n], tokw[:, c, :], start=(c == 0), stop=False)
                        mm = nc.tensor.matmul(out, ones[0:1, 0:n], tok_b[:, :], start=False, stop=True)
                    mm.then_inc(full[g], 1)

            def tokens_t(u, q):
                pe.wait_ge(u_done, q * 3 + 3)
                for c in range(2):
                    fill(c, u, "tokT")
                    for j, (t0, n) in enumerate(TT):
                        mm = nc.tensor.transpose(misc[c][:, t0:t0 + n], u_tok[0:n, j, c * 128:(c + 1) * 128],
                                                 ident[0:n, 0:n])
                    mm.then_inc(full[c], 1)

            def inproj(u, m):
                p, d = after(u), (u[1] + 1) % 2
                if m == 0:
                    pe.wait_ge(uT_done, batch(p, 2, 2))
                j = m % 2
                fill(j, u, ("x0", "x1", "z0", "z1")[m // 2])
                for c in range(2):
                    mm = nc.tensor.matmul(misc[j][:, 0:L], w_in[d][:, c, m * 128:(m + 1) * 128], u_t[:, c, :],
                                          start=(c == 0), stop=(c == 1))
                mm.then_inc(full[j], 1)

            def xproj(u, j):
                p, d = after(u), (u[1] + 1) % 2
                pe.wait_ge(xc_done, cnt(p, 1, 1))
                w, n = ((w_dt[d], R), (w_bc[d], 96))[j]
                fill(j, u, "x")
                for m in range(EC):
                    mm = nc.tensor.matmul(misc[j][0:n, 0:L], w[:, m, :], xc[d][:, m, :],
                                          start=(m == 0), stop=(m == EC - 1))
                mm.then_inc(full[j], 1)

            def dtproj(u, m):
                p, d = after(u), (u[1] + 1) % 2
                if m == 0:
                    pe.wait_ge(r_done, cnt(p, 1, 1))
                j = m % 2
                fill(j, u, ("dt0", "dt1")[m // 2])
                nc.tensor.matmul(misc[j][:, 0:L], w_r[d][:, m * 128:(m + 1) * 128], r_sb,
                                 start=True, stop=True).then_inc(full[j], 1)

            def spread(u, n):
                d = u[1] % 2
                if n == 0:
                    pe.wait_ge(bc_v, cnt(u, 4, 4))
                if later(due := cnt(u, NS, n)):
                    pe.wait_ge(bc_copied, due)
                nc.tensor.matmul(bc_ps[:, 0, 0:L], sel[:, n, :], bcs[d][:, :], start=True, stop=True)
                nc.tensor.matmul(bc_ps[:, 1, 0:L], sel[:, NS + n, :], bcs[d][:, :], start=True, stop=True).then_inc(bc_mm, 1)

            def add_state(u, n):
                if n == 0:
                    if later(due := cnt(u, 1)):
                        pe.wait_ge(y2_done, due)
                pe.wait_ge(p_done, cnt(u, NS, n + 1))
                for m in range(EC):
                    mm = nc.tensor.matmul(y_ps[:, m, 0:L], ident[:, :], pr[n % NP][:, m, 0:L],
                                          start=(n == 0), stop=(n == NS - 1))
                mm.then_inc(sum_done, 1)
                if n in N_SKIP:
                    for m in range(2 * N_SKIP.index(n), 2 * N_SKIP.index(n) + 2):
                        nc.tensor.matmul(y_ps[:, m, 0:L], skip[u[1] % 2][:, m, :], xc[u[1] % 2][:, m, :], start=False, stop=False)

            def outproj(u, g):
                d = (u[1] + 1) % 2
                pe.wait_ge(y2_done, cnt(u, 1))
                fill(g, u, "out")
                for j in ((0, 1) if g == 0 else (2,)):
                    t0, n = TT[j]
                    for m in range(EC):
                        mm = nc.tensor.matmul(misc[g][0:n, (j % 2) * D:(j % 2) * D + D], y2[:, m, t0:t0 + n],
                                              w_out[d][:, m, :], start=(m == 0), stop=(m == EC - 1))
                mm.then_inc(full[g], 1)

            def prepare(u, step):
                if step in T_IN:
                    m = 2 * T_IN.index(step)
                    inproj(u, m)
                    inproj(u, m + 1)
                for j in range(2):
                    if u[1] % 2 == 0 and step == T_TOK[j]:
                        tokens(u, batch(u, 1, 1), (j,))
                for j in range(2):
                    if step == T_X[j]:
                        xproj(u, j)
                if step in T_DT:
                    m = 2 * T_DT.index(step)
                    dtproj(u, m)
                    dtproj(u, m + 1)
                if u[1] % 2 == 0 and step == T_TOKT:
                    tokens_t(u, batch(u, 1, 1))

            def unit(u, before=True, own=True, nxt=True):
                for step in range(NS if own else T_F2[1] + 1):
                    if own and step + AHEAD_BC < NS:
                        spread(u, step + AHEAD_BC)
                    elif nxt:
                        spread(after(u), step + AHEAD_BC - NS)
                    if step >= 2 and own:
                        add_state(u, step - 2)
                    elif step < 2 and before:
                        add_state(after(u, -1), step - 2 + NS)
                    for j in range(2):
                        if before and step == T_F2[j]:
                            outproj(u, j)
                    if nxt:
                        prepare(u, step)

            pe.wait_ge(setup_done, 1)
            tokens(PROLOGUE, 0)
            tokens_t(PROLOGUE, 0)
            for step in range(NS):
                prepare(PROLOGUE, step)
            for n in range(AHEAD_BC):
                spread((0, 0), n)
            unit((0, 0), before=False)
            with pe.Fori(0, B - 1) as i:
                for u in units(i):
                    unit(u)
            unit((0, 2 * B - 1), nxt=False)
            unit((0, 2 * B), own=False, nxt=False)

        @block.scalar
        def _(act):
            def got(j, u, what):
                act.wait_ge(full[j], uses(j, u, what) + 1)

            def tokens_t(u, q):
                for c in range(2):
                    got(c, u, "tokT")
                    nc.scalar.activation(u_t[:, c, :], misc[c][:, 0:L], ACT.Copy).then_inc(uT_done, 1)
                    act.wait_ge(uT_done, q * 2 + (c + 1))
                    act.sem_inc(free[c], 1)

            def evacuate(u, m):
                p, d = after(u), (u[1] + 1) % 2
                j = m % 2
                got(j, u, ("x0", "x1", "z0", "z1")[m // 2])
                if m == 0:
                    if later(due := cnt(p, 1, -1)):
                        act.wait_ge(y2_done, due)
                    if later(due := cnt(p, 3 * EC)):
                        act.wait_ge(conv, due)
                if m < EC:
                    nc.scalar.activation(xraw[:, m, TAPS - 1:TAPS - 1 + L], misc[j][:, 0:L], ACT.Copy).then_inc(raw_done, 1)
                    nc.scalar.activation(xc[d][:, m, :], misc[j][:, 0:L], ACT.Identity, scale=vec[d][:, m, TAPS - 1:TAPS],
                                         bias=vec[d][:, m, TAPS:TAPS + 1]).then_inc(free[j], 1)
                else:
                    nc.scalar.activation(sz[d][:, m - EC, :], misc[j][:, 0:L], ACT.Copy).then_inc(free[j], 1)

            def silu_x(u):
                p, d = after(u), (u[1] + 1) % 2
                act.wait_ge(conv, cnt(p, 3 * EC, 3 * EC))
                nc.scalar.activation(xc[d][:, :, :], xc[d][:, :, :], ACT.Silu).then_inc(xc_done, 1)
                for j in range(2):
                    act.wait_ge(free[j], uses(j, u, "z1") + 1)
                nc.scalar.activation(sz[d][:, :, :], sz[d][:, :, :], ACT.Silu).then_inc(sz_done, 1)
                act.preload_act_table_set(EXP_LN)

            def take_r(u):
                p = after(u)
                got(0, u, "x")
                nc.scalar.activation(r_sb, misc[0][0:R, 0:L], ACT.Copy).then_inc(r_done, 1)
                act.wait_ge(r_done, cnt(p, 1, 1))
                act.sem_inc(free[0], 1)

            def take_bc(u):
                p, d = after(u), (u[1] + 1) % 2
                got(1, u, "x")
                nc.scalar.activation(bcs[d][:, :], misc[1][0:96, 0:L], ACT.Copy).then_inc(bc_hi, 1)

            def softplus_in(u, m):
                p, d = after(u), (u[1] + 1) % 2
                j = m % 2
                got(j, u, ("dt0", "dt1")[m // 2])
                b = vec[d][:, m, TAPS + 1:TAPS + 2]
                nc.scalar.activation(dt_[d][:, m, :], misc[j][:, 0:L], ACT.Relu, bias=b)
                nc.scalar.activation(xraw[:, m, TAPS - 1:TAPS - 1 + L], misc[j][:, 0:L], ACT.Abs, bias=b).then_inc(free[j], 1)

            def softplus_exp(u):
                p = after(u)
                v = xraw[:, :, TAPS - 1:TAPS - 1 + L]
                act.wait_ge(free[0], uses(0, u, "dt1") + 1)
                act.wait_ge(free[1], uses(1, u, "dt1") + 1)
                nc.scalar.activation(v, v, ACT.Exp, scale=-1.0).then_inc(sp_a, 1)

            def softplus_ln(u):
                p, d = after(u), (u[1] + 1) % 2
                act.wait_ge(sp_a, cnt(p, 4, 1))
                if later(due := cnt(p, NS, -NS)):
                    act.wait_ge(h_done, due)
                nc.scalar.activation(dtx[d][:, :, :], xraw[:, :, TAPS - 1:TAPS - 1 + L], ACT.Relu, bias=eps_c[:, 2:3]).then_inc(sp_a, 1)
                act.wait_ge(sp_a, cnt(p, 4, 2))
                nc.scalar.activation(dtx[d][:, :, :], dtx[d][:, :, :], ACT.Ln, bias=eps_c[:, 1:2]).then_inc(sp_a, 1)

            def square_small(u):
                p = after(u)
                act.wait_ge(sp_v, cnt(p, 3, 1))
                nc.scalar.activation(y2[:, :, :], xraw[:, :, TAPS - 1:TAPS - 1 + L], ACT.Square, scale=SQUARE[0],
                                     bias=eps_c[:, 3:4]).then_inc(sp_a, 1)

            def copy_bc(u, n):
                act.wait_ge(bc_mm, cnt(u, NS, n + 1))
                if later(due := cnt(u, NS, last_in(B_SLOT, n) + 1)):
                    act.wait_ge(p_done, due)
                dv = sum(1 for x in range(last_in(B_SLOT, n) + 1 + NS) if x % NS not in POOL_B) - NDVE
                if later(due := cnt(u, NDVE, dv)):
                    act.wait_ge(dbx_v, due)
                nc.scalar.activation(bc[B_SLOT[n]][:, :, 0:L], bc_ps[:, :, 0:L], ACT.Copy).then_inc(bc_copied, 1)

            def decay(u, n):
                d = u[1] % 2
                if n == 0:
                    act.wait_ge(dt_done, cnt(u, 1, 1))
                if later(due := cnt(u, NS, last_in(A_SLOT, n) + 1)):
                    act.wait_ge(h_done, due)
                for m in range(EC):
                    a = nc.scalar.activation(da[A_SLOT[n]][:, m, 1:L], dt_[d][:, m, 1 - d:L - d], ACT.Exp,
                                             scale=neg_a[d][:, m, n:n + 1])
                a.then_inc(da_done, 1)

            def squares(u):
                act.wait_ge(s_done, cnt(u, 2))
                act.wait_ge(q_done, cnt(u, 1))
                for j, (t0, n) in enumerate(TT):
                    nc.scalar.activation(y2[0:n, j, 0:D], s_tok[0:n, j, :], ACT.Square, accum_out=ss[0:n, j:j + 1]).then_inc(ss_done, 1)
                act.wait_ge(ss_done, cnt(u, 4, -1))
                nc.scalar.activation(ss[:, :], ss[:, :], ACT.Identity, scale=1.0 / D, bias=eps_c[:, 0:1]).then_inc(ss_done, 1)

            def prepare(u, step):
                if step in T_EVAC:
                    m = 2 * T_EVAC.index(step)
                    evacuate(u, m)
                    evacuate(u, m + 1)
                if step == T_SILU:
                    silu_x(u)
                if step - 1 == T_X[0]:
                    take_r(u)
                if step - 1 == T_X[1]:
                    take_bc(u)
                if step - 1 in T_DT:
                    m = 2 * T_DT.index(step - 1)
                    softplus_in(u, m)
                    softplus_in(u, m + 1)
                    if m == 2:
                        softplus_exp(u)
                if step == T_LN:
                    softplus_ln(u)
                if step == T_SQUARE:
                    square_small(u)
                if u[1] % 2 == 0 and step - 1 == T_TOKT:
                    tokens_t(u, batch(u, 1, 1))

            def unit(u, before=True, own=True, nxt=True):
                for step in range(NS if own else T_SQ + 1):
                    if before and step == T_SQ:
                        squares(u)
                    if nxt:
                        prepare(u, step)
                    if own and step + AHEAD_BC < NS:
                        copy_bc(u, step + AHEAD_BC)
                    elif nxt:
                        copy_bc(after(u), step + AHEAD_BC - NS)
                    if own and step + AHEAD_DECAY < NS:
                        decay(u, step + AHEAD_DECAY)
                    elif nxt:
                        decay(after(u), step + AHEAD_DECAY - NS)

            act.preload_act_table_set(EXP_LN)
            act.wait_ge(loads, N_LOADS)
            act.wait_ge(setup_v, 1)
            nc.scalar.activation(log_t[:, :], eps_c[:, 1:2], ACT.Ln).then_inc(setup_a, 1)
            for d in range(2):
                nc.scalar.activation(neg_a[d][:, :, :], vec[d][:, :, TAPS + 3:NV], ACT.Exp).then_inc(setup_a, 1)
            tokens_t(PROLOGUE, 0)
            for step in range(NS):
                prepare(PROLOGUE, step)
            for n in range(AHEAD_BC):
                copy_bc((0, 0), n)
            for n in range(AHEAD_DECAY):
                decay((0, 0), n)
            unit((0, 0), before=False)
            with act.Fori(0, B - 1) as i:
                for u in units(i):
                    unit(u)
            unit((0, 2 * B - 1), nxt=False)
            unit((0, 2 * B), own=False, nxt=False)

        @block.vector
        def _(dve):
            def got(j, u, what):
                dve.wait_ge(full[j], uses(j, u, what) + 1)

            def rows2(x):
                return x.rearrange("p (a n) -> p a n", a=2)

            def tokens(u, q):
                got(0, u, "tok")
                if later(due := q * 2):
                    dve.wait_ge(moved, due)
                nc.vector.scalar_tensor_tensor(h_new[:, 0:2, :], rows2(misc[0][:, :]), 0.0, tok_scale.rearrange("p (a n) -> p a n", a=1).to_broadcast([128, 2, D]),
                                               ALU.max, ALU.mult).then_inc(free[0], 1)
                got(1, u, "tok")
                n = TT[2][1]
                nc.vector.scalar_tensor_tensor(h_new[0:n, 2, :], misc[1][0:n, 0:D], 0.0, tok_scale[0:n, :],
                                               ALU.max, ALU.mult).then_inc(free[1], 1)
                dve.wait_ge(free[0], uses(0, u, "tok") + 1)
                nc.vector.tensor_tensor(h_new[:, 0:2, :], h_new[:, 0:2, :], tok_shift.rearrange("p (a n) -> p a n", a=1).to_broadcast([128, 2, D]),
                                        ALU.add).then_inc(tok_v, 1)
                dve.wait_ge(free[1], uses(1, u, "tok") + 1)
                nc.vector.tensor_tensor(h_new[0:n, 2, :], h_new[0:n, 2, :], tok_shift[0:n, :], ALU.add).then_inc(tok_v, 1)
                for j, (t0, n) in enumerate(TT):
                    dve.wait_ge(tok_v, q * 10 + (1 if j < 2 else 2))
                    nc.vector.bn_stats(bn[0:n, j, :], h_new[0:n, j, :]).then_inc(tok_v, 1)
                dve.wait_ge(tok_v, q * 10 + 5)
                dve.sem_inc(stats_go, 1)
                for j, (t0, n) in enumerate(TT):
                    nc.vector.bn_aggr(mv[0:n, j, :], bn[0:n, j, :]).then_inc(tok_v, 1)
                dve.wait_ge(tok_v, q * 10 + 8)
                nc.vector.tensor_scalar(norm_x[:, 0, :], mv[:, :, 1], 1.0, EPS, ALU.mult, ALU.add).then_inc(tok_v, 1)
                nc.vector.tensor_scalar(norm_x[:, 1, :], mv[:, :, 1], 1.0 + EPS, EPS * EPS, ALU.mult, ALU.add).then_inc(tok_v, 1)

            def normalise(u, q):
                dve.wait_ge(tok_q, q + 1)
                for j, (t0, n) in enumerate(TT):
                    nc.vector.tensor_scalar(u_tok[0:n, j, :], h_new[0:n, j, :], mv[0:n, j, 0:1], scales[0:n, 1, j:j + 1],
                                            ALU.subtract, ALU.mult).then_inc(u_done, 1)
                for j, (t0, n) in enumerate(TT):
                    a = nc.vector.tensor_scalar(r_new[0:n, j, :], h_new[0:n, j, :], mv[0:n, j, 0:1], scales[0:n, 0, j:j + 1],
                                                ALU.subtract, ALU.mult)
                a.then_inc(moved, 1)

            def take_tokens(u):
                q = batch(u, 1)
                dve.wait_ge(moved, q * 2 + 1)
                nc.vector.tensor_copy(h_cur[:, 0:2, :], h_new[:, 0:2, :])
                nc.vector.tensor_copy(r_cur[:, 0:2, :], r_new[:, 0:2, :])
                n = TT[2][1]
                nc.vector.tensor_copy(h_cur[0:n, 2, :], h_new[0:n, 2, :])
                nc.vector.tensor_copy(r_cur[0:n, 2, :], r_new[0:n, 2, :]).then_inc(moved, 1)

            def convolve(u, k):
                p, d = after(u), (u[1] + 1) % 2
                for m in range(EC):
                    if k == 0:
                        dve.wait_ge(free[m % 2], uses(m % 2, u, ("x0", "x1")[m // 2]) + 1)
                        if m == 0:
                            dve.wait_ge(raw_done, cnt(p, EC, EC))
                    else:
                        dve.wait_ge(conv, cnt(p, 3 * EC, (k - 1) * EC + m + 1))
                    t0 = k if d == 0 else 2 * (TAPS - 1) - k
                    nc.vector.scalar_tensor_tensor(xc[d][:, m, :], xraw[:, m, t0:t0 + L], vec[d][:, m, k:k + 1], xc[d][:, m, :],
                                                   ALU.mult, ALU.add).then_inc(conv, 1)

            def split_bc(u):
                p, d = after(u), (u[1] + 1) % 2
                dve.wait_ge(bc_hi, cnt(p, 1, 1))
                nc.vector.tensor_tensor(mid[64:96, :], misc[1][64:96, 0:L], bcs[d][64:96, :], ALU.subtract).then_inc(bc_v, 1)
                nc.vector.tensor_tensor(rest[64:96, :], misc[1][64:96, 0:L], bcs[d][64:96, :], ALU.subtract).then_inc(bc_v, 1)
                nc.vector.tensor_tensor(bcs[d][32:64, :], misc[1][32:64, 0:L], bcs[d][32:64, :], ALU.subtract).then_inc(free[1], 1)
                dve.wait_ge(bc_v, cnt(p, 4, 2))
                nc.vector.tensor_tensor(bcs[d][64:96, :], rest[64:96, :], mid[64:96, :], ALU.subtract).then_inc(bc_v, 1)
                dve.wait_ge(free[1], uses(1, u, "x") + 1)
                dve.sem_inc(bc_v, 1)

            def limit(u):
                p = after(u)
                m = xraw[:, :, TAPS - 1:TAPS - 1 + L]
                dve.wait_ge(sp_a, cnt(p, 4, 2))
                nc.vector.tensor_scalar(m, m, LOG_T, None, ALU.min).then_inc(sp_v, 1)

            def log1p_small(u):
                p = after(u)
                m = xraw[:, :, TAPS - 1:TAPS - 1 + L]
                dve.wait_ge(sp_a, cnt(p, 4, 4))
                nc.vector.scalar_tensor_tensor(y2[:, :, :], y2[:, :, :], SQUARE[2], m, ALU.add, ALU.mult).then_inc(sp_v, 1)

            def add_dt(u):
                p, d = after(u), (u[1] + 1) % 2
                dve.wait_ge(sp_a, cnt(p, 4, 3))
                nc.vector.scalar_tensor_tensor(dt_[d][:, :, :], dtx[d][:, :, :], log_t[:, 0:1], dt_[d][:, :, :],
                                               ALU.subtract, ALU.add).then_inc(sp_v, 1)
                dve.wait_ge(sp_v, cnt(p, 3, 3))
                nc.vector.tensor_tensor(dt_[d][:, :, :], dt_[d][:, :, :], y2[:, :, :], ALU.add).then_inc(dt_done, 1)

            def form_dtx(u):
                p, d = after(u), (u[1] + 1) % 2
                dve.wait_ge(dt_done, cnt(p, 1, 1))
                if later(due := cnt(p, NPOOL, -NPOOL)):
                    dve.wait_ge(dbx_p, due)
                nc.vector.tensor_tensor(dtx[d][:, :, :], dt_[d][:, :, :], xc[d][:, :, :], ALU.mult).then_inc(dtx_done, 1)

            def drive(u, n):
                if n in POOL_B:
                    return
                d = u[1] % 2
                if n == 0:
                    dve.wait_ge(dtx_done, cnt(u, 1, 1))
                dve.wait_ge(bc_copied, cnt(u, NS, n + 1))
                if later(due := cnt(u, NS, last_in(X_SLOT, n) + 1)):
                    dve.wait_ge(h_done, due)
                nc.vector.tensor_tensor(dbx[X_SLOT[n]][:, :, d:d + L], dtx[d][:, :, :],
                                        bc[B_SLOT[n]][:, 0, None, 0:L].to_broadcast([128, EC, L]), ALU.mult).then_inc(dbx_v, 1)

            def scan(u, n):
                d = u[1] % 2
                if n in POOL_B:
                    dve.wait_ge(dbx_p, cnt(u, NPOOL, sum(1 for x in POOL_B if x <= n)))
                else:
                    dve.wait_ge(dbx_v, cnt(u, NDVE, sum(1 for x in range(n + 1) if x not in POOL_B)))
                dve.wait_ge(da_done, cnt(u, NS, n + 1))
                if later(due := cnt(u, NS, last_in(H_SLOT, n) + 1)):
                    dve.wait_ge(p_done, due)
                flat = lambda x: x[:, :, :].rearrange("p m l -> p (m l)")
                a, b, o = flat(da[A_SLOT[n]]), flat(dbx[X_SLOT[n]]), flat(hs[H_SLOT[n]])
                if d:
                    a, b, o = a[:, ::-1], b[:, ::-1], o[:, ::-1]
                nc.vector.tensor_tensor_scan(o, a, b, 0.0, ALU.mult, ALU.add).then_inc(h_done, 1)

            def gate(u):
                d = (u[1] + 1) % 2
                dve.wait_ge(sum_done, cnt(u, NS))
                dve.wait_ge(sz_done, cnt(u, 1))
                nc.vector.tensor_tensor(y2[:, :, :], y_ps[:, :, 0:L], sz[d][:, :, :], ALU.mult).then_inc(y2_done, 1)

            def residual(u):
                got(0, u, "out")
                nc.vector.tensor_tensor(s_tok[:, 0:2, :], rows2(misc[0][:, :]), r_cur[:, 0:2, :], ALU.add).then_inc(s_done, 1)
                got(1, u, "out")
                n = TT[2][1]
                nc.vector.tensor_tensor(s_tok[0:n, 2, :], misc[1][0:n, 0:D], r_cur[0:n, 2, :], ALU.add).then_inc(s_done, 1)
                dve.wait_ge(s_done, cnt(u, 2))
                dve.sem_inc(free[0], 1)
                dve.sem_inc(free[1], 1)

            def accumulate(u):
                d = (u[1] + 1) % 2
                dve.wait_ge(q_done, cnt(u, 1, 1))
                for j, (t0, n) in enumerate(TT):
                    nc.vector.scalar_tensor_tensor(s_tok[0:n, j, :], s_tok[0:n, j, :], rms[0:n, j:j + 1], tok_rows[0:n, 4, :],
                                                   ALU.mult, ALU.mult).then_inc(acc_v, 1)
                if d == 0:
                    dve.wait_ge(h2_sent, batch(u, 48, 1))
                other = h_cur if d == 0 else acc
                n = TT[2][1]
                dve.wait_ge(acc_v, cnt(u, 5, 1 - 5 + 3))
                nc.vector.tensor_tensor(acc[:, 0:2, :], s_tok[:, 0:2, :], other[:, 0:2, :], ALU.add).then_inc(acc_v, 1)
                nc.vector.tensor_tensor(acc[0:n, 2, :], s_tok[0:n, 2, :], other[0:n, 2, :], ALU.add).then_inc(acc_v, 1)

            def prepare(u, step):
                if step in T_CONV:
                    convolve(u, T_CONV.index(step))
                if u[1] % 2 == 0 and step == T_TOKV:
                    tokens(u, batch(u, 1, 1))
                if step - 1 == T_X[1]:
                    split_bc(u)
                if u[1] % 2 == 0 and step == T_NORM:
                    normalise(u, batch(u, 1, 1))
                if step == T_LIMIT:
                    limit(u)
                if step == T_SMALL:
                    log1p_small(u)
                if step == T_ADD:
                    add_dt(u)
                if step == T_DTX:
                    form_dtx(u)

            def unit(u, before=True, own=True, nxt=True):
                for step in range(NS if own else T_F4 + 1):
                    if before and step == T_F1:
                        gate(u)
                    if own and step + 1 < NS:
                        drive(u, step + 1)
                    elif nxt:
                        drive(after(u), 0)
                    if own:
                        scan(u, step)
                    if before and step == T_F3:
                        residual(u)
                    if before and step == T_F4:
                        accumulate(u)
                    if own and u[1] % 2 == 0 and step == T_TAKE:
                        take_tokens(u)
                    if nxt:
                        prepare(u, step)

            dve.sem_inc(acc_v, 1)
            for x in da:
                nc.vector.memset(x[:, :, :], 0.0)
            for x in dbx:
                nc.vector.memset(x[:, :, :], 0.0)
            nc.vector.memset(xraw[:, :, :], 0.0)
            nc.vector.memset(mv[:, :, :], 1.0)
            nc.vector.memset(ss[:, :], 1.0)
            nc.vector.memset(ones[:, :], 1.0)
            nc.vector.memset(eps_c[:, 0:1], EPS)
            nc.vector.memset(eps_c[:, 2:3], -LOG_T)
            nc.vector.memset(eps_c[:, 3:4], SQUARE[1])
            nc.vector.memset(eps_c[:, 1:2], 1.0 + LOG_T).then_inc(setup_v, 1)
            dve.wait_ge(setup_v, 1)
            dve.wait_ge(setup_a, 3)
            nc.vector.tensor_scalar(tok_x, tok_rows[:, 3, :], EPS, None, ALU.add).then_inc(setup_v, 1)
            dve.wait_ge(setup_v, 2)
            dve.wait_ge(setup_p, 2)
            nc.vector.tensor_tensor(tok_scale, tok_scale, tok_power, ALU.mult).then_inc(setup_v, 1)
            dve.wait_ge(setup_v, 3)
            nc.vector.tensor_tensor(tok_rows[:, 2, :], tok_rows[:, 2, :], tok_scale, ALU.mult).then_inc(setup_v, 1)
            dve.wait_ge(setup_v, 4)
            nc.vector.tensor_tensor(tok_shift, tok_shift, tok_rows[:, 2, :], ALU.subtract).then_inc(setup_v, 1)
            for d in range(2):
                nc.vector.tensor_scalar(neg_a[d][:, :, :], neg_a[d][:, :, :], -1.0, None, ALU.mult).then_inc(setup_v, 1)
                for c in range(2):
                    nc.vector.tensor_scalar(w_in[d][:, c, :], w_in[d][:, c, :], norm[d][:, c:c + 1], None, ALU.mult).then_inc(setup_v, 1)
                for m in range(EC):
                    nc.vector.tensor_scalar(skip[d][:, m, :], ident[:, :], vec[d][:, m, TAPS + 2:TAPS + 3], None,
                                            ALU.mult).then_inc(setup_v, 1)
            dve.wait_ge(setup_v, 11 + 2 * EC)
            dve.sem_inc(setup_done, 1)
            tokens(PROLOGUE, 0)
            normalise(PROLOGUE, 0)
            for step in range(NS):
                prepare(PROLOGUE, step)
            drive((0, 0), 0)
            unit((0, 0), before=False)
            with dve.Fori(0, B - 1) as i:
                for u in units(i):
                    unit(u)
            unit((0, 2 * B - 1), nxt=False)
            unit((0, 2 * B), own=False, nxt=False)

        @block.gpsimd
        def _(pool):
            def drive(u, n):
                if n not in POOL_B:
                    return
                d = u[1] % 2
                if n == POOL_B[0]:
                    pool.wait_ge(dtx_done, cnt(u, 1, 1))
                pool.wait_ge(bc_copied, cnt(u, NS, n + 1))
                pool.wait_ge(h_done, cnt(u, NS, last_in(X_SLOT, n) + 1))
                nc.gpsimd.tensor_tensor(dbx[X_SLOT[n]][:, :, d:d + L], dtx[d][:, :, :],
                                        bc[B_SLOT[n]][:, 0, None, 0:L].to_broadcast([128, EC, L]), ALU.mult).then_inc(dbx_p, 1)

            def weigh(u, n):
                d = u[1] % 2
                pool.wait_ge(h_done, cnt(u, NS, n + 1))
                if later(due := cnt(u, NS, n + 1 - NP)):
                    pool.wait_ge(sum_done, due)
                nc.gpsimd.tensor_tensor(pr[n % NP][:, :, 0:L], hs[H_SLOT[n]][:, :, d:d + L],
                                        bc[B_SLOT[n]][:, 1, None, 0:L].to_broadcast([128, EC, L]), ALU.mult).then_inc(p_done, 1)

            def token_power(q):
                pool.wait_ge(tok_v, q * 10 + 10)
                if later(due := q * 2):
                    pool.wait_ge(moved, due)
                nc.gpsimd.tensor_tensor(scales[:, :, :].rearrange("p a b -> p (a b)"), norm_x[:, :, :].rearrange("p a b -> p (a b)"),
                                        half[:, 0:6], ALU.pow).then_inc(tok_q, 1)

            def unit_power(u):
                pool.wait_ge(ss_done, cnt(u, 4))
                pool.wait_ge(acc_v, cnt(u, 5, 1 - 5))
                nc.gpsimd.tensor_tensor(rms[:, :], ss[:, :], half[:, 0:3], ALU.pow).then_inc(q_done, 1)

            def unit(u, before=True, own=True, nxt=True):
                for step in range(NS if own else T_SQ + 1):
                    if own and step + 1 < NS:
                        drive(u, step + 1)
                    elif nxt:
                        drive(after(u), 0)
                    if step >= 1 and own:
                        weigh(u, step - 1)
                    elif step == 0 and before:
                        weigh(after(u, -1), NS - 1)
                    if before and step == T_SQ:
                        unit_power(u)
                    if nxt and u[1] % 2 == 0 and step == T_TOKQ:
                        token_power(batch(u, 1, 1))

            pool.sem_inc(q_done, 1)
            nc.gpsimd.memset(half[:, :], -0.5).then_inc(setup_p, 1)
            pool.wait_ge(setup_p, 1)
            pool.wait_ge(setup_v, 2)
            nc.gpsimd.tensor_tensor(tok_power, tok_x, half[:, 0:1].to_broadcast([128, D]), ALU.pow).then_inc(setup_p, 1)
            token_power(0)
            unit((0, 0), before=False)
            with pool.Fori(0, B - 1) as i:
                for u in units(i):
                    unit(u)
            unit((0, 2 * B - 1), nxt=False)
            unit((0, 2 * B), own=False, nxt=False)


def experts(nc, t, h2_dram, x_dram, y_dram, out):
    ctx = ExitStack()
    with ctx:
        def sb(name, shape, dt=F32):
            return ctx.enter_context(nc.sbuf_tensor(name, shape, dt))

        def pb(name, shape):
            return ctx.enter_context(nc.psum_tensor(name, shape, F32))

        def sem(name):
            return ctx.enter_context(nc.semaphore(name))

        def later(value):
            return not isinstance(value, int) or value > 0

        flip_id = sb("flip_id", [128, 128])
        before = sb("before", [128, 128], BF16)
        all_ones = sb("all_ones", [128, 128], BF16)
        one1 = sb("one1", [1, 1])
        w_sel = sb("w_sel", [128, 2, X])
        iota_x = sb("iota_x", [128, X])
        iota_p = sb("iota_p", [X, PAGES])
        index_x = sb("index_x", [X, 128])
        ones_x = sb("ones_x", [128, X])

        h_all = sb("h_all", [128, max(NT, XS0 + TP), D])
        stats = sb("stats", [128, GM, 6])
        mv = sb("mv_x", [128, GM, 2])
        mean = sb("mean", [128, NT])
        var_x = sb("var_x", [128, NT])
        rstd = sb("rstd", [128, NT])
        shift = sb("shift", [128, NT])
        minus_half = sb("minus_half", [128, NT])
        vals = sb("vals", [128, NT, TOPK])
        gates = sb("gates", [128, NT, TOPK])
        pos_all = sb("pos_all", [128, NT, TOPK])

        hn_all = sb("hn_all", [128, GR, D])
        hn = [hn_all[:, j, :] for j in range(GR)]
        hn_t = [sb(f"hn_t{j}", [128, 2, 128]) for j in range(DEEP)]
        lg = sb("lg", [128, X])
        top = sb("top", [128, 8])
        top_i = sb("top_i", [128, 8], U32)
        top_f = sb("top_f", [128, TOPK])
        oh = [sb(f"oh{j}", [128, TOPK, X], BF16) for j in range(2)]
        at = sb("at", [128, TOPK, X])
        pos_f = sb("pos_f", [128, TOPK])
        pos = [sb(f"pos{j}", [128, TOPK], I32) for j in range(GR)]
        taken = [sb(f"taken{j}", [128, TOPK], I32) for j in range(TS)]
        lack = sb("lack", [128, X])
        end128 = sb("end128", [128, X])
        given = [sb(f"given{j}", [128, X]) for j in range(2)]
        need = sb("need", [128, X])
        flag = sb("flag", [128, X])
        jump = sb("jump", [128, X])
        step_ = sb("step_", [128, X])
        rel = sb("rel", [128, X])
        rel_jump = sb("rel_jump", [128, X])
        slot = sb("slot", [128, X])
        fresh = [sb(f"fresh{j}", [1, X]) for j in range(2)]
        owner = sb("owner", [X, PAGES])
        owner_i = sb("owner_i", [1, PAGES], I32)

        w_all = sb("w_all", [128, X, 2 * HX + D])
        xs_t = hn_t
        hid = [at[:, 2 * j:2 * j + 2, :].rearrange("p a b -> p (a b)") for j in range(2)]

        rows = [h_all[:, TOPK * j:TOPK * j + TOPK, :] for j in range(TS)]
        h_tile = [h_all[:, TOPK * TS + j, :] for j in range(TS)]
        res = [h_all[:, TOPK * TS + TS + j, :] for j in range(TS)]
        ys = [h_all[:, 6 * TS + S2 * j:6 * TS + S2 * j + S2, :] for j in range(2)]
        xs = [h_all[:, XS0 + S2 * j:XS0 + S2 * j + S2, :] for j in range(LOADS)]
        wx = [h_all[:, 6 * TS + S + 2 * j:6 * TS + S + 2 * j + 2, :].rearrange("p a b -> p (a b)") for j in range(DEEP)]

        tp_ps = [pb(f"tp_ps{j}", [128, 512]) for j in range(DEEP)]
        up_ps = [pb(f"up_ps{j}", [128, 512]) for j in range(2)]
        dn_ps = [pb(f"dn_ps{j}", [128, 512]) for j in range(2)]
        col_ps = pb("col_ps", [128, 512])

        consts = sem("consts")
        h_in = sem("h_in")
        set_v = sem("set_v")
        set_p = sem("set_p")
        stat_v = sem("stat_v")
        power_v = sem("power_v")
        power_p = sem("power_p")
        hn_done = sem("hn_done")
        tp_mm = sem("tp_mm")
        hn_t_done = sem("hn_t_done")
        lg_mm = sem("lg_mm")
        pick = sem("pick")
        cnt_mm = sem("cnt_mm")
        place = sem("place")
        fresh_done = sem("fresh_done")
        col_mm = sem("col_mm")
        owner_v = sem("owner_v")
        pos_done = sem("pos_done")
        pool_go = sem("pool_go")
        scattered = [sem(f"scattered{j}") for j in range(GR)]
        owner_mm = sem("owner_mm")
        owner_done = sem("owner_done")
        gates_done = sem("gates_done")
        xs_in = [sem(f"xs_in{j}") for j in range(LOADS)]
        w_in = sem("w_in")
        wx_act = sem("wx_act")
        wx_dve = sem("wx_dve")
        xt_mm = sem("xt_mm")
        xt_done = sem("xt_done")
        hid_mm = sem("hid_mm")
        hid_done = sem("hid_done")
        y_mm = sem("y_mm")
        y_done = sem("y_done")
        y_sent = [sem(f"y_sent{j}") for j in range(2)]
        pages_out = sem("pages_out")
        posg_done = sem("posg_done")
        rows_in = [sem(f"rows_in{j}") for j in range(TS)]
        h_tile_in = [sem(f"h_tile_in{j}") for j in range(TS)]
        sum_v = sem("sum_v")
        out_sent = [sem(f"out_sent{j}") for j in range(TS)]

        block = ctx.enter_context(nc.Block())
        h_rows = h2_dram.rearrange("b t d -> (b t) d")
        out_rows = out.rearrange("b t d -> (b t) d")
        pages_x = x_dram.rearrange("(j p) d -> j p d", p=128)
        pages_y = y_dram.rearrange("(j p) d -> j p d", p=128)
        CH = 12
        chunks = [(a, min(a + CH, NT - 1)) for a in range(0, NT - 1, CH)]
        spans = chunks[:-1] + [(chunks[-1][0], NT)]
        XW = 8
        NV_PICK = 6
        NV_PLACE = 15

        def over_all(eng, step, total, per, ahead=0):
            for k in range(per):
                step(0, k)
            groups = max(0, (total - ahead - per) // per)
            if groups > 0:
                with eng.Fori(1, 1 + groups) as r:
                    for k in range(per):
                        step(r, k)
            for n in range(per * (1 + groups), total):
                step(n // per, n % per)

        def is_last(r, k, ahead, total, per):
            return isinstance(r, int) and r * per + k + ahead >= total

        def first(r, k):
            return isinstance(r, int) and r == 0 and k == 0

        def of_tile(x, i):
            if isinstance(i, int):
                return x[:, i, :]
            return x[:, bass.ds(i, 1), :].rearrange("p a d -> p (a d)")

        def col(x, i):
            return x[:, i:i + 1] if isinstance(i, int) else x[:, bass.ds(i, 1)]

        def cols(x, i, n):
            return x[:, i:i + n] if isinstance(i, int) else x[:, bass.ds(i, n)]

        def some_pages(pages, j):
            if isinstance(j, int):
                return pages[j * S2:j * S2 + S2].rearrange("j p d -> p j d")
            return pages[bass.ds(j * S2, S2), :, :].rearrange("j p d -> p j d")

        def rows_of(i):
            return LAST if isinstance(i, int) and i == NT - 1 else 128

        SUMMED = (TRIPS - LAG) * TS

        def over_trips(eng, trip):
            trip(0, False)
            with eng.Fori(1, LAG) as r:
                trip(r, False)
            trip(LAG, True)
            if TRIPS - 1 > LAG + 1:
                with eng.Fori(LAG + 1, TRIPS - 1) as r:
                    trip(r, True)
            trip(TRIPS - 1, True)

        def picked(r, k):
            r, k = r + k // S, k % S
            if k in ACT_PAGES:
                return wx_act, r * len(ACT_PAGES) + (ACT_PAGES.index(k) + 1)
            others = [n for n in range(S) if n not in ACT_PAGES]
            return wx_dve, r * len(others) + (others.index(k) + 1)

        def at_page(j):
            return owner_i[0:1, j:j + 1] if isinstance(j, int) else owner_i[0:1, bass.ds(j, 1)]

        def of_expert(x):
            return w_all[:, bass.ds(x, 1), :].rearrange("p a n -> p (a n)")

        @block.sync
        def _(sp):
            for dst, src in ((flip_id[:, :], t["ident"]), (before[:, :], t["before"]), (all_ones[:, :], t["all_ones"]),
                             (w_sel[:, :, :], t["sel_w"]), (iota_x[:, :], t["iota_x"]),
                             (iota_p[:, :], t["iota_p"]), (index_x[:, :], t["index_x"])):
                sp.dma_start(dst, src).then_inc(consts, 16)
            for c, (a, b) in enumerate(chunks):
                if later(due := 16 * c):
                    sp.wait_ge(h_in, due)
                src = h_rows[a * 128:b * 128, :].rearrange("(i p) d -> p i d", p=128)
                sp.dma_start(h_all[:, a:b, :], src).then_inc(h_in, 16)
            sp.wait_ge(h_in, 16 * len(chunks))
            sp.dma_start(h_all[0:LAST, NT - 1, :], h_rows[(NT - 1) * 128:N, :]).then_inc(h_in, 16)
            sp.wait_ge(h_in, 16 * (len(chunks) + 1))
            sp.dma_start(h_all[LAST:128, NT - 1, :], h_rows[0:128 - LAST, :]).then_inc(h_in, 16)
            for x in range(0, X, XW):
                sp.dma_start(w_all[:, x:x + XW, :], t["experts"][x:x + XW].rearrange("x p n -> p x n")).then_inc(w_in, 16)

            for s in range(GR):
                sp.wait_ge(scattered[s], 64 * len(range(s, NT, GR)))

            def load(r, k):
                if later(due := r * TP + (k + 1 - LOADS) * S2):
                    sp.wait_ge(xt_mm, due)
                sp.dma_start(xs[k % LOADS][:, :, :], some_pages(pages_x, r * LOADS + k)).then_inc(xs_in[k % LOADS], 16)

            def load_h(i, k):
                src = h_rows[i * 128:i * 128 + rows_of(i), :] if isinstance(i, int) else h_rows[bass.ds(i * 128, 128), :]
                sp.dma_start(h_tile[k][0:rows_of(i), :], src).then_inc(h_tile_in[k], 16)

            def store_sum(i, k):
                sp.wait_ge(sum_v, i * 5 + 4)
                dst = out_rows[i * 128:i * 128 + rows_of(i), :] if isinstance(i, int) else out_rows[bass.ds(i * 128, 128), :]
                sp.dma_start(dst, res[k][0:rows_of(i), :]).then_inc(out_sent[k], 16)

            def trip(r, sums):
                for k in range(LOADS):
                    if not is_last(r, k, LOADS, PAGES // S2, LOADS):
                        load(r, k + LOADS)
                    sp.wait_ge(y_done, r * TP + (k * S2 + S2))
                    sp.dma_start(some_pages(pages_y, r * LOADS + k), ys[k % 2][:, :, :]).then_inc(y_sent[k % 2], 16)
                    if later(due := (r * 2 + (k + 1) // 2) * 16):
                        sp.wait_ge(y_sent[(k + 1) % 2], due)
                        sp.sem_inc(pages_out, S2)
                    if sums and k > 0:
                        next_tile(r * TS + (k - 1 - LAG * TS), k - 1)

            def next_tile(i, k):
                store_sum(i, k)
                if not (isinstance(i, int) and i + TS >= NT):
                    load_h(i + TS, k)

            for k in range(TS):
                load_h(k, k)
            for k in range(LOADS):
                load(0, k)
            over_trips(sp, trip)
            sp.wait_ge(y_sent[(LOADS - 1) % 2], TRIPS * 2 * 16)
            sp.sem_inc(pages_out, S2)
            for i in range(SUMMED, NT):
                next_tile(i, i % TS)
            for k in range(TS):
                sp.wait_ge(out_sent[k], 16 * len(range(k, NT, TS)))

        @block.tensor
        def _(pe):
            pe.wait_ge(consts, 16 * 7)
            pe.wait_ge(set_v, 1)

            def logits(r, k):
                i, p = r * GR + k, k % 2
                pe.wait_ge(hn_done, i + 1)
                if later(due := i - 1):
                    pe.wait_ge(hn_t_done, due)
                for c in range(2):
                    mm = nc.tensor.transpose(tp_ps[p][:, c * 128:(c + 1) * 128], hn[k % GR][:, c * 128:(c + 1) * 128], flip_id[:, :])
                mm.then_inc(tp_mm, 1)
                pe.wait_ge(hn_t_done, i + 1)
                if later(due := (i - 2) * NV_PICK + 1):
                    pe.wait_ge(pick, due)
                for c in range(2):
                    mm = nc.tensor.matmul(up_ps[p][:, 0:X], hn_t[p][:, c, :], w_sel[:, c, :], start=(c == 0), stop=(c == 1))
                mm.then_inc(lg_mm, 1)

            def fresh_column(r, k):
                i, p = r * GR + k, k % 2
                pe.wait_ge(fresh_done, i + 1)
                pe.wait_ge(owner_v, i + 1)
                nc.tensor.matmul(col_ps[0:X, 0:1], fresh[p][0:1, :], one1[:, :], start=True, stop=True).then_inc(col_mm, 1)

            def tile(r, k):
                i, p = r * GR + k, k % 2
                if not is_last(r, k, 2, NT, GR):
                    logits(r, k + 2)
                pe.wait_ge(pick, i * NV_PICK + NV_PICK)
                if later(due := (i - 1) * NV_PLACE):
                    pe.wait_ge(place, due)
                for q in range(TOPK):
                    nc.tensor.matmul(dn_ps[p][:, X:2 * X], all_ones[:, :], oh[p][:, q, :], start=(q == 0), stop=(q == TOPK - 1))
                for q in range(TOPK):
                    mm = nc.tensor.matmul(dn_ps[p][:, 0:X], before[:, :], oh[p][:, q, :], start=(q == 0), stop=(q == TOPK - 1))
                mm.then_inc(cnt_mm, 1)
                if not first(r, k):
                    fresh_column(r, k - 1)

            logits(0, 0)
            logits(0, 1)
            over_all(pe, tile, NT, GR, 2)
            fresh_column(NT // GR, NT % GR - 1)
            pe.wait_ge(owner_v, 1 + NT)
            nc.tensor.matmul(col_ps[:, 0:PAGES], index_x[:, :], owner[:, :], start=True, stop=True).then_inc(owner_mm, 1)

            def flip(r, k):
                j, s, p = r * TP + k, (k // S2) % LOADS, k % DEEP
                pe.wait_ge(xs_in[s], (r + k // TP) * 16 + 16)
                if later(due := j - (DEEP - 1)):
                    pe.wait_ge(xt_done, due)
                for c in range(2):
                    mm = nc.tensor.transpose(tp_ps[p][:, c * 128:(c + 1) * 128], xs[s][:, k % S2, c * 128:(c + 1) * 128], flip_id[:, :])
                mm.then_inc(xt_mm, 1)

            def up(r, k):
                j, p = r * TP + k, k % 2
                pe.wait_ge(*picked(r * 2 + k // S, k % S))
                if later(due := j - 1):
                    pe.wait_ge(hid_done, due)
                pe.wait_ge(xt_done, j + 1)
                for c in range(2):
                    mm = nc.tensor.matmul(up_ps[p][:, 0:128], wx[k % DEEP][:, c * HX:(c + 1) * HX], xs_t[k % DEEP][:, c, :], start=(c == 0), stop=(c == 1))
                mm.then_inc(hid_mm, 1)

            def down(r, k):
                j, p = r * TP + k, k % 2
                if later(due := j - 1):
                    pe.wait_ge(y_done, due)
                pe.wait_ge(hid_done, j + 1)
                nc.tensor.matmul(dn_ps[p][:, 0:D], hid[p], wx[k % DEEP][:, 2 * HX:2 * HX + D], start=True, stop=True).then_inc(y_mm, 1)

            def page(r, k):
                if not is_last(r, k, DEEP, PAGES, TP):
                    flip(r, k + DEEP)
                if not is_last(r, k, 1, PAGES, TP):
                    up(r, k + 1)
                down(r, k)

            for k in range(DEEP):
                flip(0, k)
            up(0, 0)
            over_all(pe, page, PAGES, TP, DEEP)

        @block.scalar
        def _(act):
            def normalise(r, k):
                i = r * GR + k
                if later(due := (r + k // GR) * 64):
                    act.wait_ge(scattered[k % GR], due)
                nc.scalar.activation(hn[k % GR], of_tile(h_all, i), ACT.Identity, bias=col(shift, i), scale=col(rstd, i)).then_inc(hn_done, 1)

            def tile(r, k):
                i, p = r * GR + k, k % 2
                act.wait_ge(tp_mm, i + 1)
                if later(due := i - 1):
                    act.wait_ge(lg_mm, due)
                nc.scalar.copy(hn_t[p][:, :, :].rearrange("p a b -> p (a b)"), tp_ps[p][:, 0:D]).then_inc(hn_t_done, 1)
                if not is_last(r, k, 2, NT, GR):
                    normalise(r, k + 2)

            act.wait_ge(power_p, 2 * len(chunks))
            normalise(0, 0)
            normalise(0, 1)
            over_all(act, tile, NT, GR, 2)
            act.wait_ge(pick, NT * NV_PICK)
            nc.scalar.activation(gates[:, :, :], vals[:, :, :], ACT.Sigmoid).then_inc(gates_done, 1)

            def relu(r, k):
                j, p = r * S + k, k % 2
                if later(due := j - 1):
                    act.wait_ge(y_mm, due)
                act.wait_ge(hid_mm, j + 1)
                nc.scalar.activation(hid[p], up_ps[p][:, 0:128], ACT.Relu).then_inc(hid_done, 1)

            def page(r, k):
                j, p = r * S + k, k % 2
                if not is_last(r, k, 1, PAGES, S):
                    relu(r, k + 1)
                act.wait_ge(y_mm, j + 1)
                if later(due := r * 16):
                    act.wait_ge(y_sent[k // S2], due)
                nc.scalar.copy(ys[k // S2][:, k % S2, :], dn_ps[p][:, 0:D]).then_inc(y_done, 1)
                if not is_last(r, k, DEEP, PAGES, S):
                    weights(r, k + DEEP)

            def weights(r, k):
                if k % S not in ACT_PAGES:
                    return
                x = act.value_load(at_page(r * S + k), min_val=0, max_val=X - 1)
                nc.scalar.copy(wx[k % DEEP], of_expert(x)).then_inc(wx_act, 1)

            act.wait_ge(owner_done, 1)
            act.wait_ge(w_in, 16 * (X // XW))
            for k in range(DEEP):
                weights(0, k)
            relu(0, 0)
            over_all(act, page, PAGES, S, DEEP)

        @block.vector
        def _(dve):
            V = nc.vector
            V.memset(one1[:, :], 1.0)
            V.memset(ones_x[:, :], 1.0)
            V.memset(lack[:, :], 0.0)
            V.memset(end128[:, :], 128.0)
            V.memset(given[1][:, :], 0.0)
            V.memset(owner[:, :], 0.0).then_inc(set_v, 1)
            dve.wait_ge(set_v, 1)
            dve.sem_inc(owner_v, 1)

            def measure(g, i, n):
                for q in range(n):
                    a = V.bn_stats(stats[:, q, :], of_tile(h_all, i + q))
                a.then_inc(stat_v, 1)
                dve.wait_ge(stat_v, g * 4 + 1)
                dve.sem_inc(stat_v, 1)
                for q in range(n):
                    a = V.bn_aggr(mv[:, q, :], stats[:, q, :])
                a.then_inc(stat_v, 1)
                dve.wait_ge(stat_v, g * 4 + 3)
                V.tensor_scalar(cols(mean, i, n), mv[:, 0:n, 0], -1.0, None, ALU.mult)
                V.tensor_scalar(cols(var_x, i, n), mv[:, 0:n, 1], EPS, None, ALU.add).then_inc(stat_v, 1)

            for c, (a, b) in enumerate(spans):
                dve.wait_ge(h_in, 16 * (c + 1 + (2 if b == NT else 0)))
                groups = (b - a) // GM
                if groups:
                    with dve.Fori(0, groups) as r:
                        measure(r + a // GM, r * GM + a, GM)
                if b - a > groups * GM:
                    measure(a // GM + groups, a + groups * GM, b - a - groups * GM)
                dve.wait_ge(stat_v, (b + GM - 1) // GM * 4)
                dve.sem_inc(power_v, 1)

            def choose(r, k):
                i, p = r * GR + k, k % 2
                c = i * NV_PICK
                dve.wait_ge(lg_mm, i + 1)
                V.tensor_scalar(lg[:, :], up_ps[p][:, 0:X], SATURATED, None, ALU.min).then_inc(pick, 1)
                dve.wait_ge(pick, c + 1)
                dve.sem_inc(pick, 1)
                V.max(top[:, :], lg[:, :]).then_inc(pick, 1)
                dve.wait_ge(pick, c + 3)
                V.tensor_copy(of_tile(vals, i), top[:, 0:TOPK])
                V.max_index(top_i[:, :], top[:, :], lg[:, :]).then_inc(pick, 1)
                dve.wait_ge(pick, c + 4)
                V.tensor_copy(top_f[:, :], top_i[:, 0:TOPK]).then_inc(pick, 1)
                dve.wait_ge(pick, c + 5)
                if later(due := i - 1):
                    dve.wait_ge(cnt_mm, due)
                V.tensor_tensor(oh[p][:, :, :], iota_x[:, None, :].to_broadcast([128, TOPK, X]),
                                top_f[:, :, None].to_broadcast([128, TOPK, X]), ALU.is_equal).then_inc(pick, 1)

            def find_slots(r, k):
                i, p = r * GR + k, k % 2
                c = i * NV_PLACE
                pre, tot = dn_ps[p][:, 0:X], dn_ps[p][:, X:2 * X]
                dve.wait_ge(cnt_mm, i + 1)
                if later(due := c):
                    dve.wait_ge(place, due)
                V.tensor_tensor(need[:, :], tot, lack[:, :], ALU.add).then_inc(place, 1)
                V.tensor_tensor(rel[:, :], pre, lack[:, :], ALU.add).then_inc(place, 1)
                dve.wait_ge(place, c + 1)
                V.tensor_scalar(flag[:, :], need[:, :], 0.0, None, ALU.is_gt).then_inc(place, 1)
                dve.wait_ge(place, c + 3)
                V.tensor_tensor_scan(given[p][:, :], ones_x[:, :], flag[:, :], given[1 - p][:, X - 1:X], ALU.mult, ALU.add).then_inc(place, 1)
                V.scalar_tensor_tensor(lack[:, :], flag[:, :], -128.0, need[:, :], ALU.mult, ALU.add).then_inc(place, 1)
                dve.wait_ge(place, c + 4)
                V.scalar_tensor_tensor(jump[:, :], given[p][:, :], 128.0, end128[:, :], ALU.mult, ALU.subtract).then_inc(place, 1)
                if later(due := i - 1):
                    dve.wait_ge(col_mm, due)
                V.tensor_tensor(fresh[p][:, :], given[p][0:1, :], flag[0:1, :], ALU.mult).then_inc(fresh_done, 1)
                dve.wait_ge(place, c + 6)
                V.scalar_tensor_tensor(rel_jump[:, :], rel[:, :], 0.0, jump[:, :], ALU.is_ge, ALU.mult).then_inc(place, 1)
                V.scalar_tensor_tensor(step_[:, :], jump[:, :], 128.0, flag[:, :], ALU.add, ALU.mult).then_inc(place, 1)
                V.scalar_tensor_tensor(slot[:, :], rel[:, :], -128.0, end128[:, :], ALU.add, ALU.add).then_inc(place, 1)
                dve.wait_ge(place, c + 9)
                V.tensor_tensor(slot[:, :], slot[:, :], rel_jump[:, :], ALU.add).then_inc(place, 1)
                V.tensor_tensor(end128[:, :], end128[:, :], step_[:, :], ALU.add).then_inc(place, 1)
                dve.wait_ge(place, c + 10)
                V.tensor_tensor(at[:, :, :], oh[p][:, :, :], slot[:, None, :].to_broadcast([128, TOPK, X]), ALU.mult).then_inc(place, 1)
                dve.wait_ge(place, c + 12)
                V.tensor_reduce(pos_f[:, :], at[:, :, :], axis=AX.X, op=ALU.add).then_inc(place, 1)
                dve.wait_ge(place, c + 13)
                if later(due := (r + k // GR) * 64):
                    dve.wait_ge(scattered[k % GR], due)
                V.tensor_copy(pos[k % GR][:, :], pos_f[:, :]).then_inc(pos_done, 1)
                V.tensor_copy(of_tile(pos_all, i), pos_f[:, :]).then_inc(place, 1)
                dve.sem_inc(place, 1)

            def note_owner(r, k):
                i = r * GR + k
                dve.wait_ge(col_mm, i + 1)
                dve.wait_ge(owner_v, i + 1)
                V.scalar_tensor_tensor(owner[:, :], iota_p[:, :], col_ps[0:X, 0:1], owner[:, :], ALU.is_equal, ALU.add).then_inc(owner_v, 1)

            def tile(r, k):
                if not is_last(r, k, 1, NT, GR):
                    choose(r, k + 1)
                find_slots(r, k)
                if not first(r, k):
                    note_owner(r, k - 1)

            dve.wait_ge(consts, 16 * 7)
            choose(0, 0)
            over_all(dve, tile, NT, GR, 1)
            note_owner(NT // GR, NT % GR - 1)
            dve.wait_ge(owner_mm, 1)
            V.tensor_copy(owner_i[:, :], col_ps[0:1, 0:PAGES]).then_inc(owner_done, 1)
            dve.wait_ge(owner_done, 1)
            dve.wait_ge(w_in, 16 * (X // XW))

            def page(j, k):
                if k % S not in ACT_PAGES:
                    x = dve.value_load(at_page(j), min_val=0, max_val=X - 1)
                    if later(due := j - (DEEP - 1)):
                        dve.wait_ge(y_mm, due)
                    V.tensor_copy(wx[k % DEEP], of_expert(x)).then_inc(wx_dve, 1)
                if later(due := j - (DEEP - 1)):
                    dve.wait_ge(hid_mm, due)
                dve.wait_ge(xt_mm, j + 1)
                V.tensor_copy(xs_t[k % DEEP][:, :, :].rearrange("p a b -> p (a b)"), tp_ps[k % DEEP][:, 0:D]).then_inc(xt_done, 1)

            def take_slots(i, k):
                V.tensor_copy(taken[k][:, :], of_tile(pos_all, i)).then_inc(posg_done, 1)

            def combine(i, n, k, q):
                if q == 0:
                    dve.wait_ge(rows_in[k], n * 64 + 64)
                    dve.wait_ge(h_tile_in[k], n * 16 + 16)
                    if later(due := n * 16):
                        dve.wait_ge(out_sent[k], due)
                else:
                    dve.wait_ge(sum_v, i * 5 + q)
                other = res[k] if q else h_tile[k]
                gate = col(gates[:, :, :].rearrange("p i q -> p (i q)"), i * TOPK + q)
                V.scalar_tensor_tensor(res[k], rows[k][:, q, :], gate, other, ALU.mult, ALU.add).then_inc(sum_v, 1)
                if q == TOPK - 1:
                    dve.wait_ge(sum_v, i * 5 + 4)
                    dve.sem_inc(sum_v, 1)
                    if not (isinstance(i, int) and i + TS >= NT):
                        take_slots(i + TS, k)

            def trip(r, sums):
                for k in range(TP):
                    page(r * TP + k, k)
                    if sums:
                        t = k // TOPK
                        combine(r * TS + (t - LAG * TS), r + -LAG, t, k % TOPK)

            for k in range(TS):
                take_slots(k, k)
            dve.wait_ge(gates_done, 1)
            over_trips(dve, trip)
            for i in range(SUMMED, NT):
                for q in range(TOPK):
                    combine(i, i // TS, i % TS, q)

        @block.gpsimd
        def _(pool):
            P = nc.gpsimd
            P.memset(minus_half[:, :], -0.5).then_inc(set_p, 1)
            pool.wait_ge(set_p, 1)
            for c, (a, b) in enumerate(spans):
                pool.wait_ge(power_v, c + 1)
                P.tensor_tensor(rstd[:, a:b], var_x[:, a:b], minus_half[:, a:b], ALU.pow).then_inc(power_p, 1)
                pool.wait_ge(power_p, 2 * c + 1)
                P.tensor_tensor(shift[:, a:b], mean[:, a:b], rstd[:, a:b], ALU.mult).then_inc(power_p, 1)

            def scatter(r, k):
                pool.wait_ge(pos_done, r * GR + (k + 1))
                pool.sem_inc(pool_go, 1)
                for q in range(TOPK):
                    P.indirect_dma_start(x_dram[:, :], bass.IndirectOffsetOnAxis(ap=pos[k][:, q:q + 1], axis=0),
                                         hn[k], None).then_inc(scattered[k], 16)

            over_all(pool, scatter, NT, GR, 1)

            for i in range(NT):
                k, table = i % TS, pages_after(i + 1)
                pool.wait_ge(posg_done, i + 1)
                pool.wait_ge(pages_out, (table + S2 - 1) // S2 * S2)
                for q in range(TOPK):
                    P.indirect_dma_start(rows[k][:, q, :], None, y_dram[0:table * 128, :],
                                         bass.IndirectOffsetOnAxis(ap=taken[k][:, q:q + 1], axis=0)).then_inc(rows_in[k], 16)


def scan_arrays(ins):
    n = {k: np.asarray(v) for k, v in ins.items()}
    c = np.ascontiguousarray
    a = {"x": c(n["x"].transpose(0, 2, 1)), "tok_w": c(n["L0_tok_W"].T.reshape(CTX, 128, D).transpose(1, 0, 2)),
         "tok_b": n["L0_tok_b"], "tok_gamma": n["L0_tok_gamma"], "tok_beta": n["L0_tok_beta"],
         "tok_mean": n["L0_tok_running_mean"], "tok_var": n["L0_tok_running_var"], "normf": n["L0_attn_normf"],
         "ident": np.eye(128, dtype=np.float32)}
    s = np.zeros((96, 2 * NS, 128), mybir.dt.np(BF16))
    for j in range(2 * NS):
        for q in range(3):
            s[32 * q + j, j, :] = 1
    a["sel"] = s
    chunks = lambda w: c(w.reshape(-1, 128, *w.shape[1:]).swapaxes(0, 1))
    for d, pre in enumerate(("L0_attn_fwd_", "L0_attn_bwd_")):
        g = lambda k: n[pre + k]
        a[f"in{d}"] = chunks(g("inproj").T)
        a[f"xdt{d}"] = chunks(g("xproj")[:R].T)
        a[f"xbc{d}"] = chunks(np.concatenate([g("xproj")[R:].T] * 3, axis=1))
        a[f"dtw{d}"] = c(g("dtw").T)
        a[f"out{d}"] = chunks(g("outproj").T)
        a[f"vec{d}"] = chunks(np.concatenate([g("convw"), g("convb")[:, None], g("dtb")[:, None], g("Dp")[:, None], g("Alog")], axis=1))
        a[f"norm{d}"] = c(g("norm").reshape(2, 128).T)
    return a


def expert_arrays(ins):
    c = np.ascontiguousarray
    sel, keys, values = (np.asarray(ins["L0_ffn_" + k]) for k in ("expert_sel", "keys", "values"))
    k2 = keys.reshape(X, 2, 128, HX).transpose(0, 2, 1, 3).reshape(X, 128, 2 * HX)
    return {"before": np.triu(np.ones((128, 128)), 1).astype(mybir.dt.np(BF16)),
            "all_ones": np.ones((128, 128), mybir.dt.np(BF16)),
            "sel_w": c(sel.T.reshape(2, 128, X).transpose(1, 0, 2)),
            "iota_x": c(np.broadcast_to(np.arange(X, dtype=np.float32), (128, X))),
            "iota_p": c(np.broadcast_to(np.arange(1, PAGES + 1, dtype=np.float32), (X, PAGES))),
            "index_x": c(np.broadcast_to(np.arange(X, dtype=np.float32)[:, None], (X, 128))),
            "zeros": np.zeros((128, D), np.float32),
            "experts": c(np.concatenate([k2, values], axis=2))}


def build(nc, t, out):
    h2_dram = nc.dram_tensor("h2_dram", [B, L, D], F32).ap()
    x_dram = nc.dram_tensor("x_dram", [PAGES * 128, D], F32).ap()
    y_dram = nc.dram_tensor("y_dram", [PAGES * 128, D], F32).ap()
    tower(nc, t, h2_dram, x_dram)
    experts(nc, t, h2_dram, x_dram, y_dram, out)


def kernel(**inputs):
    import concourse.bacc as bacc
    from concourse.bass_utils import run_bass_kernel_spmd

    arrays = {**scan_arrays(inputs), **expert_arrays(inputs)}
    nc = bacc.Bacc("TRN2", target_bir_lowering=False, num_devices=1)
    t = {k: nc.dram_tensor("in_" + k, a.shape, mybir.dt.from_np(a.dtype), kind="ExternalInput").ap() for k, a in arrays.items()}
    out = nc.dram_tensor("out", [B, L, D], F32, kind="ExternalOutput").ap()
    build(nc, t, out)
    r = run_bass_kernel_spmd(nc, [{"in_" + k: a for k, a in arrays.items()}], core_ids=[0])
    return r.results[0]["out"]
```
